# Optimizing a Trainium2 kernel written in Bass

```python
import numpy as np
import jax
import jax.numpy as jnp

def _softmax(x, axis=-1):
    return jax.nn.softmax(x, axis=axis)

def _gelu(x):
    return jax.nn.gelu(x, approximate=True)

def _silu(x):
    return jax.nn.silu(x)

def _sigmoid(x):
    return jax.nn.sigmoid(x)

def _layernorm(x, axis=-1, eps=1e-05):
    m = jnp.mean(x, axis=axis, keepdims=True)
    v = jnp.var(x, axis=axis, keepdims=True)
    return (x - m) / jnp.sqrt(v + eps)

def _scatter_add(tgt, idx, src, axis=0):
    return tgt.at[idx].add(src)

def _segment_sum(src, seg, n):
    return jax.ops.segment_sum(src, seg, n)
kernel_name = 'mk_adj_resnorm_d2_adj_r2_1547cb'

def setup_inputs(seed: int=0):
    np.random.seed(seed)
    _w = jnp.asarray

    def _rec_inputs():
        import jax
        import jax.numpy as jnp
        _gk = jax.random.key(seed)
        x = -0.0004776 + 1.001 * jax.random.normal(jax.random.fold_in(_gk, 1), (4096, 512), jnp.float32)
        _w = (1.0 + jnp.arange(4096, dtype=jnp.float32)) ** (-0.5)
        _w = _w / _w.mean()
        _pij = jnp.clip(0.00195312 * _w[:, None] * _w[None, :], 0.0, 1.0)
        _a = jax.random.uniform(jax.random.fold_in(_gk, 2), (4096, 4096)) < _pij
        _a = jnp.logical_or(_a, jnp.eye(4096, dtype=bool))
        _af = _a.astype(jnp.float32)
        adj = _af
        return (x, adj)
    x, adj = _rec_inputs()

    def _L0_gnn_setup():
        import jax, jax.numpy as jnp
        import numpy as np
        N, H, E, HEADS = (1500, 512, 10000, 8)
        DK = H // HEADS
        key = jax.random.key(seed)
        k1, k2, k3, k4 = jax.random.split(key, 4)
        inst_feature = jax.random.normal(k1, (N, H), dtype=jnp.float32)
        rel_pair_index = jax.random.randint(k2, (E, 2), 0, N, dtype=jnp.int64)
        agg = jnp.zeros((N, N), dtype=jnp.float32)
        agg = agg.at[rel_pair_index[:, 0], rel_pair_index[:, 1]].set(1.0)
        agg = agg.at[jnp.arange(N), jnp.arange(N)].set(1.0)
        std = float(np.sqrt(2.0 / (H + DK)))
        Wq = jax.random.normal(k3, (H, H), dtype=jnp.float32) * std
        Wk = jax.random.normal(k4, (H, H), dtype=jnp.float32) * std
        bq = jnp.zeros((H,), dtype=jnp.float32)
        bk = jnp.zeros((H,), dtype=jnp.float32)
        return {'inst_feature': inst_feature, 'aggregator_matrix': agg, 'rel_pair_index': rel_pair_index, 'Wq': Wq, 'bq': bq, 'Wk': Wk, 'bk': bk}
    _L0_gnn_all = _L0_gnn_setup()
    _L0_gnn_in = {k: v for k, v in _L0_gnn_all.items() if k in ('rel_pair_index', 'Wq', 'bq', 'Wk', 'bk')}
    del _L0_gnn_all

    def _L1_gnn_setup():
        import jax, jax.numpy as jnp
        import numpy as np
        ALPHA = 0.2
        NEG = -9000000000000000.0
        N, NFEAT, NHID, NHEADS = (2048, 512, 64, 8)
        EMB = NHID * NHEADS
        key = jax.random.key(seed)
        ks = jax.random.split(key, 16)
        x = jax.random.normal(ks[0], (N, NFEAT), dtype=jnp.float32)
        adj = (jax.random.uniform(ks[1], (N, N)) < 0.01).astype(jnp.float32)
        adj = jnp.maximum(adj, jnp.eye(N, dtype=jnp.float32))
        s = 0.05
        W = jax.random.normal(ks[2], (NHEADS, NFEAT, NHID), dtype=jnp.float32) * s
        a1 = jax.random.normal(ks[3], (NHEADS, NHID), dtype=jnp.float32) * s
        a2 = jax.random.normal(ks[4], (NHEADS, NHID), dtype=jnp.float32) * s
        W1 = jax.random.normal(ks[5], (EMB // 2, EMB), dtype=jnp.float32) * s
        b1 = jnp.zeros((EMB // 2,), dtype=jnp.float32)
        W2 = jax.random.normal(ks[6], (NFEAT // 4, EMB // 2), dtype=jnp.float32) * s
        b2 = jnp.zeros((NFEAT // 4,), dtype=jnp.float32)
        W3 = jax.random.normal(ks[7], (NFEAT // 2, NFEAT // 4), dtype=jnp.float32) * s
        b3 = jnp.zeros((NFEAT // 2,), dtype=jnp.float32)
        W4 = jax.random.normal(ks[8], (NFEAT, NFEAT // 2), dtype=jnp.float32) * s
        b4 = jnp.zeros((NFEAT,), dtype=jnp.float32)
        return {'x': x, 'adj': adj, 'W': W, 'a1': a1, 'a2': a2, 'W1': W1, 'b1': b1, 'W2': W2, 'b2': b2, 'W3': W3, 'b3': b3, 'W4': W4, 'b4': b4}
    _L1_gnn_all = _L1_gnn_setup()
    _L1_gnn_in = {k: v for k, v in _L1_gnn_all.items() if k in ('W', 'a1', 'a2', 'W1', 'b1', 'W2', 'b2', 'W3', 'b3', 'W4', 'b4')}
    del _L1_gnn_all
    return {'x': x, 'adj': adj, 'L0_gnn_rel_pair_index': _L0_gnn_in['rel_pair_index'], 'L0_gnn_Wq': _L0_gnn_in['Wq'], 'L0_gnn_bq': _L0_gnn_in['bq'], 'L0_gnn_Wk': _L0_gnn_in['Wk'], 'L0_gnn_bk': _L0_gnn_in['bk'], 'L1_gnn_W': _L1_gnn_in['W'], 'L1_gnn_a1': _L1_gnn_in['a1'], 'L1_gnn_a2': _L1_gnn_in['a2'], 'L1_gnn_W1': _L1_gnn_in['W1'], 'L1_gnn_b1': _L1_gnn_in['b1'], 'L1_gnn_W2': _L1_gnn_in['W2'], 'L1_gnn_b2': _L1_gnn_in['b2'], 'L1_gnn_W3': _L1_gnn_in['W3'], 'L1_gnn_b3': _L1_gnn_in['b3'], 'L1_gnn_W4': _L1_gnn_in['W4'], 'L1_gnn_b4': _L1_gnn_in['b4']}

def reference(x, adj, L0_gnn_rel_pair_index, L0_gnn_Wq, L0_gnn_bq, L0_gnn_Wk, L0_gnn_bk, L1_gnn_W, L1_gnn_a1, L1_gnn_a2, L1_gnn_W1, L1_gnn_b1, L1_gnn_W2, L1_gnn_b2, L1_gnn_W3, L1_gnn_b3, L1_gnn_W4, L1_gnn_b4):
    import jax
    import jax.numpy as jnp

    def _L0_gnn_ref(inst_feature, aggregator_matrix, rel_pair_index, Wq, bq, Wk, bk):
        import jax, jax.numpy as jnp
        import numpy as np
        N, H, E, HEADS = (1500, 512, 10000, 8)
        DK = H // HEADS
        n = inst_feature.shape[0]
        sub = rel_pair_index[:, 0]
        obj = rel_pair_index[:, 1]
        q = (inst_feature[sub] @ Wq.T + bq).reshape(-1, HEADS, DK)
        k = (inst_feature[obj] @ Wk.T + bk).reshape(-1, HEADS, DK)
        att = ((q * k).sum(-1) / np.sqrt(DK)).T.astype(inst_feature.dtype)
        scores = jnp.zeros((HEADS, n, n), dtype=inst_feature.dtype)
        scores = scores.at[:, sub, obj].set(att)
        mask = (1.0 - aggregator_matrix).astype(bool)
        scores = jnp.where(mask[None], -jnp.inf, scores)
        di = jnp.arange(n)
        scores = scores.at[:, di, di].set(1e-07)
        attn = jax.nn.softmax(scores, axis=2)
        aggregator_factor = attn.sum(axis=0) / HEADS
        return aggregator_factor @ inst_feature

    def _L1_gnn_ref(x, adj, W, a1, a2, W1, b1, W2, b2, W3, b3, W4, b4):
        import jax, jax.numpy as jnp
        import numpy as np
        ALPHA = 0.2
        NEG = -9000000000000000.0
        N, NFEAT, NHID, NHEADS = (2048, 512, 64, 8)
        EMB = NHID * NHEADS
        Wh = jnp.einsum('nf,hfd->hnd', x, W)
        e_src = jnp.einsum('hnd,hd->hn', Wh, a1)
        e_dst = jnp.einsum('hnd,hd->hn', Wh, a2)
        e = jax.nn.leaky_relu(e_src[:, :, None] + e_dst[:, None, :], ALPHA)
        e = jnp.where(adj[None] > 0, e, NEG)
        att = jax.nn.softmax(e, axis=-1)
        h = jnp.einsum('hnm,hmd->hnd', att, Wh)
        h = jax.nn.elu(h)
        enc = jnp.transpose(h, (1, 0, 2)).reshape(x.shape[0], -1)
        out = jax.nn.relu(enc @ W1.T + b1)
        out = jax.nn.relu(out @ W2.T + b2)
        out = jax.nn.relu(out @ W3.T + b3)
        out = out @ W4.T + b4
        return out
    x = _layernorm(x + _L0_gnn_ref(x, adj, L0_gnn_rel_pair_index, L0_gnn_Wq, L0_gnn_bq, L0_gnn_Wk, L0_gnn_bk), axis=-1)
    x = _layernorm(x + _L1_gnn_ref(x, adj, L1_gnn_W, L1_gnn_a1, L1_gnn_a2, L1_gnn_W1, L1_gnn_b1, L1_gnn_W2, L1_gnn_b2, L1_gnn_W3, L1_gnn_b3, L1_gnn_W4, L1_gnn_b4), axis=-1)
    return x

_drawn_inputs = setup_inputs


def setup_inputs(seed=0):
    import zlib

    import numpy as np

    out = dict(_drawn_inputs(seed))
    spreads = {'L0_gnn_bq': (0.0, 2.0),
     'L0_gnn_bk': (0.0, 2.0),
     'L1_gnn_b1': (0.0, 0.674),
     'L1_gnn_b2': (0.0, 0.353),
     'L1_gnn_b3': (0.0, 0.1),
     'L1_gnn_b4': (0.0, 0.1)}
    factors = {'L0_gnn_Wq': 102.411, 'L0_gnn_Wk': 98.79, 'L1_gnn_a1': 22.992, 'L1_gnn_a2': 4.095}
    for name, (base, spread) in spreads.items():
        noise = np.random.default_rng([zlib.crc32(name.encode()), seed]).standard_normal(out[name].shape)
        drawn = base * np.exp(spread * noise) if base else spread * noise
        out[name] = jnp.asarray(drawn.astype(out[name].dtype))
    for name, factor in factors.items():
        out[name] = (out[name] * factor).astype(out[name].dtype)
    return out
```

```python
import concourse.bass as bass
from concourse import mybir
from contextlib import ExitStack

P = 128
N, F, H, DH = 4096, 512, 8, 64
NT, KF = N // P, F // P
RP, RC = 125, 80
RT = -(-RP * RC // P)
LIST = (RT + 1) * P
SEC, SECS = 512, N // 512
CH = 4
PIECES = NT // CH
SR = 32
CR = 16
DIAG, EPS = 1e-7, 1e-5
SHIFT = 34.0
BIG = 1.0e30
OFF = 16384.0
M1, M2, M3 = 256, 128, 256

f32, f16, i32, u8 = mybir.dt.float32, mybir.dt.float16, mybir.dt.int32, mybir.dt.uint8
ALU = mybir.AluOpType
ACT = mybir.ActivationFunctionType
AX = mybir.AxisListType.X


class Chain:

    def __init__(self, eng, sem, base=0):
        self.eng, self.sem, self.base, self.n = eng, sem, base, 0

    def then(self, ins):
        self.n += 1
        ins.then_inc(self.sem, 1)
        self.eng.wait_ge(self.sem, self.base + self.n)


def tiles_of(ap):
    return ap.rearrange("(t p) f -> p t f", p=P)


def stage(nc, ctx, of):
    def sb(name, shape, dt=f32):
        return ctx.enter_context(nc.sbuf_tensor(f"{of}_{name}", shape, dt))

    def ps(name, shape):
        return ctx.enter_context(nc.psum_tensor(f"{of}_{name}", shape, f32))

    def sem(name):
        return ctx.enter_context(nc.semaphore(f"{of}_{name}"))

    return sb, ps, sem


class Kept:
    pass


def make_kept(nc, ctx):
    k = Kept()

    def sb(name, shape, dt=f32):
        return ctx.enter_context(nc.sbuf_tensor(name, shape, dt))

    def dram(name, shape, dt=f32):
        return nc.dram_tensor(name, shape, dt, kind="Internal").ap()

    k.ident = sb("ident", [P, P])
    k.before = sb("before", [P, P])
    k.ones = sb("ones", [P, P])
    k.w = sb("w", [P, KF, F])
    k.wa = sb("wa", [P, KF, 2 * H])
    k.scale = sb("scale", [P, 2])
    k.deg = sb("deg", [P, NT])
    k.nlist = sb("nlist", [P, 1], i32)
    k.adj8_d = dram("adj8_d", [SECS, PIECES, P, CH * SEC], u8)
    k.agg_d = dram("agg_d", [N, F])
    k.rel_d = dram("rel_d", [N, F])
    k.stats_d = dram("stats_d", [N, SR])
    k.coef_d = dram("coef_d", [N, CR])
    k.list_d = dram("list_d", [LIST, 1])
    k.tot_d = dram("tot_d", [1, P])
    k.x1_d = dram("x1_d", [N, F])
    k.trow_d = dram("trow_d", [H, N])
    k.empty_d = dram("empty_d", [N, 1])
    k.bcol_d = dram("bcol_d", [1, F])
    return k


def split_features(nc, k, ins, xs):
    with ExitStack() as ctx:
        sb, ps, sem = stage(nc, ctx, "split")
        x_sb = sb("x_sb", [P, NT, F])
        a_row = sb("a_row", [P, 2, F])
        a_prod = sb("a_prod", [P, KF, F])
        part_max = sb("part_max", [P, PIECES])
        own_max = sb("own_max", [P, 1])
        all_max = sb("all_max", [P, 1])
        floor_max = sb("floor_max", [P, 1])
        exponent = sb("exponent", [P, 1], i32)
        x_in = [sem(f"x_in{i}") for i in range(PIECES)]
        w_in, const_in = sem("w_in"), sem("const_in")
        dve_step, own_ready, max_ready = sem("dve_step"), sem("own_ready"), sem("max_ready")
        scale_ready, high_ready, split_done = sem("scale_ready"), sem("high_ready"), sem("split_done")
        block = ctx.enter_context(nc.Block())

        @block.sync
        def _(sp):
            sp.dma_start(k.w[:, :, :], ins["W"].rearrange("(t p) f -> p t f", p=P)).then_inc(w_in, 16)
            sp.dma_start(a_row[:, 0, :], ins["a1"].broadcast_to([P, F])).then_inc(w_in, 16)
            sp.dma_start(a_row[:, 1, :], ins["a2"].broadcast_to([P, F])).then_inc(w_in, 16)
            for i in range(PIECES):
                sp.dma_start(x_sb[:, CH * i:CH * (i + 1), :],
                             tiles_of(ins["x"])[:, CH * i:CH * (i + 1), :]).then_inc(x_in[i], 16)
            sp.dma_start(k.ident[:, :], ins["ident"]).then_inc(const_in, 16)
            sp.dma_start(k.before[:, :], ins["before"]).then_inc(const_in, 16)
            sp.wait_ge(const_in, 32)

        @block.vector
        def _(dve):
            step = Chain(dve, dve_step)
            nc.vector.memset(k.ones[:, :], 1.0)
            dve.wait_ge(w_in, 48)
            for a in range(2):
                for t in range(KF):
                    last = nc.vector.tensor_tensor(a_prod[:, t, :], k.w[:, t, :], a_row[:, a, :], ALU.mult)
                step.then(last)
                for t in range(KF):
                    last = nc.vector.tensor_reduce(k.wa[:, t, H * a:H * (a + 1)],
                                                   a_prod[:, t, :].rearrange("p (h d) -> p h d", d=DH), AX, ALU.add)
                step.then(last)
            for i in range(PIECES):
                dve.wait_ge(x_in[i], 16)
                last = nc.vector.tensor_reduce(part_max[:, i:i + 1],
                                               x_sb[:, CH * i:CH * (i + 1), :].rearrange("p t f -> p (t f)"),
                                               AX, ALU.max, apply_absolute_value=True)
            step.then(last)
            nc.vector.tensor_reduce(own_max[:, :], part_max[:, :], AX, ALU.max).then_inc(own_ready, 1)
            dve.wait_ge(max_ready, 1)
            step.then(nc.vector.tensor_scalar(floor_max[:, :], all_max[:, :], 1e-20, None, ALU.max))
            step.then(nc.vector.tensor_single_scalar(exponent[:, :], floor_max[:, :].bitcast(i32),
                                                     0x7F800000, ALU.bitwise_and))
            step.then(nc.vector.tensor_scalar(k.scale[:, 0:1].bitcast(i32), exponent[:, :],
                                              -1.0, float(268 << 23), ALU.mult, ALU.add))
            nc.vector.tensor_scalar(k.scale[:, 1:2].bitcast(i32), exponent[:, :],
                                    float(-(14 << 23)), None, ALU.add).then_inc(scale_ready, 1)
            dve.wait_ge(scale_ready, 1)
            for i in range(PIECES):
                dve.wait_ge(high_ready, i + 1)
                last = nc.vector.scalar_tensor_tensor(xs[:, CH * i:CH * (i + 1), F:2 * F],
                                                      x_sb[:, CH * i:CH * (i + 1), :], k.scale[:, 0:1],
                                                      xs[:, CH * i:CH * (i + 1), 0:F], ALU.mult, ALU.subtract)
            last.then_inc(split_done, 1)
            dve.wait_ge(split_done, 1)

        @block.gpsimd
        def _(gp):
            gp.wait_ge(own_ready, 1)
            nc.gpsimd.partition_all_reduce(all_max[:, :], own_max[:, :], P,
                                           bass.bass_isa.ReduceOp.max).then_inc(max_ready, 1)

        @block.scalar
        def _(act):
            act.wait_ge(scale_ready, 1)
            for i in range(PIECES):
                nc.scalar.activation(xs[:, CH * i:CH * (i + 1), 0:F], x_sb[:, CH * i:CH * (i + 1), :], ACT.Copy,
                                     scale=k.scale[:, 0:1]).then_inc(high_ready, 1)


def neighbour_sums(nc, k, ins, xs, key_row):
    with ExitStack() as ctx:
        sb, ps, sem = stage(nc, ctx, "sums")
        R = 4
        adj_in = sb("adj_in", [P, R, CH, SEC])
        adj16 = sb("adj16", [P, R, CH, SEC], f16)
        adj8 = sb("adj8", [P, R, CH * SEC], u8)
        agg = sb("agg", [P, 4, F])
        one16 = sb("one16", [P, 1], f16)
        zeros = sb("zeros", [P, 1024])
        rows0 = sb("rows0", [P, NT, SR])
        blank = sb("blank", [P, LIST // P])
        pairs = sb("pairs", [RP, RC, 2], i32)
        sub = sb("sub", [RP, RC])
        obj = sb("obj", [RP, RC])
        key = sb("key", [RP, RC])
        key_i = sb("key_i", [RP, RC], i32)
        apart = sb("apart", [RP, RC])
        on_edge = sb("on_edge", [RP, RC])
        valid = sb("valid", [RP, RC])
        scan = sb("scan", [RP, 2, RC])
        tot_row = sb("tot_row", [RP, RP])
        fold = sb("fold", [RP, 2, P])
        pos = sb("pos", [RP, RC])
        pos_i = sb("pos_i", [RP, RC], i32)
        eight_i = sb("eight_i", [RP, 8], i32)
        eight_f = sb("eight_f", [RP, 8])
        ps_agg = ps("ps_agg", [P, 4, F])
        ps_deg = ps("ps_deg", [P, F])

        adj_ld = [sem(f"adj_ld{i}") for i in range(R)]
        byte_st = [sem(f"byte_st{i}") for i in range(R)]
        cast_done, bytes_done, sums_done = sem("cast_done"), sem("bytes_done"), sem("sums_done")
        sec_summed, agg_ready, agg_st = sem("sec_summed"), sem("agg_ready"), sem("agg_st")
        consts, fills, pairs_ld = sem("consts"), sem("fills"), sem("pairs_ld")
        pool_step, gate, dve_step, keys_ready, sp_gate = sem("pool_step"), sem("gate"), sem("dve_step"), sem("keys_ready"), sem("sp_gate")
        flag_ld, tot_st, tot_ld, list_st, row_ld = (sem("flag_ld"), sem("tot_st"), sem("tot_ld"),
                                                    sem("list_st"), sem("row_ld"))
        block = ctx.enter_context(nc.Block())
        adj_t = tiles_of(ins["adj_t"])

        @block.sync
        def _(sp):
            sp.dma_start(pairs[:, :, :], ins["pairs"].rearrange("(p c) two -> p c two", p=RP)).then_inc(pairs_ld, 16)
            sp.sem_inc(agg_st, 16)
            for i in range(R):
                sp.sem_inc(byte_st[i], 16)

            def load(s, c):
                sp.wait_ge(cast_done, s * PIECES + c + 1)
                sp.sem_inc(sp_gate, 1)
                sp.dma_start(adj_in[:, c % R, :, :],
                             adj_t[:, CH * c:CH * (c + 1), bass.ds(s * SEC, SEC)]).then_inc(adj_ld[c % R], 16)

            def store_bytes(s, c):
                sp.wait_ge(bytes_done, s * PIECES + c + 1 + R)
                sp.sem_inc(sp_gate, 1)
                sp.dma_start(k.adj8_d[bass.ds(s, 1), c, :, :].rearrange("o p n -> p (o n)"),
                             adj8[:, c % R, :]).then_inc(byte_st[c % R], 16)

            def store_sums(s):
                sp.wait_ge(agg_ready, s + 2)
                sp.sem_inc(sp_gate, 1)
                sp.dma_start(tiles_of(k.agg_d)[:, bass.ds(s * 4, 4), :], agg[:, :, :]).then_inc(agg_st, 16)

            for c in range(R):
                load(0, c)
            sp.wait_ge(consts, 1)
            for i in range(N * F // P // 1024):
                sp.dma_start(k.rel_d.rearrange("(p t) f -> p (t f)", p=P)[:, 1024 * i:1024 * (i + 1)],
                             zeros[:, :]).then_inc(fills, 16)
            sp.dma_start(k.stats_d.rearrange("(p t) c -> p (t c)", p=P),
                         rows0[:, :, :].rearrange("p t c -> p (t c)")).then_inc(fills, 16)
            sp.dma_start(k.list_d.rearrange("(p c) o -> p (c o)", p=P), blank[:, :]).then_inc(fills, 16)
            with sp.Fori(0, SECS - 1) as s:
                for c in range(R):
                    load(s, c + R)
                    store_bytes(s, c)
                for c in range(R):
                    load(s + 1, c)
                    store_bytes(s, c + R)
                store_sums(s)
            s = SECS - 1
            for c in range(R):
                load(s, c + R)
                store_bytes(s, c)
            for c in range(R):
                store_bytes(s, c + R)
            store_sums(s)
            for i in range(R):
                sp.wait_ge(byte_st[i], 16 * (2 * SECS + 1))
            sp.wait_ge(agg_st, 16 * (SECS + 1))

        @block.scalar
        def _(act):
            act.sem_inc(cast_done, R)
            with act.Fori(0, SECS) as s:
                for c in range(PIECES):
                    act.wait_ge(adj_ld[c % R], 16 * (2 * s + c // R + 1))
                    act.wait_ge(sums_done, s * PIECES + c + 1)
                    act.wait_ge(bytes_done, s * PIECES + c + 1)
                    nc.scalar.activation(adj16[:, c % R, :, :], adj_in[:, c % R, :, :],
                                         ACT.Copy).then_inc(cast_done, 1)

        @block.tensor
        def _(pe):
            pe.sem_inc(sums_done, R)
            pe.wait_ge(consts, 1)
            with pe.Fori(0, SECS) as s:
                pe.wait_ge(agg_ready, s + 1)
                for c in range(PIECES):
                    pe.wait_ge(cast_done, s * PIECES + c + 1 + R)
                    for q in range(CH):
                        j = CH * c + q
                        for i in range(4):
                            block_t = adj16[:, c % R, q, P * i:P * (i + 1)]
                            nc.tensor.matmul(ps_agg[:, i, :], block_t, xs[:, j, 0:F], start=(j == 0), stop=False)
                            nc.tensor.matmul(ps_agg[:, i, :], block_t, xs[:, j, F:2 * F], start=False,
                                             stop=(j == NT - 1))
                            last = nc.tensor.matmul(ps_deg[:, i:i + 1], block_t, one16[:, :],
                                                    start=(j == 0 and i == 0), stop=(j == NT - 1),
                                                    skip_group_check=True)
                    last.then_inc(sums_done, 1)

        @block.vector
        def _(dve):
            dve.sem_inc(bytes_done, R)
            dve.sem_inc(agg_ready, 1)
            nc.vector.memset(one16[:, :], 1.0)
            nc.vector.memset(zeros[:, :], 0.0)
            nc.vector.memset(blank[:, :], -1.0)
            nc.vector.memset(rows0[:, :, 0:H], DIAG)
            nc.vector.memset(rows0[:, :, H:SR], 0.0).then_inc(consts, 1)
            step = Chain(dve, dve_step)
            dve.wait_ge(pairs_ld, 16)
            nc.vector.tensor_copy(sub[:, :], pairs[:, :, 0])
            step.then(nc.vector.tensor_copy(obj[:, :], pairs[:, :, 1]))
            nc.vector.tensor_tensor(apart[:, :], sub[:, :], obj[:, :], ALU.not_equal)
            step.then(nc.vector.scalar_tensor_tensor(key[:, :], obj[:, :], float(N), sub[:, :], ALU.mult, ALU.add))
            nc.vector.tensor_copy(key_i[:, :], key[:, :]).then_inc(keys_ready, 1)
            with dve.Fori(0, SECS) as s:
                for c in range(PIECES):
                    dve.wait_ge(cast_done, s * PIECES + c + 1 + R)
                    dve.wait_ge(byte_st[c % R], 16 * (2 * s + c // R + 1))
                    nc.vector.tensor_copy(adj8[:, c % R, :],
                                          adj16[:, c % R, :, :].rearrange("p q i -> p (q i)")).then_inc(bytes_done, 1)
                dve.wait_ge(sums_done, (s + 1) * PIECES + R)
                dve.wait_ge(agg_st, 16 * (s + 1))
                nc.vector.tensor_copy(k.deg[:, bass.ds(4 * s, 4)], ps_deg[:, 0:4])
                nc.vector.tensor_scalar(agg[:, :, :], ps_agg[:, :, :], k.scale[:, 1:2], None,
                                        ALU.mult).then_inc(agg_ready, 1)

        @block.gpsimd
        def _(gp):
            step = Chain(gp, pool_step)
            gp.wait_ge(keys_ready, 1)
            adj_flat = ins["adj_t"].rearrange("j (i o) -> (j i) o", o=1)
            gathered = step.n
            step.base = 0
            with gp.Fori(0, RC // 8) as g:
                nc.gpsimd.tensor_copy(eight_i[:, :], key_i[:, bass.ds(8 * g, 8)]).then_inc(pool_step, 1)
                gp.wait_ge(pool_step, gathered + 2 * g + 1)
                gp.sem_inc(gate, 1)
                for e in range(8):
                    gp.indirect_dma_start(eight_f[:, e:e + 1], None, adj_flat,
                                          bass.IndirectOffsetOnAxis(ap=eight_i[:, e:e + 1], axis=0),
                                          bounds_check=N * N - 1, oob_is_err=False).then_inc(flag_ld, 16)
                gp.wait_ge(flag_ld, 128 * (g + 1))
                gp.sem_inc(gate, 1)
                nc.gpsimd.tensor_copy(on_edge[:, bass.ds(8 * g, 8)], eight_f[:, :]).then_inc(pool_step, 1)
                gp.wait_ge(pool_step, gathered + 2 * g + 2)
                gp.sem_inc(gate, 1)
            step.n = gathered + 2 * (RC // 8)
            step.then(nc.gpsimd.tensor_tensor(valid[:, :], on_edge[:, :], apart[:, :], ALU.mult))
            step.then(nc.gpsimd.tensor_copy(scan[:, 0, :], valid[:, :]))
            src, dist = 0, 1
            while dist < RC:
                nc.gpsimd.tensor_copy(scan[:, 1 - src, 0:dist], scan[:, src, 0:dist])
                step.then(nc.gpsimd.tensor_tensor(scan[:, 1 - src, dist:RC], scan[:, src, dist:RC],
                                                  scan[:, src, 0:RC - dist], ALU.add))
                src, dist = 1 - src, 2 * dist
            gp.dma_start(k.tot_d[0:1, 0:RP].rearrange("o p -> p o"), scan[:, src, RC - 1:RC]).then_inc(tot_st, 16)
            gp.wait_ge(tot_st, 16)
            gp.dma_start(tot_row[:, :], k.tot_d[0:1, 0:RP].broadcast_to([RP, RP])).then_inc(tot_ld, 16)
            gp.wait_ge(tot_ld, 16)
            step.then(nc.gpsimd.memset(fold[:, :, :], 0.0))
            nc.gpsimd.tensor_tensor(fold[:, 0, 0:RP], tot_row[:, :], k.before[0:RP, 0:RP], ALU.mult)
            step.then(nc.gpsimd.tensor_copy(fold[:, 1, 0:RP], tot_row[:, :]))
            half = P // 2
            while half:
                step.then(nc.gpsimd.tensor_tensor(fold[:, :, 0:half], fold[:, :, 0:half],
                                                  fold[:, :, half:2 * half], ALU.add))
                half //= 2
            nc.gpsimd.tensor_copy(k.nlist[0:RP, :], fold[:, 1, 0:1])
            step.then(nc.gpsimd.tensor_scalar(pos[:, :], scan[:, src, :], fold[:, 0, 0:1], -1.0 - OFF, ALU.add, ALU.add))
            step.then(nc.gpsimd.tensor_tensor(pos[:, :], pos[:, :], valid[:, :], ALU.mult))
            step.then(nc.gpsimd.tensor_scalar(pos_i[:, :], pos[:, :], OFF, None, ALU.add))
            gp.wait_ge(fills, 16 * (N * F // P // 1024 + 2))
            placed = step.n
            with gp.Fori(0, RC // 8) as g:
                nc.gpsimd.tensor_copy(eight_i[:, :], pos_i[:, bass.ds(8 * g, 8)])
                nc.gpsimd.tensor_copy(eight_f[:, :], key[:, bass.ds(8 * g, 8)]).then_inc(pool_step, 1)
                gp.wait_ge(pool_step, placed + g + 1)
                gp.sem_inc(gate, 1)
                for e in range(8):
                    gp.indirect_dma_start(k.list_d, bass.IndirectOffsetOnAxis(ap=eight_i[:, e:e + 1], axis=0),
                                          eight_f[:, e:e + 1], None,
                                          bounds_check=LIST - 1, oob_is_err=False).then_inc(list_st, 16)
                gp.wait_ge(list_st, 128 * (g + 1))
                gp.sem_inc(gate, 1)
            gp.dma_start(key_row[:, :], k.list_d.rearrange("n o -> o n").broadcast_to([P, LIST])).then_inc(row_ld, 16)
            gp.wait_ge(row_ld, 16)


def listed_tiles(eng, n, tile):
    tile(0)
    with eng.If(n > P):
        with eng.Fori(1, RT) as t:
            with eng.If(n > t * P):
                tile(t)


def decode_tile(nc, dve, step, key_col, got):
    nc.vector.tensor_scalar(got.valid[:, :], key_col[:, :], 0.0, None, ALU.is_ge)
    step.then(nc.vector.tensor_scalar(got.key_i[:, :], key_col[:, :], 0.0, None, ALU.max))
    nc.vector.tensor_single_scalar(got.sub_i[:, :], got.key_i[:, :], N - 1, ALU.bitwise_and)
    step.then(nc.vector.tensor_single_scalar(got.obj_i[:, :], got.key_i[:, :], N.bit_length() - 1,
                                             ALU.arith_shift_right))
    step.then(nc.vector.tensor_copy(got.sub_f[:, :], got.sub_i[:, :]))
    step.then(nc.vector.scalar_tensor_tensor(got.seg[:, :], got.sub_f[:, :], 1.0, got.valid[:, :],
                                             ALU.add, ALU.mult))
    step.then(nc.vector.tensor_scalar(got.seg[:, :], got.seg[:, :], -1.0, None, ALU.add))


def same_segment(nc, dve, step, k, got, seg_row, same, first_i):
    step.then(nc.vector.tensor_scalar(same[:, :], seg_row, got.seg[:, 0:1], None, ALU.is_equal))
    step.then(nc.vector.tensor_tensor(got.earlier[:, :], same[:, :], k.before[:, :], ALU.mult))
    step.then(nc.vector.tensor_reduce(got.count[:, :], got.earlier[:, :], AX, ALU.add))
    step.then(nc.vector.scalar_tensor_tensor(got.count[:, :], got.count[:, :], 0.5, got.valid[:, :],
                                             ALU.is_lt, ALU.mult))
    step.then(nc.vector.scalar_tensor_tensor(got.index_f[:, :], got.sub_f[:, :], -OFF, got.count[:, :],
                                             ALU.add, ALU.mult))
    step.then(nc.vector.tensor_scalar(first_i[:, :], got.index_f[:, :], OFF, None, ALU.add))


def decoded(sb):
    got = Kept()
    got.valid, got.sub_f, got.seg = sb("valid", [P, 1]), sb("sub_f", [P, 1]), sb("seg", [P, 1])
    got.key_i, got.sub_i, got.obj_i = sb("key_i", [P, 1], i32), sb("sub_i", [P, 1], i32), sb("obj_i", [P, 1], i32)
    got.earlier, got.count, got.index_f = sb("earlier", [P, P]), sb("count", [P, 1]), sb("index_f", [P, 1])
    return got


def relation_scores(nc, k, ins, key_row, att_all, weight_all):
    with ExitStack() as ctx:
        sb, ps, sem = stage(nc, ctx, "score")
        got = decoded(sb)
        wq, wk = sb("wq", [P, KF, F]), sb("wk", [P, KF, F])
        bqk = sb("bqk", [1, 2, F])
        key_col = sb("key_col", [P, 1])
        hit = sb("hit", [P, LIST], mybir.dt.bfloat16)
        times, share = sb("times", [P, 1]), sb("share", [P, 1])
        diag, same = sb("diag", [P, P]), sb("same", [P, P])
        first_i = sb("first_i", [P, 1], i32)
        x_sub, x_obj = sb("x_sub", [P, F]), sb("x_obj", [P, F])
        xt_sub, xt_obj = sb("xt_sub", [P, F]), sb("xt_obj", [P, F])
        q_sb, qk = sb("q_sb", [P, F]), sb("qk", [P, F])
        att = sb("att", [P, H])
        att_diag = sb("att_diag", [P, H, P])
        away = sb("away", [P, P])
        seg_att = sb("seg_att", [P, H, P])
        old, new = sb("old", [P, SR]), sb("new", [P, SR])
        drop, ex = sb("drop", [P, 2, H]), sb("ex", [P, 2, H])
        terms = sb("terms", [P, H + 1])
        ps_seg, ps_xs, ps_xo = ps("ps_seg", [P, F]), ps("ps_xs", [P, F]), ps("ps_xo", [P, F])
        ps_q, ps_k, ps_att = ps("ps_q", [P, F]), ps("ps_k", [P, F]), ps("ps_att", [P, 2, F])

        w_ld, key_ld, tile_done, gath_ld, new_st = (sem("w_ld"), sem("key_ld"), sem("tile_done"), sem("gath_ld"),
                                                    sem("new_st"))
        diag_ready, seg_ready, idx_ready, turned, turned_sb = (sem("diag_ready"), sem("seg_ready"), sem("idx_ready"),
                                                               sem("turned"), sem("turned_sb"))
        qk_ready, q_copied, attd_ready, att_spread = (sem("qk_ready"), sem("q_copied"), sem("attd_ready"),
                                                      sem("att_spread"))
        drop_ready, ex_ready, terms_ready, sums_ready, new_ready = (sem("drop_ready"), sem("ex_ready"),
                                                                    sem("terms_ready"), sem("sums_ready"),
                                                                    sem("new_ready"))
        dve_step, gate, blanks = sem("dve_step"), sem("gate"), sem("blanks")
        LINKS = 24
        block = ctx.enter_context(nc.Block())

        @block.sync
        def _(sp):
            sp.dma_start(wq[:, :, :], tiles_of(ins["wq_t"])).then_inc(w_ld, 16)
            sp.dma_start(wk[:, :, :], tiles_of(ins["wk_t"])).then_inc(w_ld, 16)
            sp.dma_start(bqk[:, 0, :], ins["bq"]).then_inc(w_ld, 16)
            sp.dma_start(bqk[:, 1, :], ins["bk"]).then_inc(w_ld, 16)
            sp.wait_ge(w_ld, 64)
            n = sp.value_load(k.nlist[0:1, 0:1], min_val=0, max_val=RP * RC)
            def tile(t):
                sp.wait_ge(tile_done, t + 1)
                sp.sem_inc(gate, 1)
                sp.dma_start(key_col[:, :], k.list_d[bass.ds(t * P, P), :]).then_inc(key_ld, 16)

            listed_tiles(sp, n, tile)

        @block.vector
        def _(dve):
            nc.vector.memset(new[:, :], 0.0).then_inc(blanks, 1)
            dve.wait_ge(blanks, 1)
            n = dve.value_load(k.nlist[0:1, 0:1], min_val=0, max_val=RP * RC)
            def tile(t):
                step = Chain(dve, dve_step, t * LINKS)
                dve.wait_ge(key_ld, 16 * (t + 1))
                decode_tile(nc, dve, step, key_col, got)
                nc.vector.tensor_scalar(diag[:, :], k.ident[:, :], got.seg[:, 0:1], None,
                                        ALU.mult).then_inc(diag_ready, 1)
                step.then(nc.vector.tensor_scalar(hit[:, :], key_row[:, :], key_col[:, 0:1], 0.0,
                                                  ALU.is_equal, ALU.add, accum_out=times[:, :]))
                step.then(nc.vector.tensor_scalar(times[:, :], times[:, :], 1.0, None, ALU.max))
                step.then(nc.vector.reciprocal(share[:, :], times[:, :]))
                step.then(nc.vector.tensor_tensor(terms[:, H:H + 1], share[:, :], got.valid[:, :], ALU.mult))
                nc.vector.tensor_copy(weight_all[:, bass.ds(t, 1)], terms[:, H:H + 1])
                dve.wait_ge(seg_ready, t + 1)
                same_segment(nc, dve, step, k, got, ps_seg[:, 0:P], same, first_i)
                step.then(nc.vector.tensor_scalar(away[:, :], same[:, :], BIG, -BIG, ALU.mult, ALU.add))
                dve.wait_ge(q_copied, t + 1)
                step.then(nc.vector.tensor_tensor(qk[:, :], q_sb[:, :], ps_k[:, :], ALU.mult))
                step.then(nc.vector.tensor_reduce(att[:, :], qk[:, :].rearrange("p (h d) -> p h d", d=DH),
                                                  AX, ALU.add))
                step.then(nc.vector.tensor_scalar(att[:, :], att[:, :], DH ** -0.5, None, ALU.mult))
                nc.vector.tensor_scalar(att_all[:, bass.ds(t * H, H)], att[:, :], got.valid[:, 0:1], None,
                                        ALU.mult)
                nc.vector.tensor_tensor(att_diag[:, :, :], k.ident[:, :].unsqueeze(1).broadcast_to([P, H, P]),
                                        att[:, :].unsqueeze(2).broadcast_to([P, H, P]),
                                        ALU.mult).then_inc(attd_ready, 1)
                dve.wait_ge(att_spread, t + 1)
                step.then(nc.vector.tensor_tensor(seg_att[:, :, :],
                                                  ps_att[:, :, :].rearrange("p b (h f) -> p (b h) f", f=P),
                                                  away[:, :].unsqueeze(1).broadcast_to([P, H, P]), ALU.add))
                step.then(nc.vector.tensor_reduce(drop[:, 0, :], seg_att[:, :, :], AX, ALU.max))
                step.then(nc.vector.tensor_tensor(new[:, 0:H], drop[:, 0, :], old[:, 0:H], ALU.max))
                nc.vector.tensor_tensor(drop[:, 0, :], old[:, 0:H], new[:, 0:H], ALU.subtract)
                nc.vector.tensor_tensor(drop[:, 1, :], att[:, :], new[:, 0:H], ALU.subtract).then_inc(drop_ready, 1)
                dve.wait_ge(ex_ready, t + 1)
                nc.vector.tensor_scalar(terms[:, 0:H], ex[:, 1, :], terms[:, H:H + 1], None,
                                        ALU.mult).then_inc(terms_ready, 1)
                step.then(nc.vector.tensor_tensor(new[:, H:2 * H], old[:, H:2 * H], ex[:, 0, :], ALU.mult))
                dve.wait_ge(sums_ready, t + 1)
                nc.vector.tensor_tensor(new[:, H:2 * H], new[:, H:2 * H], ps_seg[:, P:P + H], ALU.add)
                last = nc.vector.tensor_tensor(new[:, 2 * H:2 * H + 1], old[:, 2 * H:2 * H + 1],
                                               ps_seg[:, P + H:P + H + 1], ALU.add)
                step.then(last)
                nc.vector.tensor_copy(got.count[:, :], got.valid[:, :]).then_inc(new_ready, 1)
                assert step.n == LINKS, step.n

            listed_tiles(dve, n, tile)

        @block.tensor
        def _(pe):
            pe.wait_ge(w_ld, 64)
            n = pe.value_load(k.nlist[0:1, 0:1], min_val=0, max_val=RP * RC)
            def tile(t):
                pe.wait_ge(diag_ready, t + 1)
                nc.tensor.matmul(ps_seg[:, 0:P], k.ones[:, :], diag[:, :], start=True,
                                 stop=True).then_inc(seg_ready, 1)
                pe.wait_ge(gath_ld, 48 * (t + 1))
                for x_rows, turned_ps in ((x_sub, ps_xs), (x_obj, ps_xo)):
                    for f in range(KF):
                        last = nc.tensor.transpose(turned_ps[:, P * f:P * (f + 1)], x_rows[:, P * f:P * (f + 1)],
                                                   k.ident[:, :])
                last.then_inc(turned, 1)
                pe.wait_ge(turned_sb, 2 * (t + 1))
                for xt, wt, out, b in ((xt_sub, wq, ps_q, 0), (xt_obj, wk, ps_k, 1)):
                    for f in range(KF):
                        nc.tensor.matmul(out[:, :], xt[:, P * f:P * (f + 1)], wt[:, f, :], start=(f == 0),
                                         stop=False)
                    last = nc.tensor.matmul(out[:, :], k.ones[0:1, :], bqk[0:1, b, :], start=False, stop=True)
                last.then_inc(qk_ready, 1)
                pe.wait_ge(attd_ready, t + 1)
                for b in range(2):
                    last = nc.tensor.matmul(ps_att[:, b, :], k.ones[:, :],
                                            att_diag[:, 4 * b:4 * (b + 1), :].rearrange("p h f -> p (h f)"),
                                            start=True, stop=True)
                last.then_inc(att_spread, 1)
                pe.wait_ge(terms_ready, t + 1)
                nc.tensor.matmul(ps_seg[:, P:P + H + 1], same[:, :], terms[:, :], start=True,
                                 stop=True).then_inc(sums_ready, 1)

            listed_tiles(pe, n, tile)

        @block.scalar
        def _(act):
            act.wait_ge(blanks, 1)
            n = act.value_load(k.nlist[0:1, 0:1], min_val=0, max_val=RP * RC)
            def tile(t):
                act.wait_ge(turned, t + 1)
                nc.scalar.copy(xt_sub[:, :], ps_xs[:, :]).then_inc(turned_sb, 1)
                nc.scalar.copy(xt_obj[:, :], ps_xo[:, :]).then_inc(turned_sb, 1)
                act.wait_ge(qk_ready, t + 1)
                nc.scalar.copy(q_sb[:, :], ps_q[:, :]).then_inc(q_copied, 1)
                act.wait_ge(drop_ready, t + 1)
                nc.scalar.activation(ex[:, :, :], drop[:, :, :], ACT.Exp).then_inc(ex_ready, 1)

            listed_tiles(act, n, tile)

        @block.gpsimd
        def _(gp):
            gp.sem_inc(tile_done, 1)
            n = gp.value_load(k.nlist[0:1, 0:1], min_val=0, max_val=RP * RC)
            def tile(t):
                gp.wait_ge(seg_ready, t + 1)
                gp.sem_inc(gate, 1)
                for rows, table, bound, index in ((x_sub, ins["x"], N - 1, got.sub_i),
                                                  (x_obj, ins["x"], N - 1, got.obj_i),
                                                  (old, k.stats_d, N - 1, got.sub_i)):
                    gp.indirect_dma_start(rows[:, :], None, table, bass.IndirectOffsetOnAxis(ap=index[:, 0:1], axis=0),
                                          bounds_check=bound, oob_is_err=False).then_inc(gath_ld, 16)
                gp.wait_ge(new_ready, t + 1)
                gp.sem_inc(gate, 1)
                gp.indirect_dma_start(k.stats_d, bass.IndirectOffsetOnAxis(ap=first_i[:, 0:1], axis=0), new[:, :],
                                      None, bounds_check=N - 1, oob_is_err=False).then_inc(new_st, 16)
                gp.wait_ge(new_st, 16 * (t + 1))
                gp.sem_inc(tile_done, 1)

            listed_tiles(gp, n, tile)


def node_coefficients(nc, k, ins, c_all, cx_all):
    with ExitStack() as ctx:
        sb, ps, sem = stage(nc, ctx, "coef")
        stats = sb("stats", [P, NT, SR])
        loop = sb("loop", [P, NT])
        ex0, exd = sb("ex0", [P, NT, H]), sb("exd", [P, NT, H])
        others = sb("others", [P, NT])
        z, prod, prod_d = sb("z", [P, NT, H]), sb("prod", [P, NT, H]), sb("prod_d", [P, NT, H])
        cd = sb("cd", [P, NT])
        rows = sb("rows", [P, NT, CR])
        diag_bias = sb("diag_bias", [P, 1])
        empty = sb("empty", [P, NT])
        st_ld, loop_ld, rows_st = sem("st_ld"), sem("loop_ld"), sem("rows_st")
        dve_step, ex_ready, bias_ready, rows_ready = sem("dve_step"), sem("ex_ready"), sem("bias_ready"), sem("rows_ready")
        block = ctx.enter_context(nc.Block())

        @block.sync
        def _(sp):
            sp.dma_start(stats[:, :, :], tiles_of(k.stats_d)).then_inc(st_ld, 16)
            sp.dma_start(loop[:, :], ins["adj_diag"]).then_inc(loop_ld, 16)
            sp.wait_ge(rows_ready, 1)
            sp.dma_start(tiles_of(k.coef_d), rows[:, :, :]).then_inc(rows_st, 16)
            sp.dma_start(k.empty_d.rearrange("(t p) o -> p (t o)", p=P), empty[:, :],
                         allow_slow_non_contiguous=True).then_inc(rows_st, 16)
            sp.wait_ge(rows_st, 32)

        @block.scalar
        def _(act):
            act.wait_ge(st_ld, 16)
            act.wait_ge(bias_ready, 1)
            nc.scalar.activation(ex0[:, :, :], stats[:, :, 0:H], ACT.Exp, scale=-1.0)
            nc.scalar.activation(exd[:, :, :], stats[:, :, 0:H], ACT.Exp, scale=-1.0,
                                 bias=diag_bias[:, 0:1]).then_inc(ex_ready, 1)

        @block.vector
        def _(dve):
            step = Chain(dve, dve_step)
            nc.vector.memset(diag_bias[:, :], DIAG).then_inc(bias_ready, 1)
            nc.vector.tensor_scalar(empty[:, :], k.deg[:, :], 0.0, None, ALU.is_equal)
            dve.wait_ge(loop_ld, 16)
            step.then(nc.vector.tensor_tensor(others[:, :], k.deg[:, :], loop[:, :], ALU.subtract))
            dve.wait_ge(st_ld, 16)
            step.then(nc.vector.tensor_tensor(others[:, :], others[:, :], stats[:, :, 2 * H], ALU.subtract))
            dve.wait_ge(ex_ready, 1)
            step.then(nc.vector.tensor_tensor(z[:, :, :], ex0[:, :, :],
                                              others[:, :].unsqueeze(2).broadcast_to([P, NT, H]), ALU.mult))
            step.then(nc.vector.tensor_tensor(z[:, :, :], z[:, :, :], exd[:, :, :], ALU.add))
            step.then(nc.vector.tensor_tensor(z[:, :, :], z[:, :, :], stats[:, :, H:2 * H], ALU.add))
            step.then(nc.vector.tensor_scalar(z[:, :, :], z[:, :, :], float(H), None, ALU.mult))
            step.then(nc.vector.reciprocal(rows[:, :, H:2 * H], z[:, :, :]))
            nc.vector.tensor_copy(rows[:, :, 0:H], stats[:, :, 0:H]).then_inc(rows_ready, 1)
            nc.vector.tensor_tensor(prod[:, :, :], ex0[:, :, :], rows[:, :, H:2 * H], ALU.mult)
            step.then(nc.vector.tensor_tensor(prod_d[:, :, :], exd[:, :, :], rows[:, :, H:2 * H], ALU.mult))
            nc.vector.tensor_reduce(c_all[:, :], prod[:, :, :], AX, ALU.add)
            step.then(nc.vector.tensor_reduce(cd[:, :], prod_d[:, :, :], AX, ALU.add))
            step.then(nc.vector.tensor_tensor(cx_all[:, :], c_all[:, :], loop[:, :], ALU.mult))
            step.then(nc.vector.tensor_tensor(cx_all[:, :], cd[:, :], cx_all[:, :], ALU.subtract))
            step.then(nc.vector.tensor_scalar(cx_all[:, :], cx_all[:, :], 1.0, None, ALU.add))


def relation_values(nc, k, ins, att_all, weight_all):
    with ExitStack() as ctx:
        sb, ps, sem = stage(nc, ctx, "value")
        got = decoded(sb)
        key_col = sb("key_col", [P, 1])
        diag, same = sb("diag", [P, P]), sb("same", [P, P])
        first_i = sb("first_i", [P, 1], i32)
        x_obj, rel_old, rel_new = sb("x_obj", [P, F]), sb("rel_old", [P, F]), sb("rel_new", [P, F])
        coef = sb("coef", [P, CR])
        drop, ex = sb("drop", [P, 2, H]), sb("ex", [P, 2, H])
        rise, weight = sb("rise", [P, H]), sb("weight", [P, 1])
        value = sb("value", [P, F])
        ps_seg = ps("ps_seg", [P, F])
        ps_val = ps("ps_val", [P, F])
        key_ld, tile_done, gath_ld, new_st = sem("key_ld"), sem("tile_done"), sem("gath_ld"), sem("new_st")
        diag_ready, seg_ready, drop_ready, ex_ready = (sem("diag_ready"), sem("seg_ready"), sem("drop_ready"),
                                                       sem("ex_ready"))
        value_ready, val_summed, new_ready = sem("value_ready"), sem("val_summed"), sem("new_ready")
        dve_step, gate = sem("dve_step"), sem("gate")
        LINKS = 16
        block = ctx.enter_context(nc.Block())

        @block.sync
        def _(sp):
            n = sp.value_load(k.nlist[0:1, 0:1], min_val=0, max_val=RP * RC)
            def tile(t):
                sp.wait_ge(tile_done, t + 1)
                sp.sem_inc(gate, 1)
                sp.dma_start(key_col[:, :], k.list_d[bass.ds(t * P, P), :]).then_inc(key_ld, 16)

            listed_tiles(sp, n, tile)

        @block.vector
        def _(dve):
            n = dve.value_load(k.nlist[0:1, 0:1], min_val=0, max_val=RP * RC)
            def tile(t):
                step = Chain(dve, dve_step, t * LINKS)
                dve.wait_ge(key_ld, 16 * (t + 1))
                decode_tile(nc, dve, step, key_col, got)
                nc.vector.tensor_scalar(diag[:, :], k.ident[:, :], got.seg[:, 0:1], None,
                                        ALU.mult).then_inc(diag_ready, 1)
                dve.wait_ge(gath_ld, 48 * (t + 1))
                nc.vector.tensor_tensor(drop[:, 0, :], att_all[:, bass.ds(t * H, H)], coef[:, 0:H], ALU.subtract)
                nc.vector.tensor_scalar(drop[:, 1, :], coef[:, 0:H], -1.0, None,
                                        ALU.mult).then_inc(drop_ready, 1)
                dve.wait_ge(seg_ready, t + 1)
                same_segment(nc, dve, step, k, got, ps_seg[:, 0:P], same, first_i)
                dve.wait_ge(ex_ready, t + 1)
                step.then(nc.vector.tensor_tensor(rise[:, :], ex[:, 0, :], ex[:, 1, :], ALU.subtract))
                step.then(nc.vector.tensor_tensor(rise[:, :], rise[:, :], coef[:, H:2 * H], ALU.mult))
                step.then(nc.vector.tensor_reduce(weight[:, :], rise[:, :], AX, ALU.add))
                step.then(nc.vector.tensor_tensor(weight[:, :], weight[:, :], weight_all[:, bass.ds(t, 1)],
                                                  ALU.mult))
                nc.vector.tensor_scalar(value[:, :], x_obj[:, :], weight[:, 0:1], None,
                                        ALU.mult).then_inc(value_ready, 1)
                dve.wait_ge(val_summed, t + 1)
                step.then(nc.vector.tensor_tensor(rel_new[:, :], rel_old[:, :], ps_val[:, :], ALU.add))
                nc.vector.tensor_copy(got.count[:, :], got.valid[:, :]).then_inc(new_ready, 1)
                assert step.n == LINKS, step.n

            listed_tiles(dve, n, tile)

        @block.tensor
        def _(pe):
            n = pe.value_load(k.nlist[0:1, 0:1], min_val=0, max_val=RP * RC)
            def tile(t):
                pe.wait_ge(diag_ready, t + 1)
                nc.tensor.matmul(ps_seg[:, 0:P], k.ones[:, :], diag[:, :], start=True,
                                 stop=True).then_inc(seg_ready, 1)
                pe.wait_ge(value_ready, t + 1)
                nc.tensor.matmul(ps_val[:, :], same[:, :], value[:, :], start=True,
                                 stop=True).then_inc(val_summed, 1)

            listed_tiles(pe, n, tile)

        @block.scalar
        def _(act):
            n = act.value_load(k.nlist[0:1, 0:1], min_val=0, max_val=RP * RC)
            def tile(t):
                act.wait_ge(drop_ready, t + 1)
                nc.scalar.activation(ex[:, :, :], drop[:, :, :], ACT.Exp).then_inc(ex_ready, 1)

            listed_tiles(act, n, tile)

        @block.gpsimd
        def _(gp):
            gp.sem_inc(tile_done, 1)
            n = gp.value_load(k.nlist[0:1, 0:1], min_val=0, max_val=RP * RC)
            def tile(t):
                gp.wait_ge(diag_ready, t + 1)
                gp.sem_inc(gate, 1)
                for rows, table, index in ((coef, k.coef_d, got.sub_i), (x_obj, ins["x"], got.obj_i),
                                           (rel_old, k.rel_d, got.sub_i)):
                    gp.indirect_dma_start(rows[:, :], None, table, bass.IndirectOffsetOnAxis(ap=index[:, 0:1], axis=0),
                                          bounds_check=N - 1, oob_is_err=False).then_inc(gath_ld, 16)
                gp.wait_ge(new_ready, t + 1)
                gp.sem_inc(gate, 1)
                gp.indirect_dma_start(k.rel_d, bass.IndirectOffsetOnAxis(ap=first_i[:, 0:1], axis=0), rel_new[:, :],
                                      None, bounds_check=N - 1, oob_is_err=False).then_inc(new_st, 16)
                gp.wait_ge(new_st, 16 * (t + 1))
                gp.sem_inc(tile_done, 1)

            listed_tiles(gp, n, tile)


def project_nodes(nc, k, ins, c_all, cx_all, v_all, sd_all, s_row, x_sum):
    with ExitStack() as ctx:
        sb, ps, sem = stage(nc, ctx, "node")
        parts = sb("parts", [P, 2, 3, F])
        mixed = sb("mixed", [P, 2, F])
        x1 = sb("x1", [P, 2, F])
        x1_t = sb("x1_t", [P, 2, F])
        seen = sb("seen", [P, 2, 6])
        moments = sb("moments", [P, 2, 2])
        rstd, minus_half = sb("rstd", [P, 2]), sb("minus_half", [P, 1])
        ps_turn = [ps(f"ps_turn{b}", [P, F]) for b in range(2)]
        ps_wh = [ps(f"ps_wh{b}", [P, F]) for b in range(2)]
        ps_sd = [ps(f"ps_sd{b}", [P, F]) for b in range(2)]
        ps_srow = [ps(f"ps_srow{b}", [P, F]) for b in range(2)]
        part_ld = [sem(f"part_ld{b}") for b in range(2)]
        x1_st = [sem(f"x1_st{b}") for b in range(2)]
        parts_used, x1_ready, x1_summed = sem("parts_used"), sem("x1_ready"), sem("x1_summed")
        turned, turned_sb, projected, copied = sem("turned"), sem("turned_sb"), sem("projected"), sem("copied")
        dve_step, gate, pool_step = sem("dve_step"), sem("gate"), sem("pool_step")
        moments_ready, rstd_ready = sem("moments_ready"), sem("rstd_ready")
        LINKS = 3
        block = ctx.enter_context(nc.Block())

        @block.sync
        def _(sp):
            sp.sem_inc(x1_st[0], 16)
            sp.sem_inc(x1_st[1], 16)

            def load(t, b):
                sp.wait_ge(parts_used, t + 1)
                sp.sem_inc(gate, 1)
                for i, table in enumerate((k.agg_d, ins["x"], k.rel_d)):
                    sp.dma_start(parts[:, b, i, :], table[bass.ds(t * P, P), :]).then_inc(part_ld[b], 16)

            def store(t, b):
                sp.wait_ge(x1_ready, t + 1)
                sp.sem_inc(gate, 1)
                sp.dma_start(k.x1_d[bass.ds(t * P, P), :], x1[:, b, :]).then_inc(x1_st[b], 16)

            load(0, 0)
            load(1, 1)
            with sp.Fori(0, NT // 2 - 1) as pair:
                for b in range(2):
                    load(2 * pair + b + 2, b)
                    store(2 * pair + b, b)
            for b in range(2):
                store(NT - 2 + b, b)
            for b in range(2):
                sp.wait_ge(x1_st[b], 16 * (NT // 2 + 1))

        @block.vector
        def _(dve):
            dve.sem_inc(parts_used, 2)
            with dve.Fori(0, NT // 2) as pair:
                for b in range(2):
                    t = 2 * pair + b
                    step = Chain(dve, dve_step, t * LINKS)
                    dve.wait_ge(part_ld[b], 48 * (pair + 1))
                    step.then(nc.vector.scalar_tensor_tensor(mixed[:, b, :], parts[:, b, 0, :],
                                                             c_all[:, bass.ds(t, 1)], parts[:, b, 2, :],
                                                             ALU.mult, ALU.add))
                    step.then(nc.vector.scalar_tensor_tensor(mixed[:, b, :], parts[:, b, 1, :],
                                                             cx_all[:, bass.ds(t, 1)], mixed[:, b, :],
                                                             ALU.mult, ALU.add))
                    step.then(nc.vector.bn_stats(seen[:, b, :], mixed[:, b, :]))
                    dve.sem_inc(parts_used, 1)
                    nc.vector.bn_aggr(moments[:, b, :], seen[:, b, :]).then_inc(moments_ready, 1)
                    dve.wait_ge(rstd_ready, t + 1)
                    dve.wait_ge(x1_st[b], 16 * (pair + 1))
                    dve.wait_ge(turned, t + 1)
                    dve.wait_ge(x1_summed, t + 1)
                    nc.vector.tensor_scalar(x1[:, b, :], mixed[:, b, :], moments[:, b, 0:1], rstd[:, b:b + 1],
                                            ALU.subtract, ALU.mult).then_inc(x1_ready, 1)
                    assert step.n == LINKS

        @block.gpsimd
        def _(gp):
            gp.sem_inc(x1_summed, 2)
            nc.gpsimd.memset(minus_half[:, :], -0.5)
            nc.gpsimd.memset(x_sum[:, :], 0.0).then_inc(pool_step, 1)
            gp.wait_ge(pool_step, 1)
            with gp.Fori(0, NT // 2) as pair:
                for b in range(2):
                    t = 2 * pair + b
                    gp.wait_ge(moments_ready, t + 1)
                    gp.sem_inc(gate, 1)
                    nc.gpsimd.tensor_scalar(rstd[:, b:b + 1], moments[:, b, 1:2], EPS, None,
                                            ALU.add).then_inc(pool_step, 1)
                    gp.wait_ge(pool_step, t + 2)
                    nc.gpsimd.tensor_tensor(rstd[:, b:b + 1], rstd[:, b:b + 1], minus_half[:, :],
                                            ALU.pow).then_inc(rstd_ready, 1)
                    gp.wait_ge(x1_ready, t + 1)
                    gp.wait_ge(x1_summed, t + 2)
                    nc.gpsimd.tensor_tensor(x_sum[:, :], x_sum[:, :], x1[:, b, :], ALU.add).then_inc(x1_summed, 1)

        @block.tensor
        def _(pe):
            pe.sem_inc(turned, 2)

            def turn(t, b):
                pe.wait_ge(x1_ready, t + 1)
                for f in range(KF):
                    last = nc.tensor.transpose(ps_turn[b][:, P * f:P * (f + 1)], x1[:, b, P * f:P * (f + 1)],
                                               k.ident[:, :])
                last.then_inc(turned, 1)

            def project(t, b):
                pe.wait_ge(turned_sb, t + 1)
                pe.wait_ge(copied, t + 1)
                for f in range(KF):
                    xt = x1_t[:, b, P * f:P * (f + 1)]
                    nc.tensor.matmul(ps_wh[b][:, :], xt, k.w[:, f, :], start=(f == 0), stop=(f == KF - 1))
                    nc.tensor.matmul(ps_sd[b][:, 0:2 * H], xt, k.wa[:, f, :], start=(f == 0), stop=(f == KF - 1))
                    last = nc.tensor.matmul(ps_srow[b][0:H, 0:P], k.wa[:, f, 0:H], xt, start=(f == 0),
                                            stop=(f == KF - 1))
                last.then_inc(projected, 1)

            turn(0, 0)
            with pe.Fori(0, NT // 2 - 1) as pair:
                turn(2 * pair + 1, 1)
                project(2 * pair, 0)
                turn(2 * pair + 2, 0)
                project(2 * pair + 1, 1)
            turn(NT - 1, 1)
            project(NT - 2, 0)
            project(NT - 1, 1)

        @block.scalar
        def _(act):
            act.sem_inc(copied, 2)

            def keep_turned(t, b):
                act.wait_ge(turned, t + 3)
                nc.scalar.copy(x1_t[:, b, :], ps_turn[b][:, :]).then_inc(turned_sb, 1)

            def keep_projected(t, b):
                act.wait_ge(projected, t + 1)
                nc.scalar.copy(v_all[:, bass.ds(t, 1), :, 0:DH].rearrange("p o h d -> p (o h) d"),
                               ps_wh[b][:, :].rearrange("p (h d) -> p h d", d=DH))
                nc.scalar.copy(sd_all[:, bass.ds(t, 1), :].rearrange("p o h -> p (o h)"), ps_sd[b][:, 0:2 * H])
                nc.scalar.copy(s_row[:, bass.ds(t * P, P)], ps_srow[b][0:H, 0:P]).then_inc(copied, 1)

            keep_turned(0, 0)
            with act.Fori(0, NT // 2 - 1) as pair:
                keep_turned(2 * pair + 1, 1)
                keep_projected(2 * pair, 0)
                keep_turned(2 * pair + 2, 0)
                keep_projected(2 * pair + 1, 1)
            keep_turned(NT - 1, 1)
            keep_projected(NT - 2, 0)
            keep_projected(NT - 1, 1)


def attention_factors(nc, k, v_all, g_all, sd_all, s_row, x_sum, wh_sum):
    with ExitStack() as ctx:
        sb, ps, sem = stage(nc, ctx, "fact")
        d_own, d_max, d_col = sb("d_own", [P, H]), sb("d_max", [P, H]), sb("d_col", [H, 1])
        d_off = sb("d_off", [P, NT, H])
        v_fac = sb("v_fac", [P, NT, H])
        t_row = sb("t_row", [H, N])
        shift = sb("shift", [P, 1])
        x_col = sb("x_col", [P, KF])
        ps_small = ps("ps_small", [P, F])
        ps_x = ps("ps_x", [P, F])
        ps_sum = ps("ps_sum", [P, F])
        own_ready, max_ready, col_ready, z_ready, t_ready = (sem("own_ready"), sem("max_ready"), sem("col_ready"),
                                                             sem("z_ready"), sem("t_ready"))
        off_ready, v_ready, shift_ready, t_st = sem("off_ready"), sem("v_ready"), sem("shift_ready"), sem("t_st")
        x_turned, x_copied, sum_ready, dve_step = (sem("x_turned"), sem("x_copied"), sem("sum_ready"),
                                                   sem("dve_step"))
        block = ctx.enter_context(nc.Block())

        @block.vector
        def _(dve):
            step = Chain(dve, dve_step)
            nc.vector.memset(shift[:, :], SHIFT).then_inc(shift_ready, 1)
            nc.vector.tensor_reduce(d_own[:, :], sd_all[:, :, H:2 * H].rearrange("p t h -> p h t"), AX,
                                    ALU.max).then_inc(own_ready, 1)
            dve.wait_ge(x_turned, 1)
            nc.vector.tensor_copy(x_col[:, :], ps_x[:, 0:KF]).then_inc(x_copied, 1)
            dve.wait_ge(max_ready, 1)
            nc.vector.tensor_tensor(d_off[:, :, :], sd_all[:, :, H:2 * H],
                                    d_max[:, :].unsqueeze(1).broadcast_to([P, NT, H]),
                                    ALU.subtract).then_inc(off_ready, 1)
            dve.wait_ge(col_ready, 1)
            step.then(nc.vector.tensor_copy(d_col[:, :], ps_small[0:H, 0:1]))
            nc.vector.tensor_scalar(t_row[:, :], s_row[:, :], d_col[:, 0:1], 0.0, ALU.add,
                                    ALU.max).then_inc(z_ready, 1)
            dve.wait_ge(sum_ready, 1)
            nc.vector.tensor_copy(wh_sum[:, :], ps_sum[0:1, :])
            dve.wait_ge(v_ready, 1)
            nc.vector.tensor_copy(v_all[:, :, :, DH], v_fac[:, :, :])
            for t in range(0, NT, CH):
                last = nc.vector.tensor_tensor(
                    v_all[:, t:t + CH, :, 0:DH].rearrange("p t h d -> p (t h) d"),
                    v_all[:, t:t + CH, :, 0:DH].rearrange("p t h d -> p (t h) d"),
                    v_fac[:, t:t + CH, :].rearrange("p t h -> p (t h)").unsqueeze(2).broadcast_to([P, CH * H, DH]),
                    ALU.mult)

        @block.gpsimd
        def _(gp):
            gp.wait_ge(own_ready, 1)
            nc.gpsimd.partition_all_reduce(d_max[:, :], d_own[:, :], P,
                                           bass.bass_isa.ReduceOp.max).then_inc(max_ready, 1)

        @block.tensor
        def _(pe):
            for f in range(KF):
                last = nc.tensor.matmul(ps_x[:, f:f + 1], x_sum[:, P * f:P * (f + 1)], k.ones[:, 0:1], start=True,
                                        stop=True)
            last.then_inc(x_turned, 1)
            pe.wait_ge(x_copied, 1)
            for f in range(KF):
                last = nc.tensor.matmul(ps_sum[0:1, :], x_col[:, f:f + 1], k.w[:, f, :], start=(f == 0),
                                        stop=(f == KF - 1))
            last.then_inc(sum_ready, 1)
            pe.wait_ge(max_ready, 1)
            nc.tensor.matmul(ps_small[0:H, 0:1], d_max[0:1, :], k.ones[0:1, 0:1], start=True,
                             stop=True).then_inc(col_ready, 1)

        @block.scalar
        def _(act):
            act.wait_ge(shift_ready, 1)
            act.wait_ge(off_ready, 1)
            nc.scalar.activation(v_fac[:, :, :], d_off[:, :, :], ACT.Exp, scale=0.2,
                                 bias=shift[:, 0:1]).then_inc(v_ready, 1)
            nc.scalar.activation(g_all[:, :, :], d_off[:, :, :], ACT.Exp, scale=0.8, bias=shift[:, 0:1])
            act.wait_ge(z_ready, 1)
            nc.scalar.activation(t_row[:, :], t_row[:, :], ACT.Exp, scale=-0.8,
                                 bias=shift[0:H, 0:1]).then_inc(t_ready, 1)
            act.wait_ge(t_ready, 1)
            act.dma_start(k.trow_d, t_row[:, :]).then_inc(t_st, 16)
            act.wait_ge(t_st, 16)


def attend(nc, k, ins, v_all, g_all, wh_sum, out):
    with ExitStack() as ctx:
        sb, ps, sem = stage(nc, ctx, "att")
        R = 4
        HG = 4
        adj8 = sb("adj8", [P, PIECES, CH * SEC], u8)
        t_bc = sb("t_bc", [P, 2, HG, SEC])
        empty = sb("empty", [1, 2, SEC])
        n_row = sb("n_row", [1, 32])
        weights = sb("weights", [P, R, HG, SEC])
        num = sb("num", [P, 2, SEC])
        den = sb("den", [P, SEC])
        den_bc = sb("den_bc", [P, 2, SEC])
        pick = sb("pick", [P, HG * DH])
        low = sb("low", [P, 2, SEC])
        enc = sb("enc", [P, 4, SEC])
        hid1, hid2, hid3 = sb("hid1", [P, 2, SEC]), sb("hid2", [P, SEC]), sb("hid3", [P, 2, SEC])
        w1, w2, w3, w4 = (sb("w1", [P, 4, M1]), sb("w2", [P, 2, M2]), sb("w3", [P, M3]), sb("w4", [P, 2, F]))
        b1, b2, b3 = sb("b1", [P, 2]), sb("b2", [P, 1]), sb("b3", [P, 2])
        b4 = sb("b4", [P, F])
        base = sb("base", [P, 4, F])
        y = sb("y", [P, 4, F])
        seen, moments, rstd = sb("seen", [P, 4, 6]), sb("moments", [P, 4, 2]), sb("rstd", [P, 4])
        ps_num = [[ps(f"ps_num{g}{p}", [P, SEC]) for p in range(2)] for g in range(2)]
        ps_den = [ps(f"ps_den{g}", [P, SEC]) for g in range(2)]
        ps_mlp = [ps(f"ps_mlp{b}", [P, SEC]) for b in range(2)]

        par_ld, x1_ld, out_st = sem("par_ld"), sem("x1_ld"), sem("out_st")
        adj_ld = [sem(f"adj_ld{i}") for i in range(PIECES)]
        t_ld = [sem(f"t_ld{g}") for g in range(2)]
        made, used = sem("made"), sem("used")
        num_copied, den_ready = sem("num_copied"), sem("den_ready")
        den_spread, den_copied, ratio_ready = sem("den_spread"), sem("den_copied"), sem("ratio_ready")
        exp_ready, enc_ready = sem("exp_ready"), sem("enc_ready")
        mlp_ready, hid_ready, y_mlp, y_part = sem("mlp_ready"), sem("hid_ready"), sem("y_mlp"), sem("y_part")
        y_ready, base_ready, n_ready = sem("y_ready"), sem("base_ready"), sem("n_ready")
        act_step, dve_step, pool_step, gate = sem("act_step"), sem("dve_step"), sem("pool_step"), sem("gate")
        moments_ready, rstd_ready, rstd_step = sem("moments_ready"), sem("rstd_ready"), sem("rstd_step")
        minus_half = sb("minus_half", [P, 4])
        y_free = sem("y_free")
        PARAMS = 9
        block = ctx.enter_context(nc.Block())

        def before_group(c, g):
            return (2 * c + g) * NT

        @block.sync
        def _(sp):
            def load_factors(c, g):
                sp.dma_start(t_bc[:, g, :, :],
                             k.trow_d[HG * g:HG * (g + 1), bass.ds(c * SEC, SEC)].unsqueeze(0)
                             .broadcast_to([P, HG, SEC])).then_inc(t_ld[g], 16)
                sp.dma_start(empty[0:1, g, :],
                             k.empty_d.rearrange("n o -> o n")[:, bass.ds(c * SEC, SEC)]).then_inc(t_ld[g], 16)

            def load_piece(c, i):
                sp.dma_start(adj8[:, i, :],
                             k.adj8_d[bass.ds(c, 1), i, :, :].rearrange("o p n -> p (o n)")).then_inc(adj_ld[i], 16)

            load_factors(0, 0)
            for i in range(PIECES):
                load_piece(0, i)
            load_factors(0, 1)
            for dst, name in ((pick, "pick"), (b1, "b1"), (b2, "b2"), (b3, "b3"), (w3, "w3_t")):
                sp.dma_start(dst[:, :], ins[name]).then_inc(par_ld, 16)
            for dst, name in ((w1, "w1_t"), (w2, "w2_t"), (w4, "w4_t")):
                sp.dma_start(dst[:, :, :], tiles_of(ins[name])).then_inc(par_ld, 16)
            sp.dma_start(b4[:, :], ins["b4"].broadcast_to([P, F])).then_inc(par_ld, 16)
            with sp.Fori(0, SECS - 1) as c:
                sp.wait_ge(used, before_group(c, 1) + R)
                sp.sem_inc(gate, 1)
                load_factors(c + 1, 0)
                for i in range(PIECES):
                    sp.wait_ge(made, before_group(c, 1) + CH * (i + 1))
                    sp.sem_inc(gate, 1)
                    load_piece(c + 1, i)
                sp.wait_ge(used, before_group(c, 2) + R)
                sp.sem_inc(gate, 1)
                load_factors(c + 1, 1)

        @block.vector
        def _(dve):
            nc.vector.memset(n_row[:, :], float(N)).then_inc(n_ready, 1)
            dve.sem_inc(y_part, 2)

            def invert_sums(c, g):
                dve.wait_ge(used, before_group(c, g + 1) + R)
                if not (isinstance(c, int) and c == 0 and g == 0):
                    dve.wait_ge(den_spread, 2 * c + g)
                nc.vector.reciprocal(den[:, :], ps_den[g][:, :]).then_inc(den_ready, 1)

            def add_residual(c, half):
                dve.wait_ge(y_mlp, 2 * c + half + 1)
                if half == 0:
                    dve.wait_ge(base_ready, c + 1)
                    dve.wait_ge(y_free, c + 1)
                nc.vector.tensor_tensor(y[:, 2 * half, :], ps_mlp[0][:, :], base[:, 2 * half, :], ALU.add)
                nc.vector.tensor_tensor(y[:, 2 * half + 1, :], ps_mlp[1][:, :], base[:, 2 * half + 1, :],
                                        ALU.add).then_inc(y_part, 1)

            def normalise(c):
                dve.wait_ge(y_part, 2 * c + 4)
                for i in range(4):
                    last = nc.vector.bn_stats(seen[:, i, :], y[:, i, :])
                last.then_inc(dve_step, 1)
                dve.wait_ge(dve_step, c + 1)
                dve.sem_inc(gate, 1)
                for i in range(4):
                    last = nc.vector.bn_aggr(moments[:, i, :], seen[:, i, :])
                last.then_inc(moments_ready, 1)

            def scale_rows(c):
                dve.wait_ge(rstd_ready, c + 1)
                for i in range(4):
                    last = nc.vector.tensor_scalar(y[:, i, :], y[:, i, :], moments[:, i, 0:1], rstd[:, i:i + 1],
                                                   ALU.subtract, ALU.mult)
                last.then_inc(y_ready, 1)

            def make_weights(c, g, meanwhile):
                dve.wait_ge(t_ld[g], 32 * (c + 1))
                for j in range(NT):
                    if j in meanwhile:
                        meanwhile[j]()
                    if g == 0 and j % CH == 0:
                        dve.wait_ge(adj_ld[j // CH], 16 * (c + 1))
                    dve.wait_ge(used, before_group(c, g) + j + 1)
                    for h in range(HG):
                        last = nc.vector.scalar_tensor_tensor(
                            weights[:, j % R, h, :], t_bc[:, g, h, :], g_all[:, j, HG * g + h:HG * g + h + 1],
                            adj8[:, j // CH, SEC * (j % CH):SEC * (j % CH + 1)], ALU.max, ALU.mult)
                    last.then_inc(made, 1)

            make_weights(0, 0, {})
            make_weights(0, 1, {R: lambda: invert_sums(0, 0)})
            with dve.Fori(1, SECS) as c:
                make_weights(c, 0, {R: lambda: invert_sums(c - 1, 1), 28: lambda: add_residual(c - 1, 0)})
                make_weights(c, 1, {2: lambda: add_residual(c - 1, 1), R: lambda: invert_sums(c, 0),
                                    8: lambda: normalise(c - 1), 24: lambda: scale_rows(c - 1)})
            c = SECS - 1
            invert_sums(c, 1)
            add_residual(c, 0)
            add_residual(c, 1)
            normalise(c)
            scale_rows(c)

        @block.tensor
        def _(pe):
            pe.sem_inc(used, R)
            pe.sem_inc(mlp_ready, 3)
            pe.wait_ge(n_ready, 1)

            def spread_sums(c, g):
                pe.wait_ge(den_ready, 2 * c + g + 1)
                if not (isinstance(c, int) and c == 0 and g == 0):
                    pe.wait_ge(den_copied, 2 * c + g)
                pe.wait_ge(y_part, 2 * c + 2)
                for p in range(2):
                    last = nc.tensor.matmul(ps_mlp[p][:, :], pick[:, P * p:P * (p + 1)], den[:, :], start=True,
                                            stop=True)
                last.then_inc(den_spread, 1)

            def hidden1(c):
                pe.wait_ge(enc_ready, 2 * c + 2)
                pe.wait_ge(den_copied, 2 * c + 2)
                for m in range(2):
                    for e in range(4):
                        last = nc.tensor.matmul(ps_mlp[m][:, :], w1[:, e, P * m:P * (m + 1)], enc[:, e, :],
                                                start=(e == 0), stop=(e == 3))
                last.then_inc(mlp_ready, 1)

            def hidden2(c):
                pe.wait_ge(hid_ready, 3 * c + 1)
                for e in range(2):
                    last = nc.tensor.matmul(ps_mlp[0][:, :], w2[:, e, :], hid1[:, e, :], start=(e == 0), stop=(e == 1))
                last.then_inc(mlp_ready, 1)

            def hidden3(c):
                pe.wait_ge(hid_ready, 3 * c + 2)
                for m in range(2):
                    last = nc.tensor.matmul(ps_mlp[m][:, :], w3[:, P * m:P * (m + 1)], hid2[:, :], start=True,
                                            stop=True)
                last.then_inc(mlp_ready, 1)

            def output(c, half):
                if half == 0:
                    pe.wait_ge(hid_ready, 3 * c + 3)
                else:
                    pe.wait_ge(y_part, 2 * c + 3)
                for b in range(2):
                    i = 2 * half + b
                    for e in range(2):
                        last = nc.tensor.matmul(ps_mlp[b][:, :], hid3[:, e, P * i:P * (i + 1)], w4[:, e, :],
                                                start=(e == 0), stop=(e == 1))
                last.then_inc(y_mlp, 1)

            def sum_group(c, g, meanwhile):
                if not (isinstance(c, int) and c == 0):
                    pe.wait_ge(num_copied, 2 * c + g - 1)
                    pe.wait_ge(den_ready, 2 * c + g - 1)
                pe.wait_ge(t_ld[g], 32 * (c + 1))
                for p in range(2):
                    for s in range(2):
                        h = HG * g + 2 * p + s
                        nc.tensor.matmul(ps_num[g][p][DH * s:DH * (s + 1), :], wh_sum[0:1, DH * h:DH * (h + 1)],
                                         empty[0:1, g, :], start=True, stop=False)
                for h in range(HG):
                    nc.tensor.matmul(ps_den[g][32 * h:32 * (h + 1), :], n_row[0:1, :], empty[0:1, g, :], start=True,
                                     stop=False, tile_position=(0, 32 * h))
                for j in range(NT):
                    if j in meanwhile:
                        meanwhile[j]()
                    pe.wait_ge(made, before_group(c, g) + j + 1)
                    for p in range(2):
                        for s in range(2):
                            h = HG * g + 2 * p + s
                            nc.tensor.matmul(ps_num[g][p][DH * s:DH * (s + 1), :], v_all[:, j, h, 0:DH],
                                             weights[:, j % R, 2 * p + s, :], start=False, stop=(j == NT - 1))
                    for h in range(HG):
                        last = nc.tensor.matmul(ps_den[g][32 * h:32 * (h + 1), :],
                                                v_all[:, j, HG * g + h, DH:DH + 1].broadcast_to([P, 32]),
                                                weights[:, j % R, h, :], start=False, stop=(j == NT - 1),
                                                tile_position=(0, 32 * h))
                    last.then_inc(used, 1)

            sum_group(0, 0, {})
            pe.wait_ge(par_ld, 16 * PARAMS)
            sum_group(0, 1, {6: lambda: spread_sums(0, 0)})
            with pe.Fori(1, SECS) as c:
                sum_group(c, 0, {6: lambda: spread_sums(c - 1, 1), 12: lambda: hidden1(c - 1),
                                 16: lambda: hidden2(c - 1), 20: lambda: hidden3(c - 1),
                                 24: lambda: output(c - 1, 0), 30: lambda: output(c - 1, 1)})
                sum_group(c, 1, {6: lambda: spread_sums(c, 0)})
            c = SECS - 1
            spread_sums(c, 1)
            hidden1(c)
            hidden2(c)
            hidden3(c)
            output(c, 0)
            output(c, 1)

        @block.scalar
        def _(act):
            act.wait_ge(par_ld, 16 * PARAMS)

            def finish_group(c, g):
                act.wait_ge(used, before_group(c, g + 1) + R)
                act.wait_ge(ratio_ready, 2 * c + g + 1)
                nc.scalar.copy(num[:, 0, :], ps_num[g][0][:, :])
                nc.scalar.copy(num[:, 1, :], ps_num[g][1][:, :]).then_inc(num_copied, 1)
                act.wait_ge(den_spread, 2 * c + g + 1)
                nc.scalar.copy(den_bc[:, 0, :], ps_mlp[0][:, :])
                nc.scalar.copy(den_bc[:, 1, :], ps_mlp[1][:, :]).then_inc(den_copied, 1)
                act.wait_ge(ratio_ready, 2 * c + g + 2)
                if not (isinstance(c, int) and c == 0 and g == 0):
                    act.wait_ge(enc_ready, 2 * c + g)
                part = enc[:, 2 * g:2 * g + 2, :]
                nc.scalar.activation(low[:, :, :], part, ACT.Relu, scale=-1.0).then_inc(act_step, 1)
                act.wait_ge(act_step, 2 * c + g + 1)
                nc.scalar.activation(low[:, :, :], low[:, :, :], ACT.Exp, scale=-1.0)
                nc.scalar.activation(part, part, ACT.Relu).then_inc(exp_ready, 1)

            def hidden(c, n):
                act.wait_ge(mlp_ready, 3 * c + n + 4)
                if n == 0:
                    nc.scalar.activation(hid1[:, 0, :], ps_mlp[0][:, :], ACT.Relu, bias=b1[:, 0:1])
                    last = nc.scalar.activation(hid1[:, 1, :], ps_mlp[1][:, :], ACT.Relu, bias=b1[:, 1:2])
                elif n == 1:
                    last = nc.scalar.activation(hid2[:, :], ps_mlp[0][:, :], ACT.Relu, bias=b2[:, 0:1])
                else:
                    act.wait_ge(y_part, 2 * c + 2)
                    nc.scalar.activation(hid3[:, 0, :], ps_mlp[0][:, :], ACT.Relu, bias=b3[:, 0:1])
                    last = nc.scalar.activation(hid3[:, 1, :], ps_mlp[1][:, :], ACT.Relu, bias=b3[:, 1:2])
                last.then_inc(hid_ready, 1)

            finish_group(0, 0)
            with act.Fori(1, SECS) as c:
                finish_group(c - 1, 1)
                for n in range(3):
                    hidden(c - 1, n)
                finish_group(c, 0)
            finish_group(SECS - 1, 1)
            for n in range(3):
                hidden(SECS - 1, n)

        @block.gpsimd
        def _(gp):
            gp.sem_inc(ratio_ready, 1)
            gp.sem_inc(y_free, 1)
            nc.gpsimd.memset(minus_half[:, :], -0.5).then_inc(rstd_step, 1)
            gp.wait_ge(par_ld, 16 * PARAMS)

            def load_x1(c):
                gp.wait_ge(y_part, 2 * c + 2)
                gp.sem_inc(gate, 1)
                gp.dma_start(base[:, :, :], tiles_of(k.x1_d)[:, bass.ds(4 * c, 4), :]).then_inc(x1_ld, 16)

            def add_bias(c):
                gp.wait_ge(x1_ld, 16 * (c + 1))
                nc.gpsimd.tensor_tensor(base[:, :, :], base[:, :, :],
                                        b4[:, :].unsqueeze(1).broadcast_to([P, 4, F]), ALU.add).then_inc(base_ready, 1)

            def invert_spread(c):
                gp.wait_ge(moments_ready, c + 1)
                gp.sem_inc(gate, 1)
                nc.gpsimd.tensor_scalar(rstd[:, :], moments[:, :, 1], EPS, None, ALU.add).then_inc(rstd_step, 1)
                gp.wait_ge(rstd_step, c + 2)
                nc.gpsimd.tensor_tensor(rstd[:, :], rstd[:, :], minus_half[:, :], ALU.pow).then_inc(rstd_ready, 1)

            def store_out(c):
                gp.wait_ge(y_ready, c + 1)
                gp.sem_inc(gate, 1)
                gp.dma_start(tiles_of(out)[:, bass.ds(4 * c, 4), :], y[:, :, :]).then_inc(out_st, 16)
                gp.wait_ge(out_st, 16 * (c + 1))
                gp.sem_inc(y_free, 1)

            def finish_group(c, g):
                gp.wait_ge(den_copied, 2 * c + g + 1)
                gp.wait_ge(num_copied, 2 * c + g + 1)
                part = enc[:, 2 * g:2 * g + 2, :]
                gp.wait_ge(mlp_ready, 3 * c + 1)
                nc.gpsimd.tensor_tensor(part, num[:, :, :], den_bc[:, :, :], ALU.mult).then_inc(ratio_ready, 1)
                gp.wait_ge(exp_ready, 2 * c + g + 1)
                gp.sem_inc(gate, 1)
                nc.gpsimd.tensor_scalar(low[:, :, :], low[:, :, :], -1.0, None, ALU.add).then_inc(pool_step, 1)
                gp.wait_ge(pool_step, 2 * c + g + 1)
                nc.gpsimd.tensor_tensor(part, part, low[:, :, :], ALU.add).then_inc(enc_ready, 1)

            load_x1(0)
            add_bias(0)
            finish_group(0, 0)
            with gp.Fori(1, SECS) as c:
                finish_group(c - 1, 1)
                load_x1(c)
                finish_group(c, 0)
                add_bias(c)
                invert_spread(c - 1)
                store_out(c - 1)
            finish_group(SECS - 1, 1)
            invert_spread(SECS - 1)
            store_out(SECS - 1)


def build(nc, ins, out):
    with ExitStack() as ctx:
        k = make_kept(nc, ctx)
        c_all = ctx.enter_context(nc.sbuf_tensor("c_all", [P, NT], f32))
        cx_all = ctx.enter_context(nc.sbuf_tensor("cx_all", [P, NT], f32))
        with nc.sbuf_tensor("key_row", [P, LIST], f32) as key_row:
            with nc.sbuf_tensor("xs", [P, NT, 2 * F], f16) as xs:
                split_features(nc, k, ins, xs)
                neighbour_sums(nc, k, ins, xs, key_row)
            with (nc.sbuf_tensor("att_all", [P, RT * H], f32) as att_all,
                  nc.sbuf_tensor("weight_all", [P, RT], f32) as weight_all):
                relation_scores(nc, k, ins, key_row, att_all, weight_all)
                node_coefficients(nc, k, ins, c_all, cx_all)
                relation_values(nc, k, ins, att_all, weight_all)
        v_all = ctx.enter_context(nc.sbuf_tensor("v_all", [P, NT, H, DH + 1], f32))
        g_all = ctx.enter_context(nc.sbuf_tensor("g_all", [P, NT, H], f32))
        wh_sum = ctx.enter_context(nc.sbuf_tensor("wh_sum", [1, F], f32))
        with (nc.sbuf_tensor("sd_all", [P, NT, 2 * H], f32) as sd_all,
              nc.sbuf_tensor("s_row", [H, N], f32) as s_row,
              nc.sbuf_tensor("x_sum", [P, F], f32) as x_sum):
            project_nodes(nc, k, ins, c_all, cx_all, v_all, sd_all, s_row, x_sum)
            attention_factors(nc, k, v_all, g_all, sd_all, s_row, x_sum, wh_sum)
        attend(nc, k, ins, v_all, g_all, wh_sum, out)

_LAY = {
    "x": lambda np, a: a["x"],
    "adj_t": lambda np, a: a["adj"].T,
    "adj_diag": lambda np, a: np.diagonal(a["adj"]).reshape(NT, P).T,
    "pairs": lambda np, a: a["L0_gnn_rel_pair_index"],
    "W": lambda np, a: a["L1_gnn_W"].transpose(1, 0, 2).reshape(F, H * DH),
    "a1": lambda np, a: a["L1_gnn_a1"].reshape(1, F),
    "a2": lambda np, a: a["L1_gnn_a2"].reshape(1, F),
    "wq_t": lambda np, a: a["L0_gnn_Wq"].T,
    "wk_t": lambda np, a: a["L0_gnn_Wk"].T,
    "bq": lambda np, a: a["L0_gnn_bq"].reshape(1, F),
    "bk": lambda np, a: a["L0_gnn_bk"].reshape(1, F),
    "w1_t": lambda np, a: a["L1_gnn_W1"].T,
    "w2_t": lambda np, a: a["L1_gnn_W2"].T,
    "w3_t": lambda np, a: a["L1_gnn_W3"].T,
    "w4_t": lambda np, a: a["L1_gnn_W4"].T,
    "b1": lambda np, a: a["L1_gnn_b1"].reshape(2, P).T,
    "b2": lambda np, a: a["L1_gnn_b2"].reshape(1, P).T,
    "b3": lambda np, a: a["L1_gnn_b3"].reshape(2, P).T,
    "b4": lambda np, a: a["L1_gnn_b4"].reshape(1, F),
    "ident": lambda np, a: np.eye(P, dtype=np.float32),
    "before": lambda np, a: np.tril(np.ones((P, P), np.float32), -1),
    "pick": lambda np, a: np.concatenate([np.repeat(np.eye(P, dtype=np.float32)[:, 32 * h:32 * h + 1], DH, axis=1)
                                          for h in range(4)], axis=1),
}


def kernel(**inputs):
    import numpy as _np
    import concourse.bacc as _bacc
    from concourse.bass_utils import run_bass_kernel_spmd as _run

    nc = _bacc.Bacc("TRN2", target_bir_lowering=False, num_devices=1)
    given = {n: _np.asarray(v) for n, v in inputs.items()}
    arrays, ins = {}, {}
    for name, lay in _LAY.items():
        a = _np.ascontiguousarray(lay(_np, given))
        arrays[f"in_{name}_dram"] = a
        ins[name] = nc.dram_tensor(f"in_{name}_dram", a.shape, mybir.dt.from_np(a.dtype), kind="ExternalInput").ap()
    out = nc.dram_tensor("out_0_dram", (N, F), f32, kind="ExternalOutput").ap()
    build(nc, ins, out)
    return _run(nc, [arrays], core_ids=[0]).results[0]["out_0_dram"]
```

```python
import concourse.bass as bass
from concourse import mybir
from contextlib import ExitStack

P = 128
N, F, H, DH = 4096, 512, 8, 64
NT, KF = N // P, F // P
RP, RC = 125, 80
RT = -(-RP * RC // P)
LIST = (RT + 1) * P
SEC, SECS = 512, N // 512
DS, NS = 256, N // 256
GT = 4
MG = 3
ROW = H * (DH + 1) + H
CH = 4
PIECES = NT // CH
SR = 32
CR = 16
DIAG, EPS = 1e-7, 1e-5
SHIFT = 34.0
BIG = 1.0e30
OFF = 16384.0
M1, M2, M3 = 256, 128, 256

f32, f16, i32, u8 = mybir.dt.float32, mybir.dt.float16, mybir.dt.int32, mybir.dt.uint8
ALU = mybir.AluOpType
ACT = mybir.ActivationFunctionType
AX = mybir.AxisListType.X


class Chain:

    def __init__(self, eng, sem, base=0):
        self.eng, self.sem, self.base, self.n = eng, sem, base, 0

    def then(self, ins):
        self.n += 1
        ins.then_inc(self.sem, 1)
        self.eng.wait_ge(self.sem, self.base + self.n)


def tiles_of(ap):
    return ap.rearrange("(t p) f -> p t f", p=P)


def stage(nc, ctx, of):
    sems = []

    def give_back():
        nc.clear_and_free_semaphores(sems)
        nc.all_engine_barrier()

    ctx.callback(give_back)

    def sb(name, shape, dt=f32):
        return ctx.enter_context(nc.sbuf_tensor(f"{of}_{name}", shape, dt))

    def ps(name, shape):
        return ctx.enter_context(nc.psum_tensor(f"{of}_{name}", shape, f32))

    def sem(name):
        sems.append(nc.alloc_semaphore(f"{of}_{name}"))
        return sems[-1]

    return sb, ps, sem


class Kept:
    pass


def make_kept(nc, ctx):
    k = Kept()

    def sb(name, shape, dt=f32):
        return ctx.enter_context(nc.sbuf_tensor(name, shape, dt))

    def dram(name, shape, dt=f32):
        return nc.dram_tensor(name, shape, dt, kind="Internal").ap()

    k.ident = sb("ident", [P, P])
    k.before = sb("before", [P, P])
    k.ones = sb("ones", [P, P])
    k.w = sb("w", [P, KF, F])
    k.wa = sb("wa", [P, KF, 2 * H])
    k.scale = sb("scale", [P, 2])
    k.deg = sb("deg", [P, NT])
    k.nlist = sb("nlist", [P, 1], i32)
    k.marks = sb("marks", [P, NS, NT], f16)
    k.groups = sb("groups", [P, NS], i32)
    k.first = sb("first", [P, NS], i32)
    k.index = sb("index", [P, NS, NT, 2], i32)
    k.rows_st = ctx.enter_context(nc.semaphore("rows_st"))
    k.row_d = dram("row_d", [N + 1, ROW])
    k.agg_d = dram("agg_d", [N, F])
    k.rel_d = dram("rel_d", [N, F])
    k.stats_d = dram("stats_d", [N, SR])
    k.coef_d = dram("coef_d", [N, CR])
    k.list_d = dram("list_d", [LIST, 1])
    k.tot_d = dram("tot_d", [1, P])
    k.x1_d = dram("x1_d", [N, F])
    k.trow_d = dram("trow_d", [H, N])
    k.empty_d = dram("empty_d", [N, 1])
    k.bcol_d = dram("bcol_d", [1, F])
    return k


def split_features(nc, k, ins, xs):
    with ExitStack() as ctx:
        sb, ps, sem = stage(nc, ctx, "split")
        x_sb = sb("x_sb", [P, NT, F])
        a_row = sb("a_row", [P, 2, F])
        a_prod = sb("a_prod", [P, KF, F])
        part_max = sb("part_max", [P, PIECES])
        own_max = sb("own_max", [P, 1])
        all_max = sb("all_max", [P, 1])
        floor_max = sb("floor_max", [P, 1])
        exponent = sb("exponent", [P, 1], i32)
        x_in = [sem(f"x_in{i}") for i in range(PIECES)]
        w_in, const_in = sem("w_in"), sem("const_in")
        dve_step, own_ready, max_ready = sem("dve_step"), sem("own_ready"), sem("max_ready")
        scale_ready, high_ready, split_done = sem("scale_ready"), sem("high_ready"), sem("split_done")
        block = ctx.enter_context(nc.Block())

        @block.sync
        def _(sp):
            sp.dma_start(k.w[:, :, :], ins["W"].rearrange("(t p) f -> p t f", p=P)).then_inc(w_in, 16)
            sp.dma_start(a_row[:, 0, :], ins["a1"].broadcast_to([P, F])).then_inc(w_in, 16)
            sp.dma_start(a_row[:, 1, :], ins["a2"].broadcast_to([P, F])).then_inc(w_in, 16)
            for i in range(PIECES):
                sp.dma_start(x_sb[:, CH * i:CH * (i + 1), :],
                             tiles_of(ins["x"])[:, CH * i:CH * (i + 1), :]).then_inc(x_in[i], 16)
            sp.dma_start(k.ident[:, :], ins["ident"]).then_inc(const_in, 16)
            sp.dma_start(k.before[:, :], ins["before"]).then_inc(const_in, 16)
            sp.wait_ge(const_in, 32)

        @block.vector
        def _(dve):
            step = Chain(dve, dve_step)
            nc.vector.memset(k.ones[:, :], 1.0)
            dve.wait_ge(w_in, 48)
            for a in range(2):
                for t in range(KF):
                    last = nc.vector.tensor_tensor(a_prod[:, t, :], k.w[:, t, :], a_row[:, a, :], ALU.mult)
                step.then(last)
                for t in range(KF):
                    last = nc.vector.tensor_reduce(k.wa[:, t, H * a:H * (a + 1)],
                                                   a_prod[:, t, :].rearrange("p (h d) -> p h d", d=DH), AX, ALU.add)
                step.then(last)
            for i in range(PIECES):
                dve.wait_ge(x_in[i], 16)
                last = nc.vector.tensor_reduce(part_max[:, i:i + 1],
                                               x_sb[:, CH * i:CH * (i + 1), :].rearrange("p t f -> p (t f)"),
                                               AX, ALU.max, apply_absolute_value=True)
            step.then(last)
            nc.vector.tensor_reduce(own_max[:, :], part_max[:, :], AX, ALU.max).then_inc(own_ready, 1)
            dve.wait_ge(max_ready, 1)
            step.then(nc.vector.tensor_scalar(floor_max[:, :], all_max[:, :], 1e-20, None, ALU.max))
            step.then(nc.vector.tensor_single_scalar(exponent[:, :], floor_max[:, :].bitcast(i32),
                                                     0x7F800000, ALU.bitwise_and))
            step.then(nc.vector.tensor_scalar(k.scale[:, 0:1].bitcast(i32), exponent[:, :],
                                              -1.0, float(268 << 23), ALU.mult, ALU.add))
            nc.vector.tensor_scalar(k.scale[:, 1:2].bitcast(i32), exponent[:, :],
                                    float(-(14 << 23)), None, ALU.add).then_inc(scale_ready, 1)
            dve.wait_ge(scale_ready, 1)
            for i in range(PIECES):
                dve.wait_ge(high_ready, i + 1)
                last = nc.vector.scalar_tensor_tensor(xs[:, CH * i:CH * (i + 1), F:2 * F],
                                                      x_sb[:, CH * i:CH * (i + 1), :], k.scale[:, 0:1],
                                                      xs[:, CH * i:CH * (i + 1), 0:F], ALU.mult, ALU.subtract)
            last.then_inc(split_done, 1)
            dve.wait_ge(split_done, 1)

        @block.gpsimd
        def _(gp):
            gp.wait_ge(own_ready, 1)
            nc.gpsimd.partition_all_reduce(all_max[:, :], own_max[:, :], P,
                                           bass.bass_isa.ReduceOp.max).then_inc(max_ready, 1)

        @block.scalar
        def _(act):
            act.wait_ge(scale_ready, 1)
            for i in range(PIECES):
                nc.scalar.activation(xs[:, CH * i:CH * (i + 1), 0:F], x_sb[:, CH * i:CH * (i + 1), :], ACT.Copy,
                                     scale=k.scale[:, 0:1]).then_inc(high_ready, 1)


def neighbour_sums(nc, k, ins, xs, key_row):
    with ExitStack() as ctx:
        sb, ps, sem = stage(nc, ctx, "sums")
        R = 4
        adj_in = sb("adj_in", [P, R, CH, SEC])
        adj16 = sb("adj16", [P, R, CH, SEC], f16)
        agg = sb("agg", [P, 4, F])
        one16 = sb("one16", [P, 1], f16)
        zeros = sb("zeros", [P, 1024])
        rows0 = sb("rows0", [P, NT, SR])
        blank = sb("blank", [P, LIST // P])
        pairs = sb("pairs", [RP, RC, 2], i32)
        sub = sb("sub", [RP, RC])
        obj = sb("obj", [RP, RC])
        key = sb("key", [RP, RC])
        key_i = sb("key_i", [RP, RC], i32)
        apart = sb("apart", [RP, RC])
        on_edge = sb("on_edge", [RP, RC])
        valid = sb("valid", [RP, RC])
        scan = sb("scan", [RP, 2, RC])
        tot_row = sb("tot_row", [RP, RP])
        fold = sb("fold", [RP, 2, P])
        pos = sb("pos", [RP, RC])
        pos_i = sb("pos_i", [RP, RC], i32)
        eight_i = sb("eight_i", [RP, 8], i32)
        eight_f = sb("eight_f", [RP, 8])
        ps_agg = ps("ps_agg", [P, 4, F])
        ps_deg = ps("ps_deg", [P, F])

        adj_ld = [sem(f"adj_ld{i}") for i in range(R)]
        cast_done, marked, sums_done = sem("cast_done"), sem("marked"), sem("sums_done")
        sec_summed, agg_ready, agg_st = sem("sec_summed"), sem("agg_ready"), sem("agg_st")
        consts, fills, pairs_ld = sem("consts"), sem("fills"), sem("pairs_ld")
        pool_step, gate, dve_step, keys_ready, sp_gate = sem("pool_step"), sem("gate"), sem("dve_step"), sem("keys_ready"), sem("sp_gate")
        flag_ld, tot_st, tot_ld, list_st, row_ld = (sem("flag_ld"), sem("tot_st"), sem("tot_ld"),
                                                    sem("list_st"), sem("row_ld"))
        block = ctx.enter_context(nc.Block())
        adj_t = tiles_of(ins["adj_t"])

        @block.sync
        def _(sp):
            sp.dma_start(pairs[:, :, :], ins["pairs"].rearrange("(p c) two -> p c two", p=RP)).then_inc(pairs_ld, 16)
            sp.sem_inc(agg_st, 16)

            def load(s, c):
                sp.wait_ge(cast_done, s * PIECES + c + 1)
                sp.sem_inc(sp_gate, 1)
                sp.dma_start(adj_in[:, c % R, :, :],
                             adj_t[:, CH * c:CH * (c + 1), bass.ds(s * SEC, SEC)]).then_inc(adj_ld[c % R], 16)

            def store_sums(s):
                sp.wait_ge(agg_ready, s + 2)
                sp.sem_inc(sp_gate, 1)
                sp.dma_start(tiles_of(k.agg_d)[:, bass.ds(s * 4, 4), :], agg[:, :, :]).then_inc(agg_st, 16)

            for c in range(R):
                load(0, c)
            sp.wait_ge(consts, 1)
            for i in range(N * F // P // 1024):
                sp.dma_start(k.rel_d.rearrange("(p t) f -> p (t f)", p=P)[:, 1024 * i:1024 * (i + 1)],
                             zeros[:, :]).then_inc(fills, 16)
            sp.dma_start(k.stats_d.rearrange("(p t) c -> p (t c)", p=P),
                         rows0[:, :, :].rearrange("p t c -> p (t c)")).then_inc(fills, 16)
            sp.dma_start(k.list_d.rearrange("(p c) o -> p (c o)", p=P), blank[:, :]).then_inc(fills, 16)
            with sp.Fori(0, SECS - 1) as s:
                for c in range(R):
                    load(s, c + R)
                for c in range(R):
                    load(s + 1, c)
                store_sums(s)
            s = SECS - 1
            for c in range(R):
                load(s, c + R)
            store_sums(s)
            sp.wait_ge(agg_st, 16 * (SECS + 1))

        @block.scalar
        def _(act):
            act.sem_inc(cast_done, R)
            with act.Fori(0, SECS) as s:
                for c in range(PIECES):
                    act.wait_ge(adj_ld[c % R], 16 * (2 * s + c // R + 1))
                    act.wait_ge(sums_done, s * PIECES + c + 1)
                    act.wait_ge(marked, s * PIECES + c + 1)
                    nc.scalar.activation(adj16[:, c % R, :, :], adj_in[:, c % R, :, :],
                                         ACT.Copy).then_inc(cast_done, 1)

        @block.tensor
        def _(pe):
            pe.sem_inc(sums_done, R)
            pe.wait_ge(consts, 1)
            with pe.Fori(0, SECS) as s:
                pe.wait_ge(agg_ready, s + 1)
                for c in range(PIECES):
                    pe.wait_ge(cast_done, s * PIECES + c + 1 + R)
                    for q in range(CH):
                        j = CH * c + q
                        for i in range(4):
                            block_t = adj16[:, c % R, q, P * i:P * (i + 1)]
                            nc.tensor.matmul(ps_agg[:, i, :], block_t, xs[:, j, 0:F], start=(j == 0), stop=False)
                            nc.tensor.matmul(ps_agg[:, i, :], block_t, xs[:, j, F:2 * F], start=False,
                                             stop=(j == NT - 1))
                            last = nc.tensor.matmul(ps_deg[:, i:i + 1], block_t, one16[:, :],
                                                    start=(j == 0 and i == 0), stop=(j == NT - 1),
                                                    skip_group_check=True)
                    last.then_inc(sums_done, 1)

        @block.vector
        def _(dve):
            dve.sem_inc(marked, R)
            dve.sem_inc(agg_ready, 1)
            nc.vector.memset(one16[:, :], 1.0)
            nc.vector.memset(zeros[:, :], 0.0)
            nc.vector.memset(blank[:, :], -1.0)
            nc.vector.memset(rows0[:, :, 0:H], DIAG)
            nc.vector.memset(rows0[:, :, H:SR], 0.0).then_inc(consts, 1)
            step = Chain(dve, dve_step)
            dve.wait_ge(pairs_ld, 16)
            nc.vector.tensor_copy(sub[:, :], pairs[:, :, 0])
            step.then(nc.vector.tensor_copy(obj[:, :], pairs[:, :, 1]))
            nc.vector.tensor_tensor(apart[:, :], sub[:, :], obj[:, :], ALU.not_equal)
            step.then(nc.vector.scalar_tensor_tensor(key[:, :], obj[:, :], float(N), sub[:, :], ALU.mult, ALU.add))
            nc.vector.tensor_copy(key_i[:, :], key[:, :]).then_inc(keys_ready, 1)
            with dve.Fori(0, SECS) as s:
                for c in range(PIECES):
                    dve.wait_ge(cast_done, s * PIECES + c + 1 + R)
                    nc.vector.tensor_reduce(
                        k.marks[:, bass.ds(2 * s, 2), CH * c:CH * (c + 1)].rearrange("p h q -> p q h"),
                        adj16[:, c % R, :, :].rearrange("p q (h i) -> p q h i", i=DS), AX, ALU.max).then_inc(marked, 1)
                dve.wait_ge(sums_done, (s + 1) * PIECES + R)
                dve.wait_ge(agg_st, 16 * (s + 1))
                nc.vector.tensor_copy(k.deg[:, bass.ds(4 * s, 4)], ps_deg[:, 0:4])
                nc.vector.tensor_scalar(agg[:, :, :], ps_agg[:, :, :], k.scale[:, 1:2], None,
                                        ALU.mult).then_inc(agg_ready, 1)

        @block.gpsimd
        def _(gp):
            step = Chain(gp, pool_step)
            gp.wait_ge(keys_ready, 1)
            adj_flat = ins["adj_t"].rearrange("j (i o) -> (j i) o", o=1)
            gathered = step.n
            step.base = 0
            with gp.Fori(0, RC // 8) as g:
                nc.gpsimd.tensor_copy(eight_i[:, :], key_i[:, bass.ds(8 * g, 8)]).then_inc(pool_step, 1)
                gp.wait_ge(pool_step, gathered + 2 * g + 1)
                gp.sem_inc(gate, 1)
                for e in range(8):
                    gp.indirect_dma_start(eight_f[:, e:e + 1], None, adj_flat,
                                          bass.IndirectOffsetOnAxis(ap=eight_i[:, e:e + 1], axis=0),
                                          bounds_check=N * N - 1, oob_is_err=False).then_inc(flag_ld, 16)
                gp.wait_ge(flag_ld, 128 * (g + 1))
                gp.sem_inc(gate, 1)
                nc.gpsimd.tensor_copy(on_edge[:, bass.ds(8 * g, 8)], eight_f[:, :]).then_inc(pool_step, 1)
                gp.wait_ge(pool_step, gathered + 2 * g + 2)
                gp.sem_inc(gate, 1)
            step.n = gathered + 2 * (RC // 8)
            step.then(nc.gpsimd.tensor_tensor(valid[:, :], on_edge[:, :], apart[:, :], ALU.mult))
            step.then(nc.gpsimd.tensor_copy(scan[:, 0, :], valid[:, :]))
            src, dist = 0, 1
            while dist < RC:
                nc.gpsimd.tensor_copy(scan[:, 1 - src, 0:dist], scan[:, src, 0:dist])
                step.then(nc.gpsimd.tensor_tensor(scan[:, 1 - src, dist:RC], scan[:, src, dist:RC],
                                                  scan[:, src, 0:RC - dist], ALU.add))
                src, dist = 1 - src, 2 * dist
            gp.dma_start(k.tot_d[0:1, 0:RP].rearrange("o p -> p o"), scan[:, src, RC - 1:RC]).then_inc(tot_st, 16)
            gp.wait_ge(tot_st, 16)
            gp.dma_start(tot_row[:, :], k.tot_d[0:1, 0:RP].broadcast_to([RP, RP])).then_inc(tot_ld, 16)
            gp.wait_ge(tot_ld, 16)
            step.then(nc.gpsimd.memset(fold[:, :, :], 0.0))
            nc.gpsimd.tensor_tensor(fold[:, 0, 0:RP], tot_row[:, :], k.before[0:RP, 0:RP], ALU.mult)
            step.then(nc.gpsimd.tensor_copy(fold[:, 1, 0:RP], tot_row[:, :]))
            half = P // 2
            while half:
                step.then(nc.gpsimd.tensor_tensor(fold[:, :, 0:half], fold[:, :, 0:half],
                                                  fold[:, :, half:2 * half], ALU.add))
                half //= 2
            nc.gpsimd.tensor_copy(k.nlist[0:RP, :], fold[:, 1, 0:1])
            step.then(nc.gpsimd.tensor_scalar(pos[:, :], scan[:, src, :], fold[:, 0, 0:1], -1.0 - OFF, ALU.add, ALU.add))
            step.then(nc.gpsimd.tensor_tensor(pos[:, :], pos[:, :], valid[:, :], ALU.mult))
            step.then(nc.gpsimd.tensor_scalar(pos_i[:, :], pos[:, :], OFF, None, ALU.add))
            gp.wait_ge(fills, 16 * (N * F // P // 1024 + 2))
            placed = step.n
            with gp.Fori(0, RC // 8) as g:
                nc.gpsimd.tensor_copy(eight_i[:, :], pos_i[:, bass.ds(8 * g, 8)])
                nc.gpsimd.tensor_copy(eight_f[:, :], key[:, bass.ds(8 * g, 8)]).then_inc(pool_step, 1)
                gp.wait_ge(pool_step, placed + g + 1)
                gp.sem_inc(gate, 1)
                for e in range(8):
                    gp.indirect_dma_start(k.list_d, bass.IndirectOffsetOnAxis(ap=eight_i[:, e:e + 1], axis=0),
                                          eight_f[:, e:e + 1], None,
                                          bounds_check=LIST - 1, oob_is_err=False).then_inc(list_st, 16)
                gp.wait_ge(list_st, 128 * (g + 1))
                gp.sem_inc(gate, 1)
            gp.dma_start(key_row[:, :], k.list_d.rearrange("n o -> o n").broadcast_to([P, LIST])).then_inc(row_ld, 16)
            gp.wait_ge(row_ld, 16)


def listed_tiles(eng, n, tile):
    tile(0)
    with eng.If(n > P):
        with eng.Fori(1, RT) as t:
            with eng.If(n > t * P):
                tile(t)


def decode_tile(nc, dve, step, key_col, got):
    nc.vector.tensor_scalar(got.valid[:, :], key_col[:, :], 0.0, None, ALU.is_ge)
    step.then(nc.vector.tensor_scalar(got.key_i[:, :], key_col[:, :], 0.0, None, ALU.max))
    nc.vector.tensor_single_scalar(got.sub_i[:, :], got.key_i[:, :], N - 1, ALU.bitwise_and)
    step.then(nc.vector.tensor_single_scalar(got.obj_i[:, :], got.key_i[:, :], N.bit_length() - 1,
                                             ALU.arith_shift_right))
    step.then(nc.vector.tensor_copy(got.sub_f[:, :], got.sub_i[:, :]))
    step.then(nc.vector.scalar_tensor_tensor(got.seg[:, :], got.sub_f[:, :], 1.0, got.valid[:, :],
                                             ALU.add, ALU.mult))
    step.then(nc.vector.tensor_scalar(got.seg[:, :], got.seg[:, :], -1.0, None, ALU.add))


def same_segment(nc, dve, step, k, got, seg_row, same, first_i):
    step.then(nc.vector.tensor_scalar(same[:, :], seg_row, got.seg[:, 0:1], None, ALU.is_equal))
    step.then(nc.vector.tensor_tensor(got.earlier[:, :], same[:, :], k.before[:, :], ALU.mult))
    step.then(nc.vector.tensor_reduce(got.count[:, :], got.earlier[:, :], AX, ALU.add))
    step.then(nc.vector.scalar_tensor_tensor(got.count[:, :], got.count[:, :], 0.5, got.valid[:, :],
                                             ALU.is_lt, ALU.mult))
    step.then(nc.vector.scalar_tensor_tensor(got.index_f[:, :], got.sub_f[:, :], -OFF, got.count[:, :],
                                             ALU.add, ALU.mult))
    step.then(nc.vector.tensor_scalar(first_i[:, :], got.index_f[:, :], OFF, None, ALU.add))


def decoded(sb):
    got = Kept()
    got.valid, got.sub_f, got.seg = sb("valid", [P, 1]), sb("sub_f", [P, 1]), sb("seg", [P, 1])
    got.key_i, got.sub_i, got.obj_i = sb("key_i", [P, 1], i32), sb("sub_i", [P, 1], i32), sb("obj_i", [P, 1], i32)
    got.earlier, got.count, got.index_f = sb("earlier", [P, P]), sb("count", [P, 1]), sb("index_f", [P, 1])
    return got


def relation_scores(nc, k, ins, key_row, att_all, weight_all):
    with ExitStack() as ctx:
        sb, ps, sem = stage(nc, ctx, "score")
        got = decoded(sb)
        wq, wk = sb("wq", [P, KF, F]), sb("wk", [P, KF, F])
        bqk = sb("bqk", [1, 2, F])
        key_col = sb("key_col", [P, 1])
        hit = sb("hit", [P, LIST], mybir.dt.bfloat16)
        times, share = sb("times", [P, 1]), sb("share", [P, 1])
        diag, same = sb("diag", [P, P]), sb("same", [P, P])
        first_i = sb("first_i", [P, 1], i32)
        x_sub, x_obj = sb("x_sub", [P, F]), sb("x_obj", [P, F])
        xt_sub, xt_obj = sb("xt_sub", [P, F]), sb("xt_obj", [P, F])
        q_sb, qk = sb("q_sb", [P, F]), sb("qk", [P, F])
        att = sb("att", [P, H])
        att_diag = sb("att_diag", [P, H, P])
        away = sb("away", [P, P])
        seg_att = sb("seg_att", [P, H, P])
        old, new = sb("old", [P, SR]), sb("new", [P, SR])
        drop, ex = sb("drop", [P, 2, H]), sb("ex", [P, 2, H])
        terms = sb("terms", [P, H + 1])
        ps_seg, ps_xs, ps_xo = ps("ps_seg", [P, F]), ps("ps_xs", [P, F]), ps("ps_xo", [P, F])
        ps_q, ps_k, ps_att = ps("ps_q", [P, F]), ps("ps_k", [P, F]), ps("ps_att", [P, 2, F])

        w_ld, key_ld, tile_done, gath_ld, new_st = (sem("w_ld"), sem("key_ld"), sem("tile_done"), sem("gath_ld"),
                                                    sem("new_st"))
        diag_ready, seg_ready, idx_ready, turned, turned_sb = (sem("diag_ready"), sem("seg_ready"), sem("idx_ready"),
                                                               sem("turned"), sem("turned_sb"))
        qk_ready, q_copied, attd_ready, att_spread = (sem("qk_ready"), sem("q_copied"), sem("attd_ready"),
                                                      sem("att_spread"))
        drop_ready, ex_ready, terms_ready, sums_ready, new_ready = (sem("drop_ready"), sem("ex_ready"),
                                                                    sem("terms_ready"), sem("sums_ready"),
                                                                    sem("new_ready"))
        dve_step, gate, blanks = sem("dve_step"), sem("gate"), sem("blanks")
        LINKS = 24
        block = ctx.enter_context(nc.Block())

        @block.sync
        def _(sp):
            sp.dma_start(wq[:, :, :], tiles_of(ins["wq_t"])).then_inc(w_ld, 16)
            sp.dma_start(wk[:, :, :], tiles_of(ins["wk_t"])).then_inc(w_ld, 16)
            sp.dma_start(bqk[:, 0, :], ins["bq"]).then_inc(w_ld, 16)
            sp.dma_start(bqk[:, 1, :], ins["bk"]).then_inc(w_ld, 16)
            sp.wait_ge(w_ld, 64)
            n = sp.value_load(k.nlist[0:1, 0:1], min_val=0, max_val=RP * RC)
            def tile(t):
                sp.wait_ge(tile_done, t + 1)
                sp.sem_inc(gate, 1)
                sp.dma_start(key_col[:, :], k.list_d[bass.ds(t * P, P), :]).then_inc(key_ld, 16)

            listed_tiles(sp, n, tile)

        @block.vector
        def _(dve):
            nc.vector.memset(new[:, :], 0.0).then_inc(blanks, 1)
            dve.wait_ge(blanks, 1)
            n = dve.value_load(k.nlist[0:1, 0:1], min_val=0, max_val=RP * RC)
            def tile(t):
                step = Chain(dve, dve_step, t * LINKS)
                dve.wait_ge(key_ld, 16 * (t + 1))
                decode_tile(nc, dve, step, key_col, got)
                nc.vector.tensor_scalar(diag[:, :], k.ident[:, :], got.seg[:, 0:1], None,
                                        ALU.mult).then_inc(diag_ready, 1)
                step.then(nc.vector.tensor_scalar(hit[:, :], key_row[:, :], key_col[:, 0:1], 0.0,
                                                  ALU.is_equal, ALU.add, accum_out=times[:, :]))
                step.then(nc.vector.tensor_scalar(times[:, :], times[:, :], 1.0, None, ALU.max))
                step.then(nc.vector.reciprocal(share[:, :], times[:, :]))
                step.then(nc.vector.tensor_tensor(terms[:, H:H + 1], share[:, :], got.valid[:, :], ALU.mult))
                nc.vector.tensor_copy(weight_all[:, bass.ds(t, 1)], terms[:, H:H + 1])
                dve.wait_ge(seg_ready, t + 1)
                same_segment(nc, dve, step, k, got, ps_seg[:, 0:P], same, first_i)
                step.then(nc.vector.tensor_scalar(away[:, :], same[:, :], BIG, -BIG, ALU.mult, ALU.add))
                dve.wait_ge(q_copied, t + 1)
                step.then(nc.vector.tensor_tensor(qk[:, :], q_sb[:, :], ps_k[:, :], ALU.mult))
                step.then(nc.vector.tensor_reduce(att[:, :], qk[:, :].rearrange("p (h d) -> p h d", d=DH),
                                                  AX, ALU.add))
                step.then(nc.vector.tensor_scalar(att[:, :], att[:, :], DH ** -0.5, None, ALU.mult))
                nc.vector.tensor_scalar(att_all[:, bass.ds(t * H, H)], att[:, :], got.valid[:, 0:1], None,
                                        ALU.mult)
                nc.vector.tensor_tensor(att_diag[:, :, :], k.ident[:, :].unsqueeze(1).broadcast_to([P, H, P]),
                                        att[:, :].unsqueeze(2).broadcast_to([P, H, P]),
                                        ALU.mult).then_inc(attd_ready, 1)
                dve.wait_ge(att_spread, t + 1)
                step.then(nc.vector.tensor_tensor(seg_att[:, :, :],
                                                  ps_att[:, :, :].rearrange("p b (h f) -> p (b h) f", f=P),
                                                  away[:, :].unsqueeze(1).broadcast_to([P, H, P]), ALU.add))
                step.then(nc.vector.tensor_reduce(drop[:, 0, :], seg_att[:, :, :], AX, ALU.max))
                step.then(nc.vector.tensor_tensor(new[:, 0:H], drop[:, 0, :], old[:, 0:H], ALU.max))
                nc.vector.tensor_tensor(drop[:, 0, :], old[:, 0:H], new[:, 0:H], ALU.subtract)
                nc.vector.tensor_tensor(drop[:, 1, :], att[:, :], new[:, 0:H], ALU.subtract).then_inc(drop_ready, 1)
                dve.wait_ge(ex_ready, t + 1)
                nc.vector.tensor_scalar(terms[:, 0:H], ex[:, 1, :], terms[:, H:H + 1], None,
                                        ALU.mult).then_inc(terms_ready, 1)
                step.then(nc.vector.tensor_tensor(new[:, H:2 * H], old[:, H:2 * H], ex[:, 0, :], ALU.mult))
                dve.wait_ge(sums_ready, t + 1)
                nc.vector.tensor_tensor(new[:, H:2 * H], new[:, H:2 * H], ps_seg[:, P:P + H], ALU.add)
                last = nc.vector.tensor_tensor(new[:, 2 * H:2 * H + 1], old[:, 2 * H:2 * H + 1],
                                               ps_seg[:, P + H:P + H + 1], ALU.add)
                step.then(last)
                nc.vector.tensor_copy(got.count[:, :], got.valid[:, :]).then_inc(new_ready, 1)
                assert step.n == LINKS, step.n

            listed_tiles(dve, n, tile)

        @block.tensor
        def _(pe):
            pe.wait_ge(w_ld, 64)
            n = pe.value_load(k.nlist[0:1, 0:1], min_val=0, max_val=RP * RC)
            def tile(t):
                pe.wait_ge(diag_ready, t + 1)
                nc.tensor.matmul(ps_seg[:, 0:P], k.ones[:, :], diag[:, :], start=True,
                                 stop=True).then_inc(seg_ready, 1)
                pe.wait_ge(gath_ld, 48 * (t + 1))
                for x_rows, turned_ps in ((x_sub, ps_xs), (x_obj, ps_xo)):
                    for f in range(KF):
                        last = nc.tensor.transpose(turned_ps[:, P * f:P * (f + 1)], x_rows[:, P * f:P * (f + 1)],
                                                   k.ident[:, :])
                last.then_inc(turned, 1)
                pe.wait_ge(turned_sb, 2 * (t + 1))
                for xt, wt, out, b in ((xt_sub, wq, ps_q, 0), (xt_obj, wk, ps_k, 1)):
                    for f in range(KF):
                        nc.tensor.matmul(out[:, :], xt[:, P * f:P * (f + 1)], wt[:, f, :], start=(f == 0),
                                         stop=False)
                    last = nc.tensor.matmul(out[:, :], k.ones[0:1, :], bqk[0:1, b, :], start=False, stop=True)
                last.then_inc(qk_ready, 1)
                pe.wait_ge(attd_ready, t + 1)
                for b in range(2):
                    last = nc.tensor.matmul(ps_att[:, b, :], k.ones[:, :],
                                            att_diag[:, 4 * b:4 * (b + 1), :].rearrange("p h f -> p (h f)"),
                                            start=True, stop=True)
                last.then_inc(att_spread, 1)
                pe.wait_ge(terms_ready, t + 1)
                nc.tensor.matmul(ps_seg[:, P:P + H + 1], same[:, :], terms[:, :], start=True,
                                 stop=True).then_inc(sums_ready, 1)

            listed_tiles(pe, n, tile)

        @block.scalar
        def _(act):
            act.wait_ge(blanks, 1)
            n = act.value_load(k.nlist[0:1, 0:1], min_val=0, max_val=RP * RC)
            def tile(t):
                act.wait_ge(turned, t + 1)
                nc.scalar.copy(xt_sub[:, :], ps_xs[:, :]).then_inc(turned_sb, 1)
                nc.scalar.copy(xt_obj[:, :], ps_xo[:, :]).then_inc(turned_sb, 1)
                act.wait_ge(qk_ready, t + 1)
                nc.scalar.copy(q_sb[:, :], ps_q[:, :]).then_inc(q_copied, 1)
                act.wait_ge(drop_ready, t + 1)
                nc.scalar.activation(ex[:, :, :], drop[:, :, :], ACT.Exp).then_inc(ex_ready, 1)

            listed_tiles(act, n, tile)

        @block.gpsimd
        def _(gp):
            gp.sem_inc(tile_done, 1)
            n = gp.value_load(k.nlist[0:1, 0:1], min_val=0, max_val=RP * RC)
            def tile(t):
                gp.wait_ge(seg_ready, t + 1)
                gp.sem_inc(gate, 1)
                for rows, table, bound, index in ((x_sub, ins["x"], N - 1, got.sub_i),
                                                  (x_obj, ins["x"], N - 1, got.obj_i),
                                                  (old, k.stats_d, N - 1, got.sub_i)):
                    gp.indirect_dma_start(rows[:, :], None, table, bass.IndirectOffsetOnAxis(ap=index[:, 0:1], axis=0),
                                          bounds_check=bound, oob_is_err=False).then_inc(gath_ld, 16)
                gp.wait_ge(new_ready, t + 1)
                gp.sem_inc(gate, 1)
                gp.indirect_dma_start(k.stats_d, bass.IndirectOffsetOnAxis(ap=first_i[:, 0:1], axis=0), new[:, :],
                                      None, bounds_check=N - 1, oob_is_err=False).then_inc(new_st, 16)
                gp.wait_ge(new_st, 16 * (t + 1))
                gp.sem_inc(tile_done, 1)

            listed_tiles(gp, n, tile)


def node_coefficients(nc, k, ins, c_all, cx_all):
    with ExitStack() as ctx:
        sb, ps, sem = stage(nc, ctx, "coef")
        stats = sb("stats", [P, NT, SR])
        loop = sb("loop", [P, NT])
        ex0, exd = sb("ex0", [P, NT, H]), sb("exd", [P, NT, H])
        others = sb("others", [P, NT])
        z, prod, prod_d = sb("z", [P, NT, H]), sb("prod", [P, NT, H]), sb("prod_d", [P, NT, H])
        cd = sb("cd", [P, NT])
        rows = sb("rows", [P, NT, CR])
        diag_bias = sb("diag_bias", [P, 1])
        empty = sb("empty", [P, NT])
        st_ld, loop_ld, rows_st = sem("st_ld"), sem("loop_ld"), sem("rows_st")
        dve_step, ex_ready, bias_ready, rows_ready = sem("dve_step"), sem("ex_ready"), sem("bias_ready"), sem("rows_ready")
        block = ctx.enter_context(nc.Block())

        @block.sync
        def _(sp):
            sp.dma_start(stats[:, :, :], tiles_of(k.stats_d)).then_inc(st_ld, 16)
            sp.dma_start(loop[:, :], ins["adj_diag"]).then_inc(loop_ld, 16)
            sp.wait_ge(rows_ready, 1)
            sp.dma_start(tiles_of(k.coef_d), rows[:, :, :]).then_inc(rows_st, 16)
            sp.dma_start(k.empty_d.rearrange("(t p) o -> p (t o)", p=P), empty[:, :],
                         allow_slow_non_contiguous=True).then_inc(rows_st, 16)
            sp.wait_ge(rows_st, 32)

        @block.scalar
        def _(act):
            act.wait_ge(st_ld, 16)
            act.wait_ge(bias_ready, 1)
            nc.scalar.activation(ex0[:, :, :], stats[:, :, 0:H], ACT.Exp, scale=-1.0)
            nc.scalar.activation(exd[:, :, :], stats[:, :, 0:H], ACT.Exp, scale=-1.0,
                                 bias=diag_bias[:, 0:1]).then_inc(ex_ready, 1)

        @block.vector
        def _(dve):
            step = Chain(dve, dve_step)
            nc.vector.memset(diag_bias[:, :], DIAG).then_inc(bias_ready, 1)
            nc.vector.tensor_scalar(empty[:, :], k.deg[:, :], 0.0, None, ALU.is_equal)
            dve.wait_ge(loop_ld, 16)
            step.then(nc.vector.tensor_tensor(others[:, :], k.deg[:, :], loop[:, :], ALU.subtract))
            dve.wait_ge(st_ld, 16)
            step.then(nc.vector.tensor_tensor(others[:, :], others[:, :], stats[:, :, 2 * H], ALU.subtract))
            dve.wait_ge(ex_ready, 1)
            step.then(nc.vector.tensor_tensor(z[:, :, :], ex0[:, :, :],
                                              others[:, :].unsqueeze(2).broadcast_to([P, NT, H]), ALU.mult))
            step.then(nc.vector.tensor_tensor(z[:, :, :], z[:, :, :], exd[:, :, :], ALU.add))
            step.then(nc.vector.tensor_tensor(z[:, :, :], z[:, :, :], stats[:, :, H:2 * H], ALU.add))
            step.then(nc.vector.tensor_scalar(z[:, :, :], z[:, :, :], float(H), None, ALU.mult))
            step.then(nc.vector.reciprocal(rows[:, :, H:2 * H], z[:, :, :]))
            nc.vector.tensor_copy(rows[:, :, 0:H], stats[:, :, 0:H]).then_inc(rows_ready, 1)
            nc.vector.tensor_tensor(prod[:, :, :], ex0[:, :, :], rows[:, :, H:2 * H], ALU.mult)
            step.then(nc.vector.tensor_tensor(prod_d[:, :, :], exd[:, :, :], rows[:, :, H:2 * H], ALU.mult))
            nc.vector.tensor_reduce(c_all[:, :], prod[:, :, :], AX, ALU.add)
            step.then(nc.vector.tensor_reduce(cd[:, :], prod_d[:, :, :], AX, ALU.add))
            step.then(nc.vector.tensor_tensor(cx_all[:, :], c_all[:, :], loop[:, :], ALU.mult))
            step.then(nc.vector.tensor_tensor(cx_all[:, :], cd[:, :], cx_all[:, :], ALU.subtract))
            step.then(nc.vector.tensor_scalar(cx_all[:, :], cx_all[:, :], 1.0, None, ALU.add))


def relation_values(nc, k, ins, att_all, weight_all):
    with ExitStack() as ctx:
        sb, ps, sem = stage(nc, ctx, "value")
        got = decoded(sb)
        key_col = sb("key_col", [P, 1])
        diag, same = sb("diag", [P, P]), sb("same", [P, P])
        first_i = sb("first_i", [P, 1], i32)
        x_obj, rel_old, rel_new = sb("x_obj", [P, F]), sb("rel_old", [P, F]), sb("rel_new", [P, F])
        coef = sb("coef", [P, CR])
        drop, ex = sb("drop", [P, 2, H]), sb("ex", [P, 2, H])
        rise, weight = sb("rise", [P, H]), sb("weight", [P, 1])
        value = sb("value", [P, F])
        ps_seg = ps("ps_seg", [P, F])
        ps_val = ps("ps_val", [P, F])
        key_ld, tile_done, gath_ld, new_st = sem("key_ld"), sem("tile_done"), sem("gath_ld"), sem("new_st")
        diag_ready, seg_ready, drop_ready, ex_ready = (sem("diag_ready"), sem("seg_ready"), sem("drop_ready"),
                                                       sem("ex_ready"))
        value_ready, val_summed, new_ready = sem("value_ready"), sem("val_summed"), sem("new_ready")
        dve_step, gate = sem("dve_step"), sem("gate")
        LINKS = 16
        block = ctx.enter_context(nc.Block())

        @block.sync
        def _(sp):
            n = sp.value_load(k.nlist[0:1, 0:1], min_val=0, max_val=RP * RC)
            def tile(t):
                sp.wait_ge(tile_done, t + 1)
                sp.sem_inc(gate, 1)
                sp.dma_start(key_col[:, :], k.list_d[bass.ds(t * P, P), :]).then_inc(key_ld, 16)

            listed_tiles(sp, n, tile)

        @block.vector
        def _(dve):
            n = dve.value_load(k.nlist[0:1, 0:1], min_val=0, max_val=RP * RC)
            def tile(t):
                step = Chain(dve, dve_step, t * LINKS)
                dve.wait_ge(key_ld, 16 * (t + 1))
                decode_tile(nc, dve, step, key_col, got)
                nc.vector.tensor_scalar(diag[:, :], k.ident[:, :], got.seg[:, 0:1], None,
                                        ALU.mult).then_inc(diag_ready, 1)
                dve.wait_ge(gath_ld, 48 * (t + 1))
                nc.vector.tensor_tensor(drop[:, 0, :], att_all[:, bass.ds(t * H, H)], coef[:, 0:H], ALU.subtract)
                nc.vector.tensor_scalar(drop[:, 1, :], coef[:, 0:H], -1.0, None,
                                        ALU.mult).then_inc(drop_ready, 1)
                dve.wait_ge(seg_ready, t + 1)
                same_segment(nc, dve, step, k, got, ps_seg[:, 0:P], same, first_i)
                dve.wait_ge(ex_ready, t + 1)
                step.then(nc.vector.tensor_tensor(rise[:, :], ex[:, 0, :], ex[:, 1, :], ALU.subtract))
                step.then(nc.vector.tensor_tensor(rise[:, :], rise[:, :], coef[:, H:2 * H], ALU.mult))
                step.then(nc.vector.tensor_reduce(weight[:, :], rise[:, :], AX, ALU.add))
                step.then(nc.vector.tensor_tensor(weight[:, :], weight[:, :], weight_all[:, bass.ds(t, 1)],
                                                  ALU.mult))
                nc.vector.tensor_scalar(value[:, :], x_obj[:, :], weight[:, 0:1], None,
                                        ALU.mult).then_inc(value_ready, 1)
                dve.wait_ge(val_summed, t + 1)
                step.then(nc.vector.tensor_tensor(rel_new[:, :], rel_old[:, :], ps_val[:, :], ALU.add))
                nc.vector.tensor_copy(got.count[:, :], got.valid[:, :]).then_inc(new_ready, 1)
                assert step.n == LINKS, step.n

            listed_tiles(dve, n, tile)

        @block.tensor
        def _(pe):
            n = pe.value_load(k.nlist[0:1, 0:1], min_val=0, max_val=RP * RC)
            def tile(t):
                pe.wait_ge(diag_ready, t + 1)
                nc.tensor.matmul(ps_seg[:, 0:P], k.ones[:, :], diag[:, :], start=True,
                                 stop=True).then_inc(seg_ready, 1)
                pe.wait_ge(value_ready, t + 1)
                nc.tensor.matmul(ps_val[:, :], same[:, :], value[:, :], start=True,
                                 stop=True).then_inc(val_summed, 1)

            listed_tiles(pe, n, tile)

        @block.scalar
        def _(act):
            n = act.value_load(k.nlist[0:1, 0:1], min_val=0, max_val=RP * RC)
            def tile(t):
                act.wait_ge(drop_ready, t + 1)
                nc.scalar.activation(ex[:, :, :], drop[:, :, :], ACT.Exp).then_inc(ex_ready, 1)

            listed_tiles(act, n, tile)

        @block.gpsimd
        def _(gp):
            gp.sem_inc(tile_done, 1)
            n = gp.value_load(k.nlist[0:1, 0:1], min_val=0, max_val=RP * RC)
            def tile(t):
                gp.wait_ge(diag_ready, t + 1)
                gp.sem_inc(gate, 1)
                for rows, table, index in ((coef, k.coef_d, got.sub_i), (x_obj, ins["x"], got.obj_i),
                                           (rel_old, k.rel_d, got.sub_i)):
                    gp.indirect_dma_start(rows[:, :], None, table, bass.IndirectOffsetOnAxis(ap=index[:, 0:1], axis=0),
                                          bounds_check=N - 1, oob_is_err=False).then_inc(gath_ld, 16)
                gp.wait_ge(new_ready, t + 1)
                gp.sem_inc(gate, 1)
                gp.indirect_dma_start(k.rel_d, bass.IndirectOffsetOnAxis(ap=first_i[:, 0:1], axis=0), rel_new[:, :],
                                      None, bounds_check=N - 1, oob_is_err=False).then_inc(new_st, 16)
                gp.wait_ge(new_st, 16 * (t + 1))
                gp.sem_inc(tile_done, 1)

            listed_tiles(gp, n, tile)


def source_index(nc, k, ins, ls):
    with ExitStack() as ctx:
        sb, ps, sem = stage(nc, ctx, "index")
        upto = sb("upto", [P, P], f16)
        cum = sb("cum", [NT, NS, P])
        cnt, cnt16 = sb("cnt", [NT, NS]), sb("cnt16", [NT, NS], f16)
        excl = sb("excl", [NT, NS])
        one16 = sb("one16", [NT, P], f16)
        slot_i, row_i, sec_i = sb("slot_i", [P, NT], i32), sb("row_i", [NT, N], i32), sb("sec_i", [P, NS], i32)
        total = sb("total", [P, NS])
        span = sb("span", [P, 2, NS])
        groups_i = sb("groups_i", [P, NS], i32)
        groups_f = sb("groups_f", [P, NS])
        ps_cum, ps_cnt = ps("ps_cum", [P, NS * P]), ps("ps_cnt", [P, 2, F])
        up_ready, cum_ps, cnt_ready, cnt_ps, sum_ready, diff_ps = (
            sem("up_ready"), sem("cum_ps"), sem("cnt_ready"), sem("cnt_ps"), sem("sum_ready"), sem("diff_ps"))
        iotas, dve_step, const_ld = sem("iotas"), sem("dve_step"), sem("const_ld")
        block = ctx.enter_context(nc.Block())

        @block.gpsimd
        def _(gp):
            nc.gpsimd.iota(slot_i[:, :], [[P, NT]], base=0, channel_multiplier=1)
            nc.gpsimd.iota(row_i[:, :], [[1, N]], base=0, channel_multiplier=0)
            nc.gpsimd.iota(sec_i[:, :], [[1, NS]], base=0, channel_multiplier=0).then_inc(iotas, 1)

        @block.sync
        def _(sp):
            sp.dma_start(ls.differ[:, :], ins["differ"]).then_inc(const_ld, 16)
            sp.wait_ge(const_ld, 16)

        @block.tensor
        def _(pe):
            pe.wait_ge(up_ready, 1)
            for s in range(NS):
                last = nc.tensor.matmul(ps_cum[0:NT, P * s:P * (s + 1)], k.marks[:, s, :], upto[:, :],
                                        start=True, stop=True)
            last.then_inc(cum_ps, 1)
            pe.wait_ge(cnt_ready, 1)
            nc.tensor.matmul(ps_cnt[0:NT, 0, 0:NS], upto[0:NT, 0:NT], cnt16[:, :], start=True, stop=True)
            nc.tensor.matmul(ps_cnt[:, 1, 0:NS], one16[:, :], cnt16[:, :], start=True, stop=True).then_inc(cnt_ps, 1)
            pe.wait_ge(sum_ready, 1)
            pe.wait_ge(const_ld, 16)
            for a in range(4):
                last = nc.tensor.matmul(ps_cum[0:NT, F * a:F * (a + 1)], ls.differ[:, 0:NT],
                                        cum[:, 4 * a:4 * (a + 1), :].rearrange("t s p -> t (s p)"),
                                        start=True, stop=True)
            last.then_inc(diff_ps, 1)

        @block.vector
        def _(dve):
            step = Chain(dve, dve_step)
            nc.vector.memset(one16[:, :], 1.0)
            nc.vector.memset(ls.node[:, :, :], float(N))
            nc.vector.tensor_scalar(upto[:, :], k.before[:, :], -1.0, 1.0, ALU.mult, ALU.add).then_inc(up_ready, 1)
            dve.wait_ge(iotas, 1)
            nc.vector.tensor_copy(ls.slot[:, :], slot_i[:, :])
            nc.vector.tensor_copy(ls.slot_row[:, :], row_i[:, :])
            nc.vector.tensor_copy(ls.sec_no[:, :], sec_i[:, :])
            dve.wait_ge(cum_ps, 1)
            sums = ps_cum[0:NT, :].rearrange("t (s p) -> t s p", p=P)
            nc.vector.tensor_copy(cnt16[:, :], sums[:, :, P - 1]).then_inc(cnt_ready, 1)
            step.then(nc.vector.tensor_copy(cnt[:, :], sums[:, :, P - 1]))
            dve.wait_ge(cnt_ps, 1)
            step.then(nc.vector.tensor_tensor(excl[:, :], ps_cnt[0:NT, 0, 0:NS], cnt[:, :], ALU.subtract))
            nc.vector.tensor_scalar(ls.lead[:, :], excl[:, :], -1.0, 1.0, ALU.mult, ALU.add)
            nc.vector.tensor_tensor(cum[:, :, :], sums, excl[:, :].unsqueeze(2).broadcast_to([NT, NS, P]),
                                    ALU.add).then_inc(sum_ready, 1)
            step.then(nc.vector.tensor_scalar(groups_i[:, :], ps_cnt[:, 1, 0:NS], float(GT * P - 1), None, ALU.add))
            step.then(nc.vector.tensor_single_scalar(groups_i[:, :], groups_i[:, :], (GT * P).bit_length() - 1,
                                                     ALU.arith_shift_right))
            step.then(nc.vector.tensor_scalar(groups_f[:, :], groups_i[:, :], float(MG), None, ALU.max))
            nc.vector.tensor_copy(k.groups[:, :], groups_f[:, :])
            step.then(nc.vector.tensor_copy(span[:, 0, :], groups_f[:, :]))
            src, dist = 0, 1
            while dist < NS:
                nc.vector.tensor_copy(span[:, 1 - src, 0:dist], span[:, src, 0:dist])
                step.then(nc.vector.tensor_tensor(span[:, 1 - src, dist:NS], span[:, src, dist:NS],
                                                  span[:, src, 0:NS - dist], ALU.add))
                src, dist = 1 - src, 2 * dist
            nc.vector.tensor_tensor(k.first[:, :], span[:, src, :], groups_f[:, :], ALU.subtract)
            dve.wait_ge(diff_ps, 1)
            nc.vector.tensor_copy(ls.steps[:, :, :], sums)


def section_groups(eng, k, s, group):
    n = eng.value_load(k.groups[0:1, bass.ds(s, 1)], min_val=MG, max_val=NT // GT)
    first = eng.value_load(k.first[0:1, bass.ds(s, 1)], min_val=0, max_val=(NS - 1) * NT // GT)
    for q in range(MG):
        group(q, first + q)
    with eng.If(n > MG):
        with eng.Fori(MG, NT // GT) as q:
            with eng.If(n > q):
                group(q, first + q)


def source_lists(nc, k, ls):
    with ExitStack() as ctx:
        sb, ps, sem = stage(nc, ctx, "list")
        W = GT * P // 2
        begun = sb("begun", [NT, 2, W])
        hit = sb("hit", [P, 2, P])
        found = sb("found", [P, 2, GT // 2])
        ps_row = [ps(f"ps_row{b}", [P, GT // 2, P]) for b in range(2)]
        ps_tile = [ps(f"ps_tile{b}", [P, F]) for b in range(2)]
        begun_ready, chosen, counted = sem("begun_ready"), sem("chosen"), sem("counted")
        passed, dve_step, gate = sem("passed"), sem("dve_step"), sem("gate")
        block = ctx.enter_context(nc.Block())

        @block.sync
        def _(sp):
            sp.wait_ge(k.rows_st, 16 * PIECES)

        @block.scalar
        def _(act):
            with act.Fori(0, NS) as s:
                def begin(q, g):
                    for b in range(2):
                        act.wait_ge(chosen, 2 * g + b + 1)
                        act.sem_inc(gate, 1)
                        nc.scalar.activation(begun[:, b, :], ls.slot_row[:, bass.ds(q * GT * P + b * W, W)],
                                             ACT.Relu, bias=ls.lead[:, bass.ds(s, 1)]).then_inc(passed, 1)

                section_groups(act, k, s, begin)

        @block.gpsimd
        def _(gp):
            with gp.Fori(0, NS) as s:
                def clip(q, g):
                    for b in range(2):
                        gp.wait_ge(passed, 2 * g + b + 1)
                        gp.sem_inc(gate, 1)
                        nc.gpsimd.tensor_scalar(begun[:, b, :], begun[:, b, :], 1.0, None,
                                                ALU.min).then_inc(begun_ready, 1)

                section_groups(gp, k, s, clip)

        @block.tensor
        def _(pe):
            pe.sem_inc(chosen, 2)
            with pe.Fori(0, NS) as s:
                def choose(q, g):
                    for b in range(2):
                        pe.wait_ge(begun_ready, 2 * g + b + 1)
                        pe.wait_ge(counted, 2 * g + b + 1)
                        pe.sem_inc(gate, 1)
                        for i in range(GT // 2):
                            slots = begun[:, b, P * i:P * (i + 1)]
                            nc.tensor.matmul(ps_row[b][:, i, :], slots,
                                             ls.steps[:, bass.ds(s, 1), :].rearrange("t o p -> t (o p)"),
                                             start=True, stop=True)
                            last = nc.tensor.matmul(ps_tile[b][:, i:i + 1], slots, ls.differ[:, NT:NT + 1],
                                                    start=True, stop=True)
                        last.then_inc(chosen, 1)

                section_groups(pe, k, s, choose)

        @block.vector
        def _(dve):
            dve.sem_inc(counted, 2)
            with dve.Fori(0, NS) as s:
                def count(q, g):
                    for b in range(2):
                        dve.wait_ge(chosen, 2 * g + b + 3)
                        for i in range(GT // 2):
                            m = q * GT + b * (GT // 2) + i
                            last = nc.vector.tensor_scalar(hit[:, i, :], ps_row[b][:, i, :],
                                                           ls.slot[:, bass.ds(m, 1)], 0.0, ALU.is_le, ALU.add,
                                                           accum_out=found[:, b, i:i + 1])
                        last.then_inc(dve_step, 1)
                        dve.wait_ge(dve_step, 2 * g + b + 1)
                        nc.vector.tensor_tensor(
                            ls.node[:, bass.ds(s, 1), bass.ds(q * GT + b * (GT // 2), GT // 2)]
                            .rearrange("p o t -> p (o t)"), found[:, b, :], ps_tile[b][:, 0:GT // 2],
                            ALU.add).then_inc(counted, 1)

                section_groups(dve, k, s, count)


def list_rows(nc, k, ls):
    with ExitStack() as ctx:
        sb, ps, sem = stage(nc, ctx, "rows")
        dve_step = sem("dve_step")
        block = ctx.enter_context(nc.Block())

        @block.vector
        def _(dve):
            step = Chain(dve, dve_step)
            nc.vector.tensor_copy(k.index[:, :, :, 0], ls.node[:, :, :])
            step.then(nc.vector.scalar_tensor_tensor(ls.node[:, :, :], ls.node[:, :, :], float(NS),
                                                     ls.sec_no[:, :].unsqueeze(2).broadcast_to([P, NS, NT]),
                                                     ALU.mult, ALU.add))
            nc.vector.tensor_scalar(k.index[:, :, :, 1], ls.node[:, :, :], float(N * NS - 1), None, ALU.min)


class Lists:
    pass


def make_lists(sb):
    ls = Lists()
    ls.differ = sb("differ", [NT, NT + 1])
    ls.steps = sb("steps", [NT, NS, P])
    ls.lead = sb("lead", [NT, NS])
    ls.slot = sb("slot", [P, NT])
    ls.slot_row = sb("slot_row", [NT, N])
    ls.sec_no = sb("sec_no", [P, NS])
    ls.node = sb("node", [P, NS, NT])
    return ls


def project_nodes(nc, k, ins, c_all, cx_all, row_all, sd_all, s_row, x_sum):
    with ExitStack() as ctx:
        sb, ps, sem = stage(nc, ctx, "node")
        parts = sb("parts", [P, 2, 3, F])
        mixed = sb("mixed", [P, 2, F])
        x1 = sb("x1", [P, 2, F])
        x1_t = sb("x1_t", [P, 2, F])
        seen = sb("seen", [P, 2, 6])
        moments = sb("moments", [P, 2, 2])
        rstd, minus_half = sb("rstd", [P, 2]), sb("minus_half", [P, 1])
        ps_turn = [ps(f"ps_turn{b}", [P, F]) for b in range(2)]
        ps_wh = [ps(f"ps_wh{b}", [P, F]) for b in range(2)]
        ps_sd = [ps(f"ps_sd{b}", [P, F]) for b in range(2)]
        ps_srow = [ps(f"ps_srow{b}", [P, F]) for b in range(2)]
        part_ld = [sem(f"part_ld{b}") for b in range(2)]
        x1_st = [sem(f"x1_st{b}") for b in range(2)]
        parts_used, x1_ready, x1_summed = sem("parts_used"), sem("x1_ready"), sem("x1_summed")
        turned, turned_sb, projected, copied = sem("turned"), sem("turned_sb"), sem("projected"), sem("copied")
        dve_step, gate, pool_step = sem("dve_step"), sem("gate"), sem("pool_step")
        moments_ready, rstd_ready = sem("moments_ready"), sem("rstd_ready")
        LINKS = 3
        block = ctx.enter_context(nc.Block())

        @block.sync
        def _(sp):
            sp.sem_inc(x1_st[0], 16)
            sp.sem_inc(x1_st[1], 16)

            def load(t, b):
                sp.wait_ge(parts_used, t + 1)
                sp.sem_inc(gate, 1)
                for i, table in enumerate((k.agg_d, ins["x"], k.rel_d)):
                    sp.dma_start(parts[:, b, i, :], table[bass.ds(t * P, P), :]).then_inc(part_ld[b], 16)

            def store(t, b):
                sp.wait_ge(x1_ready, t + 1)
                sp.sem_inc(gate, 1)
                sp.dma_start(k.x1_d[bass.ds(t * P, P), :], x1[:, b, :]).then_inc(x1_st[b], 16)

            load(0, 0)
            load(1, 1)
            with sp.Fori(0, NT // 2 - 1) as pair:
                for b in range(2):
                    load(2 * pair + b + 2, b)
                    store(2 * pair + b, b)
            for b in range(2):
                store(NT - 2 + b, b)
            for b in range(2):
                sp.wait_ge(x1_st[b], 16 * (NT // 2 + 1))

        @block.vector
        def _(dve):
            dve.sem_inc(parts_used, 2)
            with dve.Fori(0, NT // 2) as pair:
                for b in range(2):
                    t = 2 * pair + b
                    step = Chain(dve, dve_step, t * LINKS)
                    dve.wait_ge(part_ld[b], 48 * (pair + 1))
                    step.then(nc.vector.scalar_tensor_tensor(mixed[:, b, :], parts[:, b, 0, :],
                                                             c_all[:, bass.ds(t, 1)], parts[:, b, 2, :],
                                                             ALU.mult, ALU.add))
                    step.then(nc.vector.scalar_tensor_tensor(mixed[:, b, :], parts[:, b, 1, :],
                                                             cx_all[:, bass.ds(t, 1)], mixed[:, b, :],
                                                             ALU.mult, ALU.add))
                    step.then(nc.vector.bn_stats(seen[:, b, :], mixed[:, b, :]))
                    dve.sem_inc(parts_used, 1)
                    nc.vector.bn_aggr(moments[:, b, :], seen[:, b, :]).then_inc(moments_ready, 1)
                    dve.wait_ge(rstd_ready, t + 1)
                    dve.wait_ge(x1_st[b], 16 * (pair + 1))
                    dve.wait_ge(turned, t + 1)
                    dve.wait_ge(x1_summed, t + 1)
                    nc.vector.tensor_scalar(x1[:, b, :], mixed[:, b, :], moments[:, b, 0:1], rstd[:, b:b + 1],
                                            ALU.subtract, ALU.mult).then_inc(x1_ready, 1)
                    assert step.n == LINKS

        @block.gpsimd
        def _(gp):
            gp.sem_inc(x1_summed, 2)
            nc.gpsimd.memset(minus_half[:, :], -0.5)
            nc.gpsimd.memset(x_sum[:, :], 0.0).then_inc(pool_step, 1)
            gp.wait_ge(pool_step, 1)
            with gp.Fori(0, NT // 2) as pair:
                for b in range(2):
                    t = 2 * pair + b
                    gp.wait_ge(moments_ready, t + 1)
                    gp.sem_inc(gate, 1)
                    nc.gpsimd.tensor_scalar(rstd[:, b:b + 1], moments[:, b, 1:2], EPS, None,
                                            ALU.add).then_inc(pool_step, 1)
                    gp.wait_ge(pool_step, t + 2)
                    nc.gpsimd.tensor_tensor(rstd[:, b:b + 1], rstd[:, b:b + 1], minus_half[:, :],
                                            ALU.pow).then_inc(rstd_ready, 1)
                    gp.wait_ge(x1_ready, t + 1)
                    gp.wait_ge(x1_summed, t + 2)
                    nc.gpsimd.tensor_tensor(x_sum[:, :], x_sum[:, :], x1[:, b, :], ALU.add).then_inc(x1_summed, 1)

        @block.tensor
        def _(pe):
            pe.sem_inc(turned, 2)

            def turn(t, b):
                pe.wait_ge(x1_ready, t + 1)
                for f in range(KF):
                    last = nc.tensor.transpose(ps_turn[b][:, P * f:P * (f + 1)], x1[:, b, P * f:P * (f + 1)],
                                               k.ident[:, :])
                last.then_inc(turned, 1)

            def project(t, b):
                pe.wait_ge(turned_sb, t + 1)
                pe.wait_ge(copied, t + 1)
                for f in range(KF):
                    xt = x1_t[:, b, P * f:P * (f + 1)]
                    nc.tensor.matmul(ps_wh[b][:, :], xt, k.w[:, f, :], start=(f == 0), stop=(f == KF - 1))
                    nc.tensor.matmul(ps_sd[b][:, 0:2 * H], xt, k.wa[:, f, :], start=(f == 0), stop=(f == KF - 1))
                    last = nc.tensor.matmul(ps_srow[b][0:H, 0:P], k.wa[:, f, 0:H], xt, start=(f == 0),
                                            stop=(f == KF - 1))
                last.then_inc(projected, 1)

            turn(0, 0)
            with pe.Fori(0, NT // 2 - 1) as pair:
                turn(2 * pair + 1, 1)
                project(2 * pair, 0)
                turn(2 * pair + 2, 0)
                project(2 * pair + 1, 1)
            turn(NT - 1, 1)
            project(NT - 2, 0)
            project(NT - 1, 1)

        @block.scalar
        def _(act):
            act.sem_inc(copied, 2)

            def keep_turned(t, b):
                act.wait_ge(turned, t + 3)
                nc.scalar.copy(x1_t[:, b, :], ps_turn[b][:, :]).then_inc(turned_sb, 1)

            def keep_projected(t, b):
                act.wait_ge(projected, t + 1)
                nc.scalar.copy(row_all[:, bass.ds(t, 1), 0:H * (DH + 1)].rearrange("p o (h d) -> p (o h) d", d=DH + 1)[:, :, 0:DH],
                               ps_wh[b][:, :].rearrange("p (h d) -> p h d", d=DH))
                nc.scalar.copy(sd_all[:, bass.ds(t, 1), :].rearrange("p o h -> p (o h)"), ps_sd[b][:, 0:2 * H])
                nc.scalar.copy(s_row[:, bass.ds(t * P, P)], ps_srow[b][0:H, 0:P]).then_inc(copied, 1)

            keep_turned(0, 0)
            with act.Fori(0, NT // 2 - 1) as pair:
                keep_turned(2 * pair + 1, 1)
                keep_projected(2 * pair, 0)
                keep_turned(2 * pair + 2, 0)
                keep_projected(2 * pair + 1, 1)
            keep_turned(NT - 1, 1)
            keep_projected(NT - 2, 0)
            keep_projected(NT - 1, 1)


def attention_factors(nc, k, row_all, sd_all, s_row, x_sum, wh_sum):
    with ExitStack() as ctx:
        sb, ps, sem = stage(nc, ctx, "fact")
        d_own, d_max, d_col = sb("d_own", [P, H]), sb("d_max", [P, H]), sb("d_col", [H, 1])
        d_off = sb("d_off", [P, NT, H])
        v_fac = sb("v_fac", [P, NT, H])
        t_row = sb("t_row", [H, N])
        shift = sb("shift", [P, 1])
        x_col = sb("x_col", [P, KF])
        no_row = sb("no_row", [1, ROW])
        ps_small = ps("ps_small", [P, F])
        ps_x = ps("ps_x", [P, F])
        ps_sum = ps("ps_sum", [P, F])
        own_ready, max_ready, col_ready, z_ready, t_ready = (sem("own_ready"), sem("max_ready"), sem("col_ready"),
                                                             sem("z_ready"), sem("t_ready"))
        off_ready, v_ready, shift_ready, t_st = sem("off_ready"), sem("v_ready"), sem("shift_ready"), sem("t_st")
        x_turned, x_copied, sum_ready, dve_step = (sem("x_turned"), sem("x_copied"), sem("sum_ready"),
                                                   sem("dve_step"))
        g_ready, rows_ready, no_row_st = sem("g_ready"), sem("rows_ready"), sem("no_row_st")
        block = ctx.enter_context(nc.Block())

        @block.vector
        def _(dve):
            step = Chain(dve, dve_step)
            nc.vector.memset(no_row[:, :], 0.0)
            nc.vector.memset(shift[:, :], SHIFT).then_inc(shift_ready, 1)
            nc.vector.tensor_reduce(d_own[:, :], sd_all[:, :, H:2 * H].rearrange("p t h -> p h t"), AX,
                                    ALU.max).then_inc(own_ready, 1)
            dve.wait_ge(x_turned, 1)
            nc.vector.tensor_copy(x_col[:, :], ps_x[:, 0:KF]).then_inc(x_copied, 1)
            dve.wait_ge(max_ready, 1)
            nc.vector.tensor_tensor(d_off[:, :, :], sd_all[:, :, H:2 * H],
                                    d_max[:, :].unsqueeze(1).broadcast_to([P, NT, H]),
                                    ALU.subtract).then_inc(off_ready, 1)
            dve.wait_ge(col_ready, 1)
            step.then(nc.vector.tensor_copy(d_col[:, :], ps_small[0:H, 0:1]))
            nc.vector.tensor_scalar(t_row[:, :], s_row[:, :], d_col[:, 0:1], 0.0, ALU.add,
                                    ALU.max).then_inc(z_ready, 1)
            dve.wait_ge(sum_ready, 1)
            nc.vector.tensor_copy(wh_sum[:, :], ps_sum[0:1, :])
            dve.wait_ge(v_ready, 1)
            v_rows = row_all[:, :, 0:H * (DH + 1)].rearrange("p t (h d) -> p t h d", d=DH + 1)
            nc.vector.tensor_copy(v_rows[:, :, :, DH], v_fac[:, :, :])
            dve.wait_ge(g_ready, 1)
            for t in range(0, NT, CH):
                nc.vector.tensor_tensor(
                    v_rows[:, t:t + CH, :, 0:DH], v_rows[:, t:t + CH, :, 0:DH],
                    v_fac[:, t:t + CH, :].unsqueeze(3).broadcast_to([P, CH, H, DH]), ALU.mult).then_inc(rows_ready, 1)

        @block.sync
        def _(sp):
            sp.wait_ge(shift_ready, 1)
            sp.dma_start(k.row_d[N:N + 1, :], no_row[:, :]).then_inc(no_row_st, 16)
            for t in range(0, NT, CH):
                sp.wait_ge(rows_ready, t // CH + 1)
                sp.dma_start(k.row_d[P * t:P * (t + CH), :].rearrange("(t p) f -> p t f", p=P),
                             row_all[:, t:t + CH, :]).then_inc(k.rows_st, 16)
            sp.wait_ge(no_row_st, 16)

        @block.gpsimd
        def _(gp):
            gp.wait_ge(own_ready, 1)
            nc.gpsimd.partition_all_reduce(d_max[:, :], d_own[:, :], P,
                                           bass.bass_isa.ReduceOp.max).then_inc(max_ready, 1)

        @block.tensor
        def _(pe):
            for f in range(KF):
                last = nc.tensor.matmul(ps_x[:, f:f + 1], x_sum[:, P * f:P * (f + 1)], k.ones[:, 0:1], start=True,
                                        stop=True)
            last.then_inc(x_turned, 1)
            pe.wait_ge(x_copied, 1)
            for f in range(KF):
                last = nc.tensor.matmul(ps_sum[0:1, :], x_col[:, f:f + 1], k.w[:, f, :], start=(f == 0),
                                        stop=(f == KF - 1))
            last.then_inc(sum_ready, 1)
            pe.wait_ge(max_ready, 1)
            nc.tensor.matmul(ps_small[0:H, 0:1], d_max[0:1, :], k.ones[0:1, 0:1], start=True,
                             stop=True).then_inc(col_ready, 1)

        @block.scalar
        def _(act):
            act.wait_ge(shift_ready, 1)
            act.wait_ge(off_ready, 1)
            nc.scalar.activation(v_fac[:, :, :], d_off[:, :, :], ACT.Exp, scale=0.2,
                                 bias=shift[:, 0:1]).then_inc(v_ready, 1)
            nc.scalar.activation(row_all[:, :, H * (DH + 1):ROW], d_off[:, :, :], ACT.Exp, scale=0.8,
                                 bias=shift[:, 0:1]).then_inc(g_ready, 1)
            act.wait_ge(z_ready, 1)
            nc.scalar.activation(t_row[:, :], t_row[:, :], ACT.Exp, scale=-0.8,
                                 bias=shift[0:H, 0:1]).then_inc(t_ready, 1)
            act.wait_ge(t_ready, 1)
            act.dma_start(k.trow_d, t_row[:, :]).then_inc(t_st, 16)
            act.wait_ge(t_st, 16)


def attend(nc, k, adj_rows, wh_sum, num_all, den_all):
    with ExitStack() as ctx:
        sb, ps, sem = stage(nc, ctx, "att")
        HALF = GT // 2
        index = sb("index", [P, 2, HALF, 2], i32)
        rows = sb("rows", [P, GT, ROW])
        edges = sb("edges", [P, GT, DS])
        t_bc = sb("t_bc", [P, 2, H, DS])
        empty = sb("empty", [1, DS])
        n_row = sb("n_row", [1, 32])
        weights = sb("weights", [P, GT, H, DS])
        ps_num = [ps(f"ps_num{p}", [P, F]) for p in range(H // 2)]
        ps_den = [ps(f"ps_den{p}", [P, F]) for p in range(H // 4)]
        rows_ld = [sem(f"rows_ld{b}") for b in range(GT)]
        edges_ld = [sem(f"edges_ld{b}") for b in range(GT)]
        made, used, summed, copied = sem("made"), sem("used"), sem("summed"), sem("copied")
        t_ld, empty_ld, n_ready, pool_step, gate = (sem("t_ld"), sem("empty_ld"), sem("n_ready"), sem("pool_step"),
                                                    sem("gate"))
        block = ctx.enter_context(nc.Block())

        def sections(eng, section):
            with eng.Fori(0, NS // 2) as pair:
                with eng.Fori(0, 2) as odd:
                    section(2 * pair + odd, odd)

        @block.sync
        def _(sp):
            def load_t(s, odd):
                sp.dma_start(t_bc[:, odd, :, :], k.trow_d[:, bass.ds(s * DS, DS)].unsqueeze(0)
                             .broadcast_to([P, H, DS])).then_inc(t_ld, 16)

            def load_empty(s):
                sp.dma_start(empty[:, :], k.empty_d.rearrange("n o -> o n")[:, bass.ds(s * DS, DS)]).then_inc(empty_ld, 16)

            load_t(0, 0)
            load_empty(0)
            sp.wait_ge(t_ld, 16)
            load_t(1, 1)
            with sp.Fori(0, NS // 2 - 1) as pair:
                for odd in range(2):
                    s = 2 * pair + 2 + odd
                    sp.wait_ge(summed, s - 1)
                    sp.wait_ge(t_ld, 16 * s)
                    sp.sem_inc(gate, 1)
                    load_empty(s - 1)
                    load_t(s, odd)
            sp.wait_ge(summed, NS - 1)
            load_empty(NS - 1)

        @block.gpsimd
        def _(gp):
            def section(s, odd):
                def fetch(q, g):
                    for half in range(2):
                        b = HALF * half
                        gp.wait_ge(made, GT * g + b + HALF)
                        gp.sem_inc(gate, 1)
                        nc.gpsimd.tensor_copy(
                            index[:, half, :, :],
                            k.index[:, bass.ds(s, 1), bass.ds(q * GT + b, HALF), :]
                            .rearrange("p o t c -> p (o t) c")).then_inc(pool_step, 1)
                        gp.wait_ge(pool_step, 2 * g + half + 1)
                        gp.sem_inc(gate, 1)
                        for i in range(HALF):
                            gp.indirect_dma_start(edges[:, b + i, :], None, adj_rows,
                                                  bass.IndirectOffsetOnAxis(ap=index[:, half, i, 1:2], axis=0),
                                                  bounds_check=N * NS - 1, oob_is_err=False).then_inc(edges_ld[b + i], 16)
                        for i in range(HALF):
                            gp.wait_ge(used, GT * g + b + i + 1)
                            gp.sem_inc(gate, 1)
                            gp.indirect_dma_start(rows[:, b + i, :], None, k.row_d,
                                                  bass.IndirectOffsetOnAxis(ap=index[:, half, i, 0:1], axis=0),
                                                  bounds_check=N, oob_is_err=False).then_inc(rows_ld[b + i], 16)

                section_groups(gp, k, s, fetch)

            sections(gp, section)

        @block.vector
        def _(dve):
            nc.vector.memset(n_row[:, :], float(N)).then_inc(n_ready, 1)
            dve.sem_inc(made, GT)

            def section(s, odd):
                dve.wait_ge(t_ld, 16 * (s + 1))

                def weigh(q, g):
                    for b in range(GT):
                        dve.wait_ge(edges_ld[b], 16 * (g + 1))
                        dve.wait_ge(rows_ld[b], 16 * (g + 1))
                        dve.wait_ge(used, GT * g + b + 1)
                        for h in range(H):
                            last = nc.vector.scalar_tensor_tensor(
                                weights[:, b, h, :], t_bc[:, bass.ds(odd, 1), h, :].rearrange("p o i -> p (o i)"),
                                rows[:, b, ROW - H + h:ROW - H + h + 1], edges[:, b, :], ALU.max, ALU.mult)
                        last.then_inc(made, 1)

                section_groups(dve, k, s, weigh)

            sections(dve, section)

        @block.tensor
        def _(pe):
            pe.sem_inc(used, GT)
            pe.wait_ge(n_ready, 1)

            def section(s, odd):
                pe.wait_ge(copied, s + 1)

                def add(q, g):
                    for b in range(GT):
                        first = isinstance(q, int) and q == 0 and b == 0
                        pe.wait_ge(made, GT * g + b + 1 + GT)
                        for h in range(H):
                            at = DH * (h % 2)
                            nc.tensor.matmul(ps_num[h // 2][at:at + DH, 0:DS],
                                             rows[:, b, (DH + 1) * h:(DH + 1) * h + DH], weights[:, b, h, :],
                                             start=first, stop=False)
                        for h in range(H):
                            at = 32 * (h % 4)
                            v = (DH + 1) * h + DH
                            last = nc.tensor.matmul(ps_den[h // 4][at:at + 32, 0:DS],
                                                    rows[:, b, v:v + 1].broadcast_to([P, 32]), weights[:, b, h, :],
                                                    start=first, stop=False, tile_position=(0, at))
                        last.then_inc(used, 1)

                section_groups(pe, k, s, add)
                pe.wait_ge(empty_ld, 16 * (s + 1))
                for h in range(H):
                    at = DH * (h % 2)
                    nc.tensor.matmul(ps_num[h // 2][at:at + DH, 0:DS], wh_sum[0:1, DH * h:DH * (h + 1)], empty[:, :],
                                     start=False, stop=True)
                for h in range(H):
                    at = 32 * (h % 4)
                    last = nc.tensor.matmul(ps_den[h // 4][at:at + 32, 0:DS], n_row[0:1, :], empty[:, :], start=False,
                                            stop=True, tile_position=(0, at))
                last.then_inc(summed, 1)

            sections(pe, section)

        @block.scalar
        def _(act):
            act.sem_inc(copied, 1)
            with act.Fori(0, NS) as s:
                act.wait_ge(summed, s + 1)
                for p in range(H // 2):
                    nc.scalar.copy(num_all[:, p, bass.ds(s * DS, DS)], ps_num[p][:, 0:DS])
                for p in range(H // 4):
                    last = nc.scalar.copy(den_all[:, p, bass.ds(s * DS, DS)], ps_den[p][:, 0:DS])
                last.then_inc(copied, 1)


def finish_nodes(nc, k, ins, num_all, den_all, out):
    with ExitStack() as ctx:
        sb, ps, sem = stage(nc, ctx, "fin")
        den = sb("den", [P, 2, SEC])
        pick = sb("pick", [P, 4 * DH])
        low = sb("low", [P, 4, SEC])
        hid1, hid2, hid3 = sb("hid1", [P, 2, SEC]), sb("hid2", [P, SEC]), sb("hid3", [P, 2, SEC])
        w1, w2, w3, w4 = (sb("w1", [P, 4, M1]), sb("w2", [P, 2, M2]), sb("w3", [P, M3]), sb("w4", [P, 2, F]))
        b1, b2, b3 = sb("b1", [P, 2]), sb("b2", [P, 1]), sb("b3", [P, 2])
        b4 = sb("b4", [P, F])
        base = sb("base", [P, 4, F])
        y = sb("y", [P, 4, F])
        seen, moments, rstd = sb("seen", [P, 4, 6]), sb("moments", [P, 4, 2]), sb("rstd", [P, 4])
        minus_half = sb("minus_half", [P, 4])
        ps_spread = [ps(f"ps_spread{p}", [P, SEC]) for p in range(4)]
        ps_mlp = [ps(f"ps_mlp{b}", [P, SEC]) for b in range(4)]
        par_ld, x1_ld, out_st = sem("par_ld"), sem("x1_ld"), sem("out_st")
        den_ready, den_spread, ratio_ready = sem("den_ready"), sem("den_spread"), sem("ratio_ready")
        low_ready, exp_ready, enc_ready = sem("low_ready"), sem("exp_ready"), sem("enc_ready")
        mlp_ready, hid_ready, y_mlp, y_part = sem("mlp_ready"), sem("hid_ready"), sem("y_mlp"), sem("y_part")
        y_ready, y_free, base_ready = sem("y_ready"), sem("y_free"), sem("base_ready")
        dve_step, pool_step, gate = sem("dve_step"), sem("pool_step"), sem("gate")
        moments_ready, rstd_ready, rstd_step = sem("moments_ready"), sem("rstd_ready"), sem("rstd_step")
        PARAMS = 9
        block = ctx.enter_context(nc.Block())

        def cols(c):
            return bass.ds(c * SEC, SEC)

        @block.sync
        def _(sp):
            for dst, name in ((pick, "pick"), (b1, "b1"), (b2, "b2"), (b3, "b3"), (w3, "w3_t")):
                sp.dma_start(dst[:, :], ins[name]).then_inc(par_ld, 16)
            for dst, name in ((w1, "w1_t"), (w2, "w2_t"), (w4, "w4_t")):
                sp.dma_start(dst[:, :, :], tiles_of(ins[name])).then_inc(par_ld, 16)
            sp.dma_start(b4[:, :], ins["b4"].broadcast_to([P, F])).then_inc(par_ld, 16)
            with sp.Fori(0, SECS) as c:
                sp.wait_ge(y_part, c + 1)
                sp.sem_inc(gate, 1)
                sp.dma_start(base[:, :, :], tiles_of(k.x1_d)[:, bass.ds(4 * c, 4), :]).then_inc(x1_ld, 16)

        @block.vector
        def _(dve):
            dve.sem_inc(y_part, 1)

            def invert_sums(c):
                dve.wait_ge(den_spread, c + 1)
                nc.vector.reciprocal(den[:, :, :], den_all[:, :, cols(c)]).then_inc(den_ready, 1)
                dve.wait_ge(den_spread, c + 2)
                for p in range(4):
                    last = nc.vector.tensor_tensor(num_all[:, p, cols(c)], num_all[:, p, cols(c)],
                                                   ps_spread[p][:, :], ALU.mult)
                last.then_inc(ratio_ready, 1)

            def end(c):
                dve.wait_ge(base_ready, c + 1)
                dve.wait_ge(y_free, c + 1)
                dve.wait_ge(y_mlp, c + 1)
                for i in range(4):
                    last = nc.vector.tensor_tensor(y[:, i, :], ps_mlp[i][:, :], base[:, i, :], ALU.add)
                last.then_inc(y_part, 1)
                dve.wait_ge(y_part, c + 2)
                for i in range(4):
                    last = nc.vector.bn_stats(seen[:, i, :], y[:, i, :])
                last.then_inc(dve_step, 1)
                dve.wait_ge(dve_step, c + 1)
                dve.sem_inc(gate, 1)
                for i in range(4):
                    last = nc.vector.bn_aggr(moments[:, i, :], seen[:, i, :])
                last.then_inc(moments_ready, 1)
                dve.wait_ge(rstd_ready, c + 1)
                for i in range(4):
                    last = nc.vector.tensor_scalar(y[:, i, :], y[:, i, :], moments[:, i, 0:1], rstd[:, i:i + 1],
                                                   ALU.subtract, ALU.mult)
                last.then_inc(y_ready, 1)

            invert_sums(0)
            invert_sums(1)
            with dve.Fori(0, SECS - 2) as c:
                invert_sums(c + 2)
                end(c)
            end(SECS - 2)
            end(SECS - 1)

        @block.tensor
        def _(pe):
            pe.wait_ge(par_ld, 16 * PARAMS)
            pe.sem_inc(den_spread, 1)

            def spread_sums(c):
                pe.wait_ge(den_ready, c + 1)
                pe.wait_ge(ratio_ready, c + 1)
                for p in range(4):
                    last = nc.tensor.matmul(ps_spread[p][:, :], pick[:, P * (p % 2):P * (p % 2 + 1)],
                                            den[:, p // 2, :], start=True, stop=True)
                last.then_inc(den_spread, 1)

            def hidden(c):
                pe.wait_ge(enc_ready, c + 1)
                pe.wait_ge(y_part, c + 1)
                for m in range(2):
                    for e in range(4):
                        last = nc.tensor.matmul(ps_mlp[m][:, :], w1[:, e, P * m:P * (m + 1)], num_all[:, e, cols(c)],
                                                start=(e == 0), stop=(e == 3))
                last.then_inc(mlp_ready, 1)
                pe.wait_ge(hid_ready, 3 * c + 1)
                for e in range(2):
                    last = nc.tensor.matmul(ps_mlp[2][:, :], w2[:, e, :], hid1[:, e, :], start=(e == 0), stop=(e == 1))
                last.then_inc(mlp_ready, 1)
                pe.wait_ge(hid_ready, 3 * c + 2)
                for m in range(2):
                    last = nc.tensor.matmul(ps_mlp[m][:, :], w3[:, P * m:P * (m + 1)], hid2[:, :], start=True,
                                            stop=True)
                last.then_inc(mlp_ready, 1)

            def output(c):
                pe.wait_ge(hid_ready, 3 * c + 3)
                for i in range(4):
                    for e in range(2):
                        last = nc.tensor.matmul(ps_mlp[i][:, :], hid3[:, e, P * i:P * (i + 1)], w4[:, e, :],
                                                start=(e == 0), stop=(e == 1))
                last.then_inc(y_mlp, 1)

            spread_sums(0)
            spread_sums(1)
            with pe.Fori(0, SECS - 2) as c:
                hidden(c)
                spread_sums(c + 2)
                output(c)
            for c in range(SECS - 2, SECS):
                hidden(c)
                output(c)

        @block.scalar
        def _(act):
            act.wait_ge(par_ld, 16 * PARAMS)

            def elu(c):
                act.wait_ge(ratio_ready, c + 2)
                if not (isinstance(c, int) and c == 0):
                    act.wait_ge(enc_ready, c)
                part = num_all[:, :, cols(c)]
                nc.scalar.activation(low[:, :, :], part, ACT.Relu, scale=-1.0).then_inc(low_ready, 1)
                act.wait_ge(low_ready, c + 1)
                nc.scalar.activation(low[:, :, :], low[:, :, :], ACT.Exp, scale=-1.0)
                nc.scalar.activation(part, part, ACT.Relu).then_inc(exp_ready, 1)

            def hidden(c):
                act.wait_ge(mlp_ready, 3 * c + 1)
                nc.scalar.activation(hid1[:, 0, :], ps_mlp[0][:, :], ACT.Relu, bias=b1[:, 0:1])
                nc.scalar.activation(hid1[:, 1, :], ps_mlp[1][:, :], ACT.Relu, bias=b1[:, 1:2]).then_inc(hid_ready, 1)
                act.wait_ge(mlp_ready, 3 * c + 2)
                nc.scalar.activation(hid2[:, :], ps_mlp[2][:, :], ACT.Relu, bias=b2[:, 0:1]).then_inc(hid_ready, 1)
                act.wait_ge(mlp_ready, 3 * c + 3)
                nc.scalar.activation(hid3[:, 0, :], ps_mlp[0][:, :], ACT.Relu, bias=b3[:, 0:1])
                nc.scalar.activation(hid3[:, 1, :], ps_mlp[1][:, :], ACT.Relu, bias=b3[:, 1:2]).then_inc(hid_ready, 1)

            elu(0)
            with act.Fori(0, SECS - 1) as c:
                hidden(c)
                elu(c + 1)
            hidden(SECS - 1)

        @block.gpsimd
        def _(gp):
            gp.sem_inc(ratio_ready, 1)
            gp.sem_inc(y_free, 1)
            nc.gpsimd.memset(minus_half[:, :], -0.5).then_inc(rstd_step, 1)
            gp.wait_ge(par_ld, 16 * PARAMS)

            def finish_elu(c):
                gp.wait_ge(exp_ready, c + 1)
                gp.sem_inc(gate, 1)
                part = num_all[:, :, cols(c)]
                nc.gpsimd.tensor_scalar(low[:, :, :], low[:, :, :], -1.0, None, ALU.add).then_inc(pool_step, 1)
                gp.wait_ge(pool_step, c + 1)
                nc.gpsimd.tensor_tensor(part, part, low[:, :, :], ALU.add).then_inc(enc_ready, 1)

            def add_bias(c):
                gp.wait_ge(x1_ld, 16 * (c + 1))
                nc.gpsimd.tensor_tensor(base[:, :, :], base[:, :, :],
                                        b4[:, :].unsqueeze(1).broadcast_to([P, 4, F]), ALU.add).then_inc(base_ready, 1)

            def end(c):
                gp.wait_ge(moments_ready, c + 1)
                gp.sem_inc(gate, 1)
                nc.gpsimd.tensor_scalar(rstd[:, :], moments[:, :, 1], EPS, None, ALU.add).then_inc(rstd_step, 1)
                gp.wait_ge(rstd_step, c + 2)
                nc.gpsimd.tensor_tensor(rstd[:, :], rstd[:, :], minus_half[:, :], ALU.pow).then_inc(rstd_ready, 1)
                gp.wait_ge(y_ready, c + 1)
                gp.sem_inc(gate, 1)
                gp.dma_start(tiles_of(out)[:, bass.ds(4 * c, 4), :], y[:, :, :]).then_inc(out_st, 16)
                gp.wait_ge(out_st, 16 * (c + 1))
                gp.sem_inc(y_free, 1)

            finish_elu(0)
            with gp.Fori(0, SECS - 1) as c:
                add_bias(c)
                finish_elu(c + 1)
                end(c)
            add_bias(SECS - 1)
            end(SECS - 1)


def build(nc, ins, out):
    with ExitStack() as ctx:
        k = make_kept(nc, ctx)
        c_all = ctx.enter_context(nc.sbuf_tensor("c_all", [P, NT], f32))
        cx_all = ctx.enter_context(nc.sbuf_tensor("cx_all", [P, NT], f32))
        with nc.sbuf_tensor("key_row", [P, LIST], f32) as key_row:
            with nc.sbuf_tensor("xs", [P, NT, 2 * F], f16) as xs:
                split_features(nc, k, ins, xs)
                neighbour_sums(nc, k, ins, xs, key_row)
            with (nc.sbuf_tensor("att_all", [P, RT * H], f32) as att_all,
                  nc.sbuf_tensor("weight_all", [P, RT], f32) as weight_all):
                relation_scores(nc, k, ins, key_row, att_all, weight_all)
                node_coefficients(nc, k, ins, c_all, cx_all)
                relation_values(nc, k, ins, att_all, weight_all)
        wh_sum = ctx.enter_context(nc.sbuf_tensor("wh_sum", [1, F], f32))
        with nc.sbuf_tensor("row_all", [P, NT, ROW], f32) as row_all:
            with (nc.sbuf_tensor("sd_all", [P, NT, 2 * H], f32) as sd_all,
                  nc.sbuf_tensor("s_row", [H, N], f32) as s_row,
                  nc.sbuf_tensor("x_sum", [P, F], f32) as x_sum):
                project_nodes(nc, k, ins, c_all, cx_all, row_all, sd_all, s_row, x_sum)
                attention_factors(nc, k, row_all, sd_all, s_row, x_sum, wh_sum)
            with ExitStack() as lists:
                def sb(name, shape, dt=f32):
                    return lists.enter_context(nc.sbuf_tensor(f"lists_{name}", shape, dt))

                ls = make_lists(sb)
                source_index(nc, k, ins, ls)
                source_lists(nc, k, ls)
                list_rows(nc, k, ls)
        num_all = ctx.enter_context(nc.sbuf_tensor("num_all", [P, 4, N], f32))
        den_all = ctx.enter_context(nc.sbuf_tensor("den_all", [P, 2, N], f32))
        adj_rows = ins["adj_t"].rearrange("j (s i) -> (j s) i", i=DS)
        attend(nc, k, adj_rows, wh_sum, num_all, den_all)
        finish_nodes(nc, k, ins, num_all, den_all, out)

_LAY = {
    "x": lambda np, a: a["x"],
    "adj_t": lambda np, a: a["adj"].T,
    "adj_diag": lambda np, a: np.diagonal(a["adj"]).reshape(NT, P).T,
    "pairs": lambda np, a: a["L0_gnn_rel_pair_index"],
    "W": lambda np, a: a["L1_gnn_W"].transpose(1, 0, 2).reshape(F, H * DH),
    "a1": lambda np, a: a["L1_gnn_a1"].reshape(1, F),
    "a2": lambda np, a: a["L1_gnn_a2"].reshape(1, F),
    "wq_t": lambda np, a: a["L0_gnn_Wq"].T,
    "wk_t": lambda np, a: a["L0_gnn_Wk"].T,
    "bq": lambda np, a: a["L0_gnn_bq"].reshape(1, F),
    "bk": lambda np, a: a["L0_gnn_bk"].reshape(1, F),
    "w1_t": lambda np, a: a["L1_gnn_W1"].T,
    "w2_t": lambda np, a: a["L1_gnn_W2"].T,
    "w3_t": lambda np, a: a["L1_gnn_W3"].T,
    "w4_t": lambda np, a: a["L1_gnn_W4"].T,
    "b1": lambda np, a: a["L1_gnn_b1"].reshape(2, P).T,
    "b2": lambda np, a: a["L1_gnn_b2"].reshape(1, P).T,
    "b3": lambda np, a: a["L1_gnn_b3"].reshape(2, P).T,
    "b4": lambda np, a: a["L1_gnn_b4"].reshape(1, F),
    "ident": lambda np, a: np.eye(P, dtype=np.float32),
    "before": lambda np, a: np.tril(np.ones((P, P), np.float32), -1),
    "differ": lambda np, a: np.concatenate([np.eye(NT, dtype=np.float32) - np.eye(NT, k=1, dtype=np.float32),
                                            np.where(np.arange(NT) > 0, P, 0).astype(np.float32)[:, None]], axis=1),
    "pick": lambda np, a: np.concatenate([np.repeat(np.eye(P, dtype=np.float32)[:, 32 * h:32 * h + 1], DH, axis=1)
                                          for h in range(4)], axis=1),
}


def kernel(**inputs):
    import numpy as _np
    import concourse.bacc as _bacc
    from concourse.bass_utils import run_bass_kernel_spmd as _run

    nc = _bacc.Bacc("TRN2", target_bir_lowering=False, num_devices=1)
    given = {n: _np.asarray(v) for n, v in inputs.items()}
    arrays, ins = {}, {}
    for name, lay in _LAY.items():
        a = _np.ascontiguousarray(lay(_np, given))
        arrays[f"in_{name}_dram"] = a
        ins[name] = nc.dram_tensor(f"in_{name}_dram", a.shape, mybir.dt.from_np(a.dtype), kind="ExternalInput").ap()
    out = nc.dram_tensor("out_0_dram", (N, F), f32, kind="ExternalOutput").ap()
    build(nc, ins, out)
    return _run(nc, [arrays], core_ids=[0]).results[0]["out_0_dram"]
```

```python
import concourse.bass as bass
from concourse import mybir
from contextlib import ExitStack

P = 128
N, F, H, DH = 4096, 512, 8, 64
NT, KF = N // P, F // P
RP, RC = 125, 80
RT = -(-RP * RC // P)
LIST = (RT + 1) * P
SEC, SECS = 512, N // 512
DS, NS = 256, N // 256
GT = 4
TR = NT + 2
PACK = 16
MG = 3
GCOL = H * (DH + 1)
ROW = GCOL + H + 1
CH = 4
PIECES = NT // CH
SR = 32
CR = 16
DIAG, EPS = 1e-7, 1e-5
SHIFT = 34.0
BIG = 1.0e30
OFF = 16384.0
M1, M2, M3 = 256, 128, 256

f32, f16, i32, u8 = mybir.dt.float32, mybir.dt.float16, mybir.dt.int32, mybir.dt.uint8
ALU = mybir.AluOpType
ACT = mybir.ActivationFunctionType
AX = mybir.AxisListType.X


class Chain:

    def __init__(self, eng, sem, base=0):
        self.eng, self.sem, self.base, self.n = eng, sem, base, 0

    def then(self, ins):
        self.n += 1
        ins.then_inc(self.sem, 1)
        self.eng.wait_ge(self.sem, self.base + self.n)


def tiles_of(ap):
    return ap.rearrange("(t p) f -> p t f", p=P)


def stage(nc, ctx, of):
    sems = []

    def give_back():
        nc.clear_and_free_semaphores(sems)
        nc.all_engine_barrier()

    ctx.callback(give_back)

    def sb(name, shape, dt=f32):
        return ctx.enter_context(nc.sbuf_tensor(f"{of}_{name}", shape, dt))

    def ps(name, shape):
        return ctx.enter_context(nc.psum_tensor(f"{of}_{name}", shape, f32))

    def sem(name):
        sems.append(nc.alloc_semaphore(f"{of}_{name}"))
        return sems[-1]

    return sb, ps, sem


class Kept:
    pass


def make_kept(nc, ctx):
    k = Kept()

    def sb(name, shape, dt=f32):
        return ctx.enter_context(nc.sbuf_tensor(name, shape, dt))

    def dram(name, shape, dt=f32):
        return nc.dram_tensor(name, shape, dt, kind="Internal").ap()

    k.ident = sb("ident", [P, P])
    k.before = sb("before", [P, P])
    k.ones = sb("ones", [P, P])
    k.w = sb("w", [P, KF, F])
    k.wa = sb("wa", [P, KF, 2 * H])
    k.scale = sb("scale", [P, 2])
    k.deg = sb("deg", [P, NT])
    k.nlist = sb("nlist", [P, 1], i32)
    k.marks = sb("marks", [P, NS, NT], f16)
    k.groups = sb("groups", [P, NS], i32)
    k.index = sb("index", [P, NS, NT, 2], i32)
    k.empty = sb("empty", [P, NT])
    k.empty_st = ctx.enter_context(nc.semaphore("empty_st"))
    k.lonely = sb("lonely", [1, 1], i32)
    k.rows_st = ctx.enter_context(nc.semaphore("rows_st"))
    k.row_d = dram("row_d", [N + 1, ROW])
    k.agg_d = dram("agg_d", [N, F])
    k.rel_d = dram("rel_d", [N, F])
    k.stats_d = dram("stats_d", [N, SR])
    k.coef_d = dram("coef_d", [N, CR])
    k.list_d = dram("list_d", [LIST, 1])
    k.tot_d = dram("tot_d", [1, P])
    k.x1_d = dram("x1_d", [N, F])
    k.trow_d = dram("trow_d", [H, N])
    k.empty_d = dram("empty_d", [N, 1])
    return k


def split_features(nc, k, ins, xs):
    with ExitStack() as ctx:
        sb, ps, sem = stage(nc, ctx, "split")
        x_sb = sb("x_sb", [P, NT, F])
        a_row = sb("a_row", [P, 2, F])
        a_prod = sb("a_prod", [P, KF, F])
        part_max = sb("part_max", [P, PIECES])
        own_max = sb("own_max", [P, 1])
        all_max = sb("all_max", [P, 1])
        floor_max = sb("floor_max", [P, 1])
        exponent = sb("exponent", [P, 1], i32)
        x_in = [sem(f"x_in{i}") for i in range(PIECES)]
        w_in, const_in = sem("w_in"), sem("const_in")
        dve_step, own_ready, max_ready = sem("dve_step"), sem("own_ready"), sem("max_ready")
        scale_ready, high_ready, split_done = sem("scale_ready"), sem("high_ready"), sem("split_done")
        block = ctx.enter_context(nc.Block())

        @block.sync
        def _(sp):
            sp.dma_start(k.w[:, :, :], ins["W"].rearrange("(t p) f -> p t f", p=P)).then_inc(w_in, 16)
            sp.dma_start(a_row[:, 0, :], ins["a1"].broadcast_to([P, F])).then_inc(w_in, 16)
            sp.dma_start(a_row[:, 1, :], ins["a2"].broadcast_to([P, F])).then_inc(w_in, 16)
            for i in range(PIECES):
                sp.dma_start(x_sb[:, CH * i:CH * (i + 1), :],
                             tiles_of(ins["x"])[:, CH * i:CH * (i + 1), :]).then_inc(x_in[i], 16)
            sp.dma_start(k.ident[:, :], ins["ident"]).then_inc(const_in, 16)
            sp.dma_start(k.before[:, :], ins["before"]).then_inc(const_in, 16)
            sp.wait_ge(const_in, 32)

        @block.vector
        def _(dve):
            step = Chain(dve, dve_step)
            nc.vector.memset(k.ones[:, :], 1.0)
            dve.wait_ge(w_in, 48)
            for a in range(2):
                for t in range(KF):
                    last = nc.vector.tensor_tensor(a_prod[:, t, :], k.w[:, t, :], a_row[:, a, :], ALU.mult)
                step.then(last)
                for t in range(KF):
                    last = nc.vector.tensor_reduce(k.wa[:, t, H * a:H * (a + 1)],
                                                   a_prod[:, t, :].rearrange("p (h d) -> p h d", d=DH), AX, ALU.add)
                step.then(last)
            for i in range(PIECES):
                dve.wait_ge(x_in[i], 16)
                last = nc.vector.tensor_reduce(part_max[:, i:i + 1],
                                               x_sb[:, CH * i:CH * (i + 1), :].rearrange("p t f -> p (t f)"),
                                               AX, ALU.max, apply_absolute_value=True)
            step.then(last)
            nc.vector.tensor_reduce(own_max[:, :], part_max[:, :], AX, ALU.max).then_inc(own_ready, 1)
            dve.wait_ge(max_ready, 1)
            step.then(nc.vector.tensor_scalar(floor_max[:, :], all_max[:, :], 1e-20, None, ALU.max))
            step.then(nc.vector.tensor_single_scalar(exponent[:, :], floor_max[:, :].bitcast(i32),
                                                     0x7F800000, ALU.bitwise_and))
            step.then(nc.vector.tensor_scalar(k.scale[:, 0:1].bitcast(i32), exponent[:, :],
                                              -1.0, float(268 << 23), ALU.mult, ALU.add))
            nc.vector.tensor_scalar(k.scale[:, 1:2].bitcast(i32), exponent[:, :],
                                    float(-(14 << 23)), None, ALU.add).then_inc(scale_ready, 1)
            dve.wait_ge(scale_ready, 1)
            for i in range(PIECES):
                dve.wait_ge(high_ready, i + 1)
                last = nc.vector.scalar_tensor_tensor(xs[:, CH * i:CH * (i + 1), F:2 * F],
                                                      x_sb[:, CH * i:CH * (i + 1), :], k.scale[:, 0:1],
                                                      xs[:, CH * i:CH * (i + 1), 0:F], ALU.mult, ALU.subtract)
            last.then_inc(split_done, 1)
            dve.wait_ge(split_done, 1)

        @block.gpsimd
        def _(gp):
            gp.wait_ge(own_ready, 1)
            nc.gpsimd.partition_all_reduce(all_max[:, :], own_max[:, :], P,
                                           bass.bass_isa.ReduceOp.max).then_inc(max_ready, 1)

        @block.scalar
        def _(act):
            act.wait_ge(scale_ready, 1)
            for i in range(PIECES):
                nc.scalar.activation(xs[:, CH * i:CH * (i + 1), 0:F], x_sb[:, CH * i:CH * (i + 1), :], ACT.Copy,
                                     scale=k.scale[:, 0:1]).then_inc(high_ready, 1)


def neighbour_sums(nc, k, ins, xs, key_row):
    with ExitStack() as ctx:
        sb, ps, sem = stage(nc, ctx, "sums")
        R = 4
        adj_in = sb("adj_in", [P, R, CH, SEC])
        adj16 = sb("adj16", [P, R, CH, SEC], f16)
        agg = sb("agg", [P, 4, F])
        one16 = sb("one16", [P, 1], f16)
        zeros = sb("zeros", [P, 1024])
        rows0 = sb("rows0", [P, NT, SR])
        blank = sb("blank", [P, LIST // P])
        pairs = sb("pairs", [RP, RC, 2], i32)
        sub = sb("sub", [RP, RC])
        obj = sb("obj", [RP, RC])
        key = sb("key", [RP, RC])
        key_i = sb("key_i", [RP, RC], i32)
        apart = sb("apart", [RP, RC])
        on_edge = sb("on_edge", [RP, RC])
        valid = sb("valid", [RP, RC])
        scan = sb("scan", [RP, 2, RC])
        tot_row = sb("tot_row", [RP, RP])
        fold = sb("fold", [RP, 2, P])
        pos = sb("pos", [RP, RC])
        pos_i = sb("pos_i", [RP, RC], i32)
        eight_i = sb("eight_i", [RP, 8], i32)
        eight_f = sb("eight_f", [RP, 8])
        ps_agg = ps("ps_agg", [P, 4, F])
        ps_deg = ps("ps_deg", [P, F])

        adj_ld = [sem(f"adj_ld{i}") for i in range(R)]
        cast_done, marked, sums_done = sem("cast_done"), sem("marked"), sem("sums_done")
        agg_ready, agg_st = sem("agg_ready"), sem("agg_st")
        consts, fills, pairs_ld = sem("consts"), sem("fills"), sem("pairs_ld")
        pool_step, gate, dve_step, keys_ready, sp_gate = sem("pool_step"), sem("gate"), sem("dve_step"), sem("keys_ready"), sem("sp_gate")
        flag_ld, tot_st, tot_ld, list_st, row_ld = (sem("flag_ld"), sem("tot_st"), sem("tot_ld"),
                                                    sem("list_st"), sem("row_ld"))
        block = ctx.enter_context(nc.Block())
        adj_t = tiles_of(ins["adj_t"])

        @block.sync
        def _(sp):
            sp.dma_start(pairs[:, :, :], ins["pairs"].rearrange("(p c) two -> p c two", p=RP)).then_inc(pairs_ld, 16)
            sp.sem_inc(agg_st, 16)

            def load(s, c):
                sp.wait_ge(cast_done, s * PIECES + c + 1)
                sp.sem_inc(sp_gate, 1)
                sp.dma_start(adj_in[:, c % R, :, :],
                             adj_t[:, CH * c:CH * (c + 1), bass.ds(s * SEC, SEC)]).then_inc(adj_ld[c % R], 16)

            def store_sums(s):
                sp.wait_ge(agg_ready, s + 2)
                sp.sem_inc(sp_gate, 1)
                sp.dma_start(tiles_of(k.agg_d)[:, bass.ds(s * 4, 4), :], agg[:, :, :]).then_inc(agg_st, 16)

            for c in range(R):
                load(0, c)
            sp.wait_ge(consts, 1)
            for i in range(N * F // P // 1024):
                sp.dma_start(k.rel_d.rearrange("(p t) f -> p (t f)", p=P)[:, 1024 * i:1024 * (i + 1)],
                             zeros[:, :]).then_inc(fills, 16)
            sp.dma_start(k.stats_d.rearrange("(p t) c -> p (t c)", p=P),
                         rows0[:, :, :].rearrange("p t c -> p (t c)")).then_inc(fills, 16)
            sp.dma_start(k.list_d.rearrange("(p c) o -> p (c o)", p=P), blank[:, :]).then_inc(fills, 16)
            with sp.Fori(0, SECS - 1) as s:
                for c in range(R):
                    load(s, c + R)
                for c in range(R):
                    load(s + 1, c)
                store_sums(s)
            s = SECS - 1
            for c in range(R):
                load(s, c + R)
            store_sums(s)
            sp.wait_ge(agg_st, 16 * (SECS + 1))

        @block.scalar
        def _(act):
            act.sem_inc(cast_done, R)
            with act.Fori(0, SECS) as s:
                for c in range(PIECES):
                    act.wait_ge(adj_ld[c % R], 16 * (2 * s + c // R + 1))
                    act.wait_ge(sums_done, s * PIECES + c + 1)
                    act.wait_ge(marked, s * PIECES + c + 1)
                    nc.scalar.activation(adj16[:, c % R, :, :], adj_in[:, c % R, :, :],
                                         ACT.Copy).then_inc(cast_done, 1)

        @block.tensor
        def _(pe):
            pe.sem_inc(sums_done, R)
            pe.wait_ge(consts, 1)
            with pe.Fori(0, SECS) as s:
                pe.wait_ge(agg_ready, s + 1)
                for c in range(PIECES):
                    pe.wait_ge(cast_done, s * PIECES + c + 1 + R)
                    for q in range(CH):
                        j = CH * c + q
                        for i in range(4):
                            block_t = adj16[:, c % R, q, P * i:P * (i + 1)]
                            nc.tensor.matmul(ps_agg[:, i, :], block_t, xs[:, j, 0:F], start=(j == 0), stop=False)
                            nc.tensor.matmul(ps_agg[:, i, :], block_t, xs[:, j, F:2 * F], start=False,
                                             stop=(j == NT - 1))
                            last = nc.tensor.matmul(ps_deg[:, i:i + 1], block_t, one16[:, :],
                                                    start=(j == 0 and i == 0), stop=(j == NT - 1),
                                                    skip_group_check=True)
                    last.then_inc(sums_done, 1)

        @block.vector
        def _(dve):
            dve.sem_inc(marked, R)
            dve.sem_inc(agg_ready, 1)
            nc.vector.memset(one16[:, :], 1.0)
            nc.vector.memset(zeros[:, :], 0.0)
            nc.vector.memset(blank[:, :], -1.0)
            nc.vector.memset(rows0[:, :, 0:H], DIAG)
            nc.vector.memset(rows0[:, :, H:SR], 0.0).then_inc(consts, 1)
            step = Chain(dve, dve_step)
            dve.wait_ge(pairs_ld, 16)
            nc.vector.tensor_copy(sub[:, :], pairs[:, :, 0])
            step.then(nc.vector.tensor_copy(obj[:, :], pairs[:, :, 1]))
            nc.vector.tensor_tensor(apart[:, :], sub[:, :], obj[:, :], ALU.not_equal)
            step.then(nc.vector.scalar_tensor_tensor(key[:, :], obj[:, :], float(N), sub[:, :], ALU.mult, ALU.add))
            nc.vector.tensor_copy(key_i[:, :], key[:, :]).then_inc(keys_ready, 1)
            with dve.Fori(0, SECS) as s:
                for c in range(PIECES):
                    dve.wait_ge(cast_done, s * PIECES + c + 1 + R)
                    nc.vector.tensor_reduce(
                        k.marks[:, bass.ds(2 * s, 2), CH * c:CH * (c + 1)].rearrange("p h q -> p q h"),
                        adj16[:, c % R, :, :].rearrange("p q (h i) -> p q h i", i=DS), AX, ALU.max).then_inc(marked, 1)
                dve.wait_ge(sums_done, (s + 1) * PIECES + R)
                dve.wait_ge(agg_st, 16 * (s + 1))
                nc.vector.tensor_copy(k.deg[:, bass.ds(4 * s, 4)], ps_deg[:, 0:4])
                nc.vector.tensor_scalar(agg[:, :, :], ps_agg[:, :, :], k.scale[:, 1:2], None,
                                        ALU.mult).then_inc(agg_ready, 1)

        @block.gpsimd
        def _(gp):
            step = Chain(gp, pool_step)
            gp.wait_ge(keys_ready, 1)
            adj_flat = ins["adj_t"].rearrange("j (i o) -> (j i) o", o=1)
            gathered = step.n
            step.base = 0
            with gp.Fori(0, RC // 8) as g:
                nc.gpsimd.tensor_copy(eight_i[:, :], key_i[:, bass.ds(8 * g, 8)]).then_inc(pool_step, 1)
                gp.wait_ge(pool_step, gathered + 2 * g + 1)
                gp.sem_inc(gate, 1)
                for e in range(8):
                    gp.indirect_dma_start(eight_f[:, e:e + 1], None, adj_flat,
                                          bass.IndirectOffsetOnAxis(ap=eight_i[:, e:e + 1], axis=0),
                                          bounds_check=N * N - 1, oob_is_err=False).then_inc(flag_ld, 16)
                gp.wait_ge(flag_ld, 128 * (g + 1))
                gp.sem_inc(gate, 1)
                nc.gpsimd.tensor_copy(on_edge[:, bass.ds(8 * g, 8)], eight_f[:, :]).then_inc(pool_step, 1)
                gp.wait_ge(pool_step, gathered + 2 * g + 2)
                gp.sem_inc(gate, 1)
            step.n = gathered + 2 * (RC // 8)
            step.then(nc.gpsimd.tensor_tensor(valid[:, :], on_edge[:, :], apart[:, :], ALU.mult))
            step.then(nc.gpsimd.tensor_copy(scan[:, 0, :], valid[:, :]))
            src, dist = 0, 1
            while dist < RC:
                nc.gpsimd.tensor_copy(scan[:, 1 - src, 0:dist], scan[:, src, 0:dist])
                step.then(nc.gpsimd.tensor_tensor(scan[:, 1 - src, dist:RC], scan[:, src, dist:RC],
                                                  scan[:, src, 0:RC - dist], ALU.add))
                src, dist = 1 - src, 2 * dist
            gp.dma_start(k.tot_d[0:1, 0:RP].rearrange("o p -> p o"), scan[:, src, RC - 1:RC]).then_inc(tot_st, 16)
            gp.wait_ge(tot_st, 16)
            gp.dma_start(tot_row[:, :], k.tot_d[0:1, 0:RP].broadcast_to([RP, RP])).then_inc(tot_ld, 16)
            gp.wait_ge(tot_ld, 16)
            step.then(nc.gpsimd.memset(fold[:, :, :], 0.0))
            nc.gpsimd.tensor_tensor(fold[:, 0, 0:RP], tot_row[:, :], k.before[0:RP, 0:RP], ALU.mult)
            step.then(nc.gpsimd.tensor_copy(fold[:, 1, 0:RP], tot_row[:, :]))
            half = P // 2
            while half:
                step.then(nc.gpsimd.tensor_tensor(fold[:, :, 0:half], fold[:, :, 0:half],
                                                  fold[:, :, half:2 * half], ALU.add))
                half //= 2
            nc.gpsimd.tensor_copy(k.nlist[0:RP, :], fold[:, 1, 0:1])
            step.then(nc.gpsimd.tensor_scalar(pos[:, :], scan[:, src, :], fold[:, 0, 0:1], -1.0 - OFF, ALU.add, ALU.add))
            step.then(nc.gpsimd.tensor_tensor(pos[:, :], pos[:, :], valid[:, :], ALU.mult))
            step.then(nc.gpsimd.tensor_scalar(pos_i[:, :], pos[:, :], OFF, None, ALU.add))
            gp.wait_ge(fills, 16 * (N * F // P // 1024 + 2))
            placed = step.n
            with gp.Fori(0, RC // 8) as g:
                nc.gpsimd.tensor_copy(eight_i[:, :], pos_i[:, bass.ds(8 * g, 8)])
                nc.gpsimd.tensor_copy(eight_f[:, :], key[:, bass.ds(8 * g, 8)]).then_inc(pool_step, 1)
                gp.wait_ge(pool_step, placed + g + 1)
                gp.sem_inc(gate, 1)
                for e in range(8):
                    gp.indirect_dma_start(k.list_d, bass.IndirectOffsetOnAxis(ap=eight_i[:, e:e + 1], axis=0),
                                          eight_f[:, e:e + 1], None,
                                          bounds_check=LIST - 1, oob_is_err=False).then_inc(list_st, 16)
                gp.wait_ge(list_st, 128 * (g + 1))
                gp.sem_inc(gate, 1)
            gp.dma_start(key_row[:, :], k.list_d.rearrange("n o -> o n").broadcast_to([P, LIST])).then_inc(row_ld, 16)
            gp.wait_ge(row_ld, 16)


def listed_tiles(eng, n, tile):
    tile(0)
    with eng.If(n > P):
        with eng.Fori(1, RT) as t:
            with eng.If(n > t * P):
                tile(t)


def decode_tile(nc, dve, step, key_col, got):
    nc.vector.tensor_scalar(got.valid[:, :], key_col[:, :], 0.0, None, ALU.is_ge)
    step.then(nc.vector.tensor_scalar(got.key_i[:, :], key_col[:, :], 0.0, None, ALU.max))
    nc.vector.tensor_single_scalar(got.sub_i[:, :], got.key_i[:, :], N - 1, ALU.bitwise_and)
    step.then(nc.vector.tensor_single_scalar(got.obj_i[:, :], got.key_i[:, :], N.bit_length() - 1,
                                             ALU.arith_shift_right))
    step.then(nc.vector.tensor_copy(got.sub_f[:, :], got.sub_i[:, :]))
    step.then(nc.vector.scalar_tensor_tensor(got.seg[:, :], got.sub_f[:, :], 1.0, got.valid[:, :],
                                             ALU.add, ALU.mult))
    step.then(nc.vector.tensor_scalar(got.seg[:, :], got.seg[:, :], -1.0, None, ALU.add))


def same_segment(nc, dve, step, k, got, seg_row, same, first_i):
    step.then(nc.vector.tensor_scalar(same[:, :], seg_row, got.seg[:, 0:1], None, ALU.is_equal))
    step.then(nc.vector.tensor_tensor(got.earlier[:, :], same[:, :], k.before[:, :], ALU.mult))
    step.then(nc.vector.tensor_reduce(got.count[:, :], got.earlier[:, :], AX, ALU.add))
    step.then(nc.vector.scalar_tensor_tensor(got.count[:, :], got.count[:, :], 0.5, got.valid[:, :],
                                             ALU.is_lt, ALU.mult))
    step.then(nc.vector.scalar_tensor_tensor(got.index_f[:, :], got.sub_f[:, :], -OFF, got.count[:, :],
                                             ALU.add, ALU.mult))
    step.then(nc.vector.tensor_scalar(first_i[:, :], got.index_f[:, :], OFF, None, ALU.add))


def decoded(sb):
    got = Kept()
    got.valid, got.sub_f, got.seg = sb("valid", [P, 1]), sb("sub_f", [P, 1]), sb("seg", [P, 1])
    got.key_i, got.sub_i, got.obj_i = sb("key_i", [P, 1], i32), sb("sub_i", [P, 1], i32), sb("obj_i", [P, 1], i32)
    got.earlier, got.count, got.index_f = sb("earlier", [P, P]), sb("count", [P, 1]), sb("index_f", [P, 1])
    return got


def relation_scores(nc, k, ins, key_row, att_all, weight_all):
    with ExitStack() as ctx:
        sb, ps, sem = stage(nc, ctx, "score")
        got = decoded(sb)
        wq, wk = sb("wq", [P, KF, F]), sb("wk", [P, KF, F])
        bqk = sb("bqk", [1, 2, F])
        key_col = sb("key_col", [P, 1])
        hit = sb("hit", [P, LIST], mybir.dt.bfloat16)
        times, share = sb("times", [P, 1]), sb("share", [P, 1])
        diag, same = sb("diag", [P, P]), sb("same", [P, P])
        first_i = sb("first_i", [P, 1], i32)
        x_sub, x_obj = sb("x_sub", [P, F]), sb("x_obj", [P, F])
        xt_sub, xt_obj = sb("xt_sub", [P, F]), sb("xt_obj", [P, F])
        q_sb, qk = sb("q_sb", [P, F]), sb("qk", [P, F])
        att = sb("att", [P, H])
        att_diag = sb("att_diag", [P, H, P])
        away = sb("away", [P, P])
        seg_att = sb("seg_att", [P, H, P])
        old, new = sb("old", [P, SR]), sb("new", [P, SR])
        drop, ex = sb("drop", [P, 2, H]), sb("ex", [P, 2, H])
        terms = sb("terms", [P, H + 1])
        ps_seg, ps_xs, ps_xo = ps("ps_seg", [P, F]), ps("ps_xs", [P, F]), ps("ps_xo", [P, F])
        ps_q, ps_k, ps_att = ps("ps_q", [P, F]), ps("ps_k", [P, F]), ps("ps_att", [P, 2, F])

        w_ld, key_ld, tile_done, gath_ld, new_st = (sem("w_ld"), sem("key_ld"), sem("tile_done"), sem("gath_ld"),
                                                    sem("new_st"))
        diag_ready, seg_ready, turned, turned_sb = (sem("diag_ready"), sem("seg_ready"), sem("turned"),
                                                    sem("turned_sb"))
        qk_ready, q_copied, attd_ready, att_spread = (sem("qk_ready"), sem("q_copied"), sem("attd_ready"),
                                                      sem("att_spread"))
        drop_ready, ex_ready, terms_ready, sums_ready, new_ready = (sem("drop_ready"), sem("ex_ready"),
                                                                    sem("terms_ready"), sem("sums_ready"),
                                                                    sem("new_ready"))
        dve_step, gate, blanks = sem("dve_step"), sem("gate"), sem("blanks")
        LINKS = 24
        block = ctx.enter_context(nc.Block())

        @block.sync
        def _(sp):
            sp.dma_start(wq[:, :, :], tiles_of(ins["wq_t"])).then_inc(w_ld, 16)
            sp.dma_start(wk[:, :, :], tiles_of(ins["wk_t"])).then_inc(w_ld, 16)
            sp.dma_start(bqk[:, 0, :], ins["bq"]).then_inc(w_ld, 16)
            sp.dma_start(bqk[:, 1, :], ins["bk"]).then_inc(w_ld, 16)
            sp.wait_ge(w_ld, 64)
            n = sp.value_load(k.nlist[0:1, 0:1], min_val=0, max_val=RP * RC)
            def tile(t):
                sp.wait_ge(tile_done, t + 1)
                sp.sem_inc(gate, 1)
                sp.dma_start(key_col[:, :], k.list_d[bass.ds(t * P, P), :]).then_inc(key_ld, 16)

            listed_tiles(sp, n, tile)

        @block.vector
        def _(dve):
            nc.vector.memset(new[:, :], 0.0).then_inc(blanks, 1)
            dve.wait_ge(blanks, 1)
            n = dve.value_load(k.nlist[0:1, 0:1], min_val=0, max_val=RP * RC)
            def tile(t):
                step = Chain(dve, dve_step, t * LINKS)
                dve.wait_ge(key_ld, 16 * (t + 1))
                decode_tile(nc, dve, step, key_col, got)
                nc.vector.tensor_scalar(diag[:, :], k.ident[:, :], got.seg[:, 0:1], None,
                                        ALU.mult).then_inc(diag_ready, 1)
                step.then(nc.vector.tensor_scalar(hit[:, :], key_row[:, :], key_col[:, 0:1], 0.0,
                                                  ALU.is_equal, ALU.add, accum_out=times[:, :]))
                step.then(nc.vector.tensor_scalar(times[:, :], times[:, :], 1.0, None, ALU.max))
                step.then(nc.vector.reciprocal(share[:, :], times[:, :]))
                step.then(nc.vector.tensor_tensor(terms[:, H:H + 1], share[:, :], got.valid[:, :], ALU.mult))
                nc.vector.tensor_copy(weight_all[:, bass.ds(t, 1)], terms[:, H:H + 1])
                dve.wait_ge(seg_ready, t + 1)
                same_segment(nc, dve, step, k, got, ps_seg[:, 0:P], same, first_i)
                step.then(nc.vector.tensor_scalar(away[:, :], same[:, :], BIG, -BIG, ALU.mult, ALU.add))
                dve.wait_ge(q_copied, t + 1)
                step.then(nc.vector.tensor_tensor(qk[:, :], q_sb[:, :], ps_k[:, :], ALU.mult))
                step.then(nc.vector.tensor_reduce(att[:, :], qk[:, :].rearrange("p (h d) -> p h d", d=DH),
                                                  AX, ALU.add))
                step.then(nc.vector.tensor_scalar(att[:, :], att[:, :], DH ** -0.5, None, ALU.mult))
                nc.vector.tensor_scalar(att_all[:, bass.ds(t * H, H)], att[:, :], got.valid[:, 0:1], None,
                                        ALU.mult)
                nc.vector.tensor_tensor(att_diag[:, :, :], k.ident[:, :].unsqueeze(1).broadcast_to([P, H, P]),
                                        att[:, :].unsqueeze(2).broadcast_to([P, H, P]),
                                        ALU.mult).then_inc(attd_ready, 1)
                dve.wait_ge(att_spread, t + 1)
                step.then(nc.vector.tensor_tensor(seg_att[:, :, :],
                                                  ps_att[:, :, :].rearrange("p b (h f) -> p (b h) f", f=P),
                                                  away[:, :].unsqueeze(1).broadcast_to([P, H, P]), ALU.add))
                step.then(nc.vector.tensor_reduce(drop[:, 0, :], seg_att[:, :, :], AX, ALU.max))
                step.then(nc.vector.tensor_tensor(new[:, 0:H], drop[:, 0, :], old[:, 0:H], ALU.max))
                nc.vector.tensor_tensor(drop[:, 0, :], old[:, 0:H], new[:, 0:H], ALU.subtract)
                nc.vector.tensor_tensor(drop[:, 1, :], att[:, :], new[:, 0:H], ALU.subtract).then_inc(drop_ready, 1)
                dve.wait_ge(ex_ready, t + 1)
                nc.vector.tensor_scalar(terms[:, 0:H], ex[:, 1, :], terms[:, H:H + 1], None,
                                        ALU.mult).then_inc(terms_ready, 1)
                step.then(nc.vector.tensor_tensor(new[:, H:2 * H], old[:, H:2 * H], ex[:, 0, :], ALU.mult))
                dve.wait_ge(sums_ready, t + 1)
                nc.vector.tensor_tensor(new[:, H:2 * H], new[:, H:2 * H], ps_seg[:, P:P + H], ALU.add)
                last = nc.vector.tensor_tensor(new[:, 2 * H:2 * H + 1], old[:, 2 * H:2 * H + 1],
                                               ps_seg[:, P + H:P + H + 1], ALU.add)
                step.then(last)
                nc.vector.tensor_copy(got.count[:, :], got.valid[:, :]).then_inc(new_ready, 1)
                assert step.n == LINKS, step.n

            listed_tiles(dve, n, tile)

        @block.tensor
        def _(pe):
            pe.wait_ge(w_ld, 64)
            n = pe.value_load(k.nlist[0:1, 0:1], min_val=0, max_val=RP * RC)
            def tile(t):
                pe.wait_ge(diag_ready, t + 1)
                nc.tensor.matmul(ps_seg[:, 0:P], k.ones[:, :], diag[:, :], start=True,
                                 stop=True).then_inc(seg_ready, 1)
                pe.wait_ge(gath_ld, 48 * (t + 1))
                for x_rows, turned_ps in ((x_sub, ps_xs), (x_obj, ps_xo)):
                    for f in range(KF):
                        last = nc.tensor.transpose(turned_ps[:, P * f:P * (f + 1)], x_rows[:, P * f:P * (f + 1)],
                                                   k.ident[:, :])
                last.then_inc(turned, 1)
                pe.wait_ge(turned_sb, 2 * (t + 1))
                for xt, wt, out, b in ((xt_sub, wq, ps_q, 0), (xt_obj, wk, ps_k, 1)):
                    for f in range(KF):
                        nc.tensor.matmul(out[:, :], xt[:, P * f:P * (f + 1)], wt[:, f, :], start=(f == 0),
                                         stop=False)
                    last = nc.tensor.matmul(out[:, :], k.ones[0:1, :], bqk[0:1, b, :], start=False, stop=True)
                last.then_inc(qk_ready, 1)
                pe.wait_ge(attd_ready, t + 1)
                for b in range(2):
                    last = nc.tensor.matmul(ps_att[:, b, :], k.ones[:, :],
                                            att_diag[:, 4 * b:4 * (b + 1), :].rearrange("p h f -> p (h f)"),
                                            start=True, stop=True)
                last.then_inc(att_spread, 1)
                pe.wait_ge(terms_ready, t + 1)
                nc.tensor.matmul(ps_seg[:, P:P + H + 1], same[:, :], terms[:, :], start=True,
                                 stop=True).then_inc(sums_ready, 1)

            listed_tiles(pe, n, tile)

        @block.scalar
        def _(act):
            act.wait_ge(blanks, 1)
            n = act.value_load(k.nlist[0:1, 0:1], min_val=0, max_val=RP * RC)
            def tile(t):
                act.wait_ge(turned, t + 1)
                nc.scalar.copy(xt_sub[:, :], ps_xs[:, :]).then_inc(turned_sb, 1)
                nc.scalar.copy(xt_obj[:, :], ps_xo[:, :]).then_inc(turned_sb, 1)
                act.wait_ge(qk_ready, t + 1)
                nc.scalar.copy(q_sb[:, :], ps_q[:, :]).then_inc(q_copied, 1)
                act.wait_ge(drop_ready, t + 1)
                nc.scalar.activation(ex[:, :, :], drop[:, :, :], ACT.Exp).then_inc(ex_ready, 1)

            listed_tiles(act, n, tile)

        @block.gpsimd
        def _(gp):
            gp.sem_inc(tile_done, 1)
            n = gp.value_load(k.nlist[0:1, 0:1], min_val=0, max_val=RP * RC)
            def tile(t):
                gp.wait_ge(seg_ready, t + 1)
                gp.sem_inc(gate, 1)
                for rows, table, bound, index in ((x_sub, ins["x"], N - 1, got.sub_i),
                                                  (x_obj, ins["x"], N - 1, got.obj_i),
                                                  (old, k.stats_d, N - 1, got.sub_i)):
                    gp.indirect_dma_start(rows[:, :], None, table, bass.IndirectOffsetOnAxis(ap=index[:, 0:1], axis=0),
                                          bounds_check=bound, oob_is_err=False).then_inc(gath_ld, 16)
                gp.wait_ge(new_ready, t + 1)
                gp.sem_inc(gate, 1)
                gp.indirect_dma_start(k.stats_d, bass.IndirectOffsetOnAxis(ap=first_i[:, 0:1], axis=0), new[:, :],
                                      None, bounds_check=N - 1, oob_is_err=False).then_inc(new_st, 16)
                gp.wait_ge(new_st, 16 * (t + 1))
                gp.sem_inc(tile_done, 1)

            listed_tiles(gp, n, tile)


def node_coefficients(nc, k, ins, c_all, cx_all):
    with ExitStack() as ctx:
        sb, ps, sem = stage(nc, ctx, "coef")
        stats = sb("stats", [P, NT, SR])
        loop = sb("loop", [P, NT])
        ex0, exd = sb("ex0", [P, NT, H]), sb("exd", [P, NT, H])
        others = sb("others", [P, NT])
        z, prod, prod_d = sb("z", [P, NT, H]), sb("prod", [P, NT, H]), sb("prod_d", [P, NT, H])
        cd = sb("cd", [P, NT])
        rows = sb("rows", [P, NT, CR])
        diag_bias = sb("diag_bias", [P, 1])
        st_ld, loop_ld, rows_st = sem("st_ld"), sem("loop_ld"), sem("rows_st")
        dve_step, ex_ready, bias_ready, rows_ready = sem("dve_step"), sem("ex_ready"), sem("bias_ready"), sem("rows_ready")
        block = ctx.enter_context(nc.Block())

        @block.sync
        def _(sp):
            sp.dma_start(stats[:, :, :], tiles_of(k.stats_d)).then_inc(st_ld, 16)
            sp.dma_start(loop[:, :], ins["adj_diag"]).then_inc(loop_ld, 16)
            sp.wait_ge(rows_ready, 1)
            sp.dma_start(tiles_of(k.coef_d), rows[:, :, :]).then_inc(rows_st, 16)
            sp.dma_start(k.empty_d.rearrange("(t p) o -> p (t o)", p=P), k.empty[:, :],
                         allow_slow_non_contiguous=True).then_inc(k.empty_st, 16)
            sp.wait_ge(rows_st, 16)

        @block.scalar
        def _(act):
            act.wait_ge(st_ld, 16)
            act.wait_ge(bias_ready, 1)
            nc.scalar.activation(ex0[:, :, :], stats[:, :, 0:H], ACT.Exp, scale=-1.0)
            nc.scalar.activation(exd[:, :, :], stats[:, :, 0:H], ACT.Exp, scale=-1.0,
                                 bias=diag_bias[:, 0:1]).then_inc(ex_ready, 1)

        @block.vector
        def _(dve):
            step = Chain(dve, dve_step)
            nc.vector.memset(diag_bias[:, :], DIAG).then_inc(bias_ready, 1)
            nc.vector.tensor_scalar(k.empty[:, :], k.deg[:, :], 0.0, None, ALU.is_equal)
            dve.wait_ge(loop_ld, 16)
            step.then(nc.vector.tensor_tensor(others[:, :], k.deg[:, :], loop[:, :], ALU.subtract))
            dve.wait_ge(st_ld, 16)
            step.then(nc.vector.tensor_tensor(others[:, :], others[:, :], stats[:, :, 2 * H], ALU.subtract))
            dve.wait_ge(ex_ready, 1)
            step.then(nc.vector.tensor_tensor(z[:, :, :], ex0[:, :, :],
                                              others[:, :].unsqueeze(2).broadcast_to([P, NT, H]), ALU.mult))
            step.then(nc.vector.tensor_tensor(z[:, :, :], z[:, :, :], exd[:, :, :], ALU.add))
            step.then(nc.vector.tensor_tensor(z[:, :, :], z[:, :, :], stats[:, :, H:2 * H], ALU.add))
            step.then(nc.vector.tensor_scalar(z[:, :, :], z[:, :, :], float(H), None, ALU.mult))
            step.then(nc.vector.reciprocal(rows[:, :, H:2 * H], z[:, :, :]))
            nc.vector.tensor_copy(rows[:, :, 0:H], stats[:, :, 0:H]).then_inc(rows_ready, 1)
            nc.vector.tensor_tensor(prod[:, :, :], ex0[:, :, :], rows[:, :, H:2 * H], ALU.mult)
            step.then(nc.vector.tensor_tensor(prod_d[:, :, :], exd[:, :, :], rows[:, :, H:2 * H], ALU.mult))
            nc.vector.tensor_reduce(c_all[:, :], prod[:, :, :], AX, ALU.add)
            step.then(nc.vector.tensor_reduce(cd[:, :], prod_d[:, :, :], AX, ALU.add))
            step.then(nc.vector.tensor_tensor(cx_all[:, :], c_all[:, :], loop[:, :], ALU.mult))
            step.then(nc.vector.tensor_tensor(cx_all[:, :], cd[:, :], cx_all[:, :], ALU.subtract))
            step.then(nc.vector.tensor_scalar(cx_all[:, :], cx_all[:, :], 1.0, None, ALU.add))


def relation_values(nc, k, ins, att_all, weight_all):
    with ExitStack() as ctx:
        sb, ps, sem = stage(nc, ctx, "value")
        got = decoded(sb)
        key_col = sb("key_col", [P, 1])
        diag, same = sb("diag", [P, P]), sb("same", [P, P])
        first_i = sb("first_i", [P, 1], i32)
        x_obj, rel_old, rel_new = sb("x_obj", [P, F]), sb("rel_old", [P, F]), sb("rel_new", [P, F])
        coef = sb("coef", [P, CR])
        drop, ex = sb("drop", [P, 2, H]), sb("ex", [P, 2, H])
        rise, weight = sb("rise", [P, H]), sb("weight", [P, 1])
        value = sb("value", [P, F])
        ps_seg = ps("ps_seg", [P, F])
        ps_val = ps("ps_val", [P, F])
        key_ld, tile_done, gath_ld, new_st = sem("key_ld"), sem("tile_done"), sem("gath_ld"), sem("new_st")
        diag_ready, seg_ready, drop_ready, ex_ready = (sem("diag_ready"), sem("seg_ready"), sem("drop_ready"),
                                                       sem("ex_ready"))
        value_ready, val_summed, new_ready = sem("value_ready"), sem("val_summed"), sem("new_ready")
        dve_step, gate = sem("dve_step"), sem("gate")
        LINKS = 16
        block = ctx.enter_context(nc.Block())

        @block.sync
        def _(sp):
            n = sp.value_load(k.nlist[0:1, 0:1], min_val=0, max_val=RP * RC)
            def tile(t):
                sp.wait_ge(tile_done, t + 1)
                sp.sem_inc(gate, 1)
                sp.dma_start(key_col[:, :], k.list_d[bass.ds(t * P, P), :]).then_inc(key_ld, 16)

            listed_tiles(sp, n, tile)

        @block.vector
        def _(dve):
            n = dve.value_load(k.nlist[0:1, 0:1], min_val=0, max_val=RP * RC)
            def tile(t):
                step = Chain(dve, dve_step, t * LINKS)
                dve.wait_ge(key_ld, 16 * (t + 1))
                decode_tile(nc, dve, step, key_col, got)
                nc.vector.tensor_scalar(diag[:, :], k.ident[:, :], got.seg[:, 0:1], None,
                                        ALU.mult).then_inc(diag_ready, 1)
                dve.wait_ge(gath_ld, 48 * (t + 1))
                nc.vector.tensor_tensor(drop[:, 0, :], att_all[:, bass.ds(t * H, H)], coef[:, 0:H], ALU.subtract)
                nc.vector.tensor_scalar(drop[:, 1, :], coef[:, 0:H], -1.0, None,
                                        ALU.mult).then_inc(drop_ready, 1)
                dve.wait_ge(seg_ready, t + 1)
                same_segment(nc, dve, step, k, got, ps_seg[:, 0:P], same, first_i)
                dve.wait_ge(ex_ready, t + 1)
                step.then(nc.vector.tensor_tensor(rise[:, :], ex[:, 0, :], ex[:, 1, :], ALU.subtract))
                step.then(nc.vector.tensor_tensor(rise[:, :], rise[:, :], coef[:, H:2 * H], ALU.mult))
                step.then(nc.vector.tensor_reduce(weight[:, :], rise[:, :], AX, ALU.add))
                step.then(nc.vector.tensor_tensor(weight[:, :], weight[:, :], weight_all[:, bass.ds(t, 1)],
                                                  ALU.mult))
                nc.vector.tensor_scalar(value[:, :], x_obj[:, :], weight[:, 0:1], None,
                                        ALU.mult).then_inc(value_ready, 1)
                dve.wait_ge(val_summed, t + 1)
                step.then(nc.vector.tensor_tensor(rel_new[:, :], rel_old[:, :], ps_val[:, :], ALU.add))
                nc.vector.tensor_copy(got.count[:, :], got.valid[:, :]).then_inc(new_ready, 1)
                assert step.n == LINKS, step.n

            listed_tiles(dve, n, tile)

        @block.tensor
        def _(pe):
            n = pe.value_load(k.nlist[0:1, 0:1], min_val=0, max_val=RP * RC)
            def tile(t):
                pe.wait_ge(diag_ready, t + 1)
                nc.tensor.matmul(ps_seg[:, 0:P], k.ones[:, :], diag[:, :], start=True,
                                 stop=True).then_inc(seg_ready, 1)
                pe.wait_ge(value_ready, t + 1)
                nc.tensor.matmul(ps_val[:, :], same[:, :], value[:, :], start=True,
                                 stop=True).then_inc(val_summed, 1)

            listed_tiles(pe, n, tile)

        @block.scalar
        def _(act):
            n = act.value_load(k.nlist[0:1, 0:1], min_val=0, max_val=RP * RC)
            def tile(t):
                act.wait_ge(drop_ready, t + 1)
                nc.scalar.activation(ex[:, :, :], drop[:, :, :], ACT.Exp).then_inc(ex_ready, 1)

            listed_tiles(act, n, tile)

        @block.gpsimd
        def _(gp):
            gp.sem_inc(tile_done, 1)
            n = gp.value_load(k.nlist[0:1, 0:1], min_val=0, max_val=RP * RC)
            def tile(t):
                gp.wait_ge(diag_ready, t + 1)
                gp.sem_inc(gate, 1)
                for rows, table, index in ((coef, k.coef_d, got.sub_i), (x_obj, ins["x"], got.obj_i),
                                           (rel_old, k.rel_d, got.sub_i)):
                    gp.indirect_dma_start(rows[:, :], None, table, bass.IndirectOffsetOnAxis(ap=index[:, 0:1], axis=0),
                                          bounds_check=N - 1, oob_is_err=False).then_inc(gath_ld, 16)
                gp.wait_ge(new_ready, t + 1)
                gp.sem_inc(gate, 1)
                gp.indirect_dma_start(k.rel_d, bass.IndirectOffsetOnAxis(ap=first_i[:, 0:1], axis=0), rel_new[:, :],
                                      None, bounds_check=N - 1, oob_is_err=False).then_inc(new_st, 16)
                gp.wait_ge(new_st, 16 * (t + 1))
                gp.sem_inc(tile_done, 1)

            listed_tiles(gp, n, tile)


def source_index(nc, k, ins, ls):
    with ExitStack() as ctx:
        sb, ps, sem = stage(nc, ctx, "index")
        upto = sb("upto", [P, P], f16)
        cum = sb("cum", [NT, NS, P])
        cnt, cnt16 = sb("cnt", [NT, NS]), sb("cnt16", [NT, NS], f16)
        excl = sb("excl", [NT, NS])
        one16 = sb("one16", [NT, P], f16)
        slot_i, sec_i = sb("slot_i", [P, NT], i32), sb("sec_i", [P, NS], i32)
        span = sb("span", [P, 2, NS])
        alone_sum = sb("alone_sum", [P, 1])
        ps_lone, alone_ready = ps("ps_lone", [P, F]), sem("alone_ready")
        rounded = sb("rounded", [TR, NS, P], f16)
        groups_i = sb("groups_i", [P, NS], i32)
        groups_f = sb("groups_f", [P, NS])
        ps_cum, ps_cnt = ps("ps_cum", [P, NS * P]), ps("ps_cnt", [P, 2, F])
        up_ready, cum_ps, cnt_ready, cnt_ps, sum_ready, diff_ps = (
            sem("up_ready"), sem("cum_ps"), sem("cnt_ready"), sem("cnt_ps"), sem("sum_ready"), sem("diff_ps"))
        iotas, dve_step, const_ld = sem("iotas"), sem("dve_step"), sem("const_ld")
        block = ctx.enter_context(nc.Block())

        @block.gpsimd
        def _(gp):
            nc.gpsimd.iota(slot_i[:, :], [[P, NT]], base=0, channel_multiplier=1)
            nc.gpsimd.iota(sec_i[:, :], [[1, NS]], base=0, channel_multiplier=0).then_inc(iotas, 1)

        @block.sync
        def _(sp):
            sp.dma_start(ls.differ[:, :], ins["differ"]).then_inc(const_ld, 16)
            sp.dma_start(ls.tile_step[:, :], ins["tile_step"]).then_inc(const_ld, 16)
            sp.wait_ge(const_ld, 32)

        @block.tensor
        def _(pe):
            pe.wait_ge(alone_ready, 1)
            nc.tensor.matmul(ps_lone[0:1, 0:1], alone_sum[:, :], k.ones[:, 0:1], start=True, stop=True)
            pe.wait_ge(up_ready, 1)
            for s in range(NS):
                last = nc.tensor.matmul(ps_cum[0:NT, P * s:P * (s + 1)], k.marks[:, s, :], upto[:, :],
                                        start=True, stop=True)
            last.then_inc(cum_ps, 1)
            pe.wait_ge(cnt_ready, 1)
            nc.tensor.matmul(ps_cnt[0:NT, 0, 0:NS], upto[0:NT, 0:NT], cnt16[:, :], start=True, stop=True)
            nc.tensor.matmul(ps_cnt[:, 1, 0:NS], one16[:, :], cnt16[:, :], start=True, stop=True).then_inc(cnt_ps, 1)
            pe.wait_ge(sum_ready, 1)
            pe.wait_ge(const_ld, 32)
            for a in range(4):
                last = nc.tensor.matmul(ps_cum[0:TR, F * a:F * (a + 1)], ls.differ[:, :],
                                        cum[:, 4 * a:4 * (a + 1), :].rearrange("t s p -> t (s p)"),
                                        start=True, stop=True)
            last.then_inc(diff_ps, 1)

        @block.vector
        def _(dve):
            step = Chain(dve, dve_step)
            nc.vector.memset(one16[:, :], 1.0)
            nc.vector.tensor_reduce(alone_sum[:, :], k.empty[:, :], AX, ALU.add).then_inc(alone_ready, 1)
            nc.vector.memset(ls.node[:, :, :], float(P))
            nc.vector.memset(ls.tile_node[:, :, :], float(N - P))
            nc.vector.tensor_scalar(upto[:, :], k.before[:, :], -1.0, 1.0, ALU.mult, ALU.add).then_inc(up_ready, 1)
            dve.wait_ge(iotas, 1)
            nc.vector.tensor_copy(ls.slot[:, :], slot_i[:, :])
            nc.vector.tensor_copy(ls.sec_no[:, :], sec_i[:, :])
            dve.wait_ge(cum_ps, 1)
            sums = ps_cum[0:NT, :].rearrange("t (s p) -> t s p", p=P)
            nc.vector.tensor_copy(cnt16[:, :], sums[:, :, P - 1]).then_inc(cnt_ready, 1)
            step.then(nc.vector.tensor_copy(cnt[:, :], sums[:, :, P - 1]))
            nc.vector.tensor_copy(k.lonely[:, :], ps_lone[0:1, 0:1])
            dve.wait_ge(cnt_ps, 1)
            step.then(nc.vector.tensor_tensor(excl[:, :], ps_cnt[0:NT, 0, 0:NS], cnt[:, :], ALU.subtract))
            nc.vector.tensor_scalar(ls.lead[:, :], excl[:, :], -1.0, 0.5, ALU.mult, ALU.add)
            nc.vector.tensor_tensor(cum[:, :, :], sums, excl[:, :].unsqueeze(2).broadcast_to([NT, NS, P]),
                                    ALU.add).then_inc(sum_ready, 1)
            step.then(nc.vector.tensor_scalar(groups_i[:, :], ps_cnt[:, 1, 0:NS], float(GT * P - 1), None, ALU.add))
            step.then(nc.vector.tensor_single_scalar(groups_i[:, :], groups_i[:, :], (GT * P).bit_length() - 1,
                                                     ALU.arith_shift_right))
            step.then(nc.vector.tensor_scalar(groups_f[:, :], groups_i[:, :], float(MG), None, ALU.max))
            step.then(nc.vector.tensor_copy(span[:, 0, :], groups_f[:, :]))
            src, dist = 0, 1
            while dist < NS:
                nc.vector.tensor_copy(span[:, 1 - src, 0:dist], span[:, src, 0:dist])
                step.then(nc.vector.tensor_tensor(span[:, 1 - src, dist:NS], span[:, src, dist:NS],
                                                  span[:, src, 0:NS - dist], ALU.add))
                src, dist = 1 - src, 2 * dist
            step.then(nc.vector.tensor_tensor(span[:, src, :], span[:, src, :], groups_f[:, :], ALU.subtract))
            nc.vector.scalar_tensor_tensor(k.groups[:, :], span[:, src, :], float(PACK), groups_f[:, :],
                                           ALU.mult, ALU.add)
            dve.wait_ge(diff_ps, 1)
            halves = ps_cum[0:TR, :].rearrange("t (s p) -> t s p", p=P)
            step.then(nc.vector.tensor_copy(rounded[:, :, :], halves))
            dve.wait_ge(const_ld, 32)
            nc.vector.scalar_tensor_tensor(ls.steps[:, :, 0:P], rounded[:, :, :], ls.tile_step[:, 1:2], halves,
                                           ALU.mult, ALU.add)
            nc.vector.tensor_copy(ls.steps[:, :, P], ls.tile_step[:, 0:1].broadcast_to([TR, NS]))


def section_groups(eng, k, s, group):
    both = eng.value_load(k.groups[0:1, bass.ds(s, 1)], min_val=MG, max_val=(NS - 1) * NT // GT * PACK + NT // GT)
    n = eng.snap(both % PACK, min_val=MG, max_val=NT // GT)
    first = eng.snap(both // PACK, min_val=0, max_val=(NS - 1) * NT // GT)
    for q in range(MG):
        group(q, first + q)
    with eng.If(n > MG):
        with eng.Fori(MG, NT // GT) as q:
            with eng.If(n > q):
                group(q, first + q)


def source_lists(nc, k, ls):
    with ExitStack() as ctx:
        sb, ps, sem = stage(nc, ctx, "list")
        begun = sb("begun", [TR, GT, P], f16)
        hit = sb("hit", [P, GT, P])
        found = sb("found", [P, GT])
        ps_row = [ps(f"ps_row{b}", [P, P + 1]) for b in range(GT)]
        begun_ready, chosen, counted = sem("begun_ready"), sem("chosen"), sem("counted")
        ones_ready, dve_step, gate = sem("ones_ready"), sem("dve_step"), sem("gate")
        found_kept = sem("found_kept")
        block = ctx.enter_context(nc.Block())

        @block.sync
        def _(sp):
            sp.wait_ge(k.rows_st, 16 * PIECES)

        @block.scalar
        def _(act):
            with act.Fori(0, NS) as s:
                def begin(q, g):
                    for b in range(GT):
                        act.wait_ge(chosen, GT * g + b + 1)
                        act.sem_inc(gate, 1)
                        nc.scalar.activation(begun[0:NT, b, :], ls.slot_row[:, bass.ds(q * GT * P + b * P, P)],
                                             ACT.Sign, bias=ls.lead[:, bass.ds(s, 1)]).then_inc(begun_ready, 1)

                section_groups(act, k, s, begin)

        @block.tensor
        def _(pe):
            pe.sem_inc(chosen, GT)
            pe.wait_ge(ones_ready, 1)
            with pe.Fori(0, NS) as s:
                def choose(q, g):
                    for b in range(GT):
                        pe.wait_ge(begun_ready, GT * g + b + 1)
                        pe.wait_ge(counted, GT * g + b + 1)
                        pe.sem_inc(gate, 1)
                        nc.tensor.matmul(ps_row[b][:, :], begun[:, b, :],
                                         ls.steps[:, bass.ds(s, 1), :].rearrange("t o p -> t (o p)"),
                                         start=True, stop=True).then_inc(chosen, 1)

                section_groups(pe, k, s, choose)

        @block.vector
        def _(dve):
            nc.vector.memset(begun[NT:TR, :, :], 1.0).then_inc(ones_ready, 1)
            dve.sem_inc(counted, GT)
            dve.sem_inc(found_kept, 1)
            with dve.Fori(0, NS) as s:
                def count(q, g):
                    dve.wait_ge(found_kept, g + 1)
                    for b in range(GT):
                        m = q * GT + b
                        dve.wait_ge(chosen, GT * g + b + 1 + GT)
                        nc.vector.tensor_scalar(hit[:, b, :], ps_row[b][:, 0:P], ls.slot[:, bass.ds(m, 1)], 0.0,
                                                ALU.is_le, ALU.add, accum_out=found[:, b:b + 1]).then_inc(dve_step, 1)
                        nc.vector.tensor_copy(ls.tile_node[:, bass.ds(s, 1), bass.ds(m, 1)]
                                              .rearrange("p o t -> p (o t)"), ps_row[b][:, P:P + 1]).then_inc(counted, 1)
                    dve.wait_ge(dve_step, GT * (g + 1))
                    nc.vector.tensor_copy(ls.node[:, bass.ds(s, 1), bass.ds(q * GT, GT)]
                                          .rearrange("p o t -> p (o t)"), found[:, :]).then_inc(found_kept, 1)

                section_groups(dve, k, s, count)


def list_rows(nc, k, ls):
    with ExitStack() as ctx:
        sb, ps, sem = stage(nc, ctx, "rows")
        dve_step = sem("dve_step")
        block = ctx.enter_context(nc.Block())

        @block.vector
        def _(dve):
            step = Chain(dve, dve_step)
            step.then(nc.vector.tensor_tensor(ls.node[:, :, :], ls.node[:, :, :], ls.tile_node[:, :, :], ALU.add))
            nc.vector.tensor_copy(k.index[:, :, :, 0], ls.node[:, :, :])
            step.then(nc.vector.scalar_tensor_tensor(ls.node[:, :, :], ls.node[:, :, :], float(NS),
                                                     ls.sec_no[:, :].unsqueeze(2).broadcast_to([P, NS, NT]),
                                                     ALU.mult, ALU.add))
            nc.vector.tensor_scalar(k.index[:, :, :, 1], ls.node[:, :, :], float(N * NS - 1), None, ALU.min)


class Lists:
    pass


def make_lists(sb):
    ls = Lists()
    ls.differ = sb("lists_differ", [NT, TR])
    ls.tile_step = sb("lists_tile_step", [TR, 2])
    ls.steps = sb("lists_steps", [TR, NS, P + 1], f16)
    ls.lead = sb("lists_lead", [NT, NS])
    ls.slot = sb("lists_slot", [P, NT])
    ls.slot_row = sb("lists_slot_row", [NT, N])
    ls.sec_no = sb("lists_sec_no", [P, NS])
    ls.node = sb("lists_node", [P, NS, NT])
    ls.tile_node = sb("lists_tile_node", [P, NS, NT])
    return ls


def project_nodes(nc, k, ins, c_all, cx_all, row_all, sd_all, s_row, x_sum):
    with ExitStack() as ctx:
        sb, ps, sem = stage(nc, ctx, "node")
        parts = sb("parts", [P, 2, 3, F])
        mixed = sb("mixed", [P, 2, F])
        x1 = sb("x1", [P, 2, F])
        x1_t = sb("x1_t", [P, 2, F])
        seen = sb("seen", [P, 2, 6])
        moments = sb("moments", [P, 2, 2])
        rstd, minus_half = sb("rstd", [P, 2]), sb("minus_half", [P, 1])
        ps_turn = [ps(f"ps_turn{b}", [P, F]) for b in range(2)]
        ps_wh = [ps(f"ps_wh{b}", [P, F]) for b in range(2)]
        ps_sd = [ps(f"ps_sd{b}", [P, F]) for b in range(2)]
        ps_srow = [ps(f"ps_srow{b}", [P, F]) for b in range(2)]
        part_ld = [sem(f"part_ld{b}") for b in range(2)]
        x1_st = [sem(f"x1_st{b}") for b in range(2)]
        parts_used, x1_ready, x1_summed = sem("parts_used"), sem("x1_ready"), sem("x1_summed")
        turned, turned_sb, projected, copied = sem("turned"), sem("turned_sb"), sem("projected"), sem("copied")
        dve_step, gate, pool_step = sem("dve_step"), sem("gate"), sem("pool_step")
        moments_ready, rstd_ready = sem("moments_ready"), sem("rstd_ready")
        LINKS = 3
        block = ctx.enter_context(nc.Block())

        @block.sync
        def _(sp):
            sp.sem_inc(x1_st[0], 16)
            sp.sem_inc(x1_st[1], 16)

            def load(t, b):
                sp.wait_ge(parts_used, t + 1)
                sp.sem_inc(gate, 1)
                for i, table in enumerate((k.agg_d, ins["x"], k.rel_d)):
                    sp.dma_start(parts[:, b, i, :], table[bass.ds(t * P, P), :]).then_inc(part_ld[b], 16)

            def store(t, b):
                sp.wait_ge(x1_ready, t + 1)
                sp.sem_inc(gate, 1)
                sp.dma_start(k.x1_d[bass.ds(t * P, P), :], x1[:, b, :]).then_inc(x1_st[b], 16)

            load(0, 0)
            load(1, 1)
            with sp.Fori(0, NT // 2 - 1) as pair:
                for b in range(2):
                    load(2 * pair + b + 2, b)
                    store(2 * pair + b, b)
            for b in range(2):
                store(NT - 2 + b, b)
            for b in range(2):
                sp.wait_ge(x1_st[b], 16 * (NT // 2 + 1))
            sp.wait_ge(k.empty_st, 16)

        @block.vector
        def _(dve):
            dve.sem_inc(parts_used, 2)
            with dve.Fori(0, NT // 2) as pair:
                for b in range(2):
                    t = 2 * pair + b
                    step = Chain(dve, dve_step, t * LINKS)
                    dve.wait_ge(part_ld[b], 48 * (pair + 1))
                    step.then(nc.vector.scalar_tensor_tensor(mixed[:, b, :], parts[:, b, 0, :],
                                                             c_all[:, bass.ds(t, 1)], parts[:, b, 2, :],
                                                             ALU.mult, ALU.add))
                    step.then(nc.vector.scalar_tensor_tensor(mixed[:, b, :], parts[:, b, 1, :],
                                                             cx_all[:, bass.ds(t, 1)], mixed[:, b, :],
                                                             ALU.mult, ALU.add))
                    step.then(nc.vector.bn_stats(seen[:, b, :], mixed[:, b, :]))
                    dve.sem_inc(parts_used, 1)
                    nc.vector.bn_aggr(moments[:, b, :], seen[:, b, :]).then_inc(moments_ready, 1)
                    dve.wait_ge(rstd_ready, t + 1)
                    dve.wait_ge(x1_st[b], 16 * (pair + 1))
                    dve.wait_ge(turned, t + 1)
                    dve.wait_ge(x1_summed, t + 1)
                    nc.vector.tensor_scalar(x1[:, b, :], mixed[:, b, :], moments[:, b, 0:1], rstd[:, b:b + 1],
                                            ALU.subtract, ALU.mult).then_inc(x1_ready, 1)
                    assert step.n == LINKS

        @block.gpsimd
        def _(gp):
            gp.sem_inc(x1_summed, 2)
            nc.gpsimd.memset(minus_half[:, :], -0.5)
            nc.gpsimd.memset(x_sum[:, :], 0.0).then_inc(pool_step, 1)
            gp.wait_ge(pool_step, 1)
            with gp.Fori(0, NT // 2) as pair:
                for b in range(2):
                    t = 2 * pair + b
                    gp.wait_ge(moments_ready, t + 1)
                    gp.sem_inc(gate, 1)
                    nc.gpsimd.tensor_scalar(rstd[:, b:b + 1], moments[:, b, 1:2], EPS, None,
                                            ALU.add).then_inc(pool_step, 1)
                    gp.wait_ge(pool_step, t + 2)
                    nc.gpsimd.tensor_tensor(rstd[:, b:b + 1], rstd[:, b:b + 1], minus_half[:, :],
                                            ALU.pow).then_inc(rstd_ready, 1)
                    gp.wait_ge(x1_ready, t + 1)
                    gp.wait_ge(x1_summed, t + 2)
                    nc.gpsimd.tensor_tensor(x_sum[:, :], x_sum[:, :], x1[:, b, :], ALU.add).then_inc(x1_summed, 1)

        @block.tensor
        def _(pe):
            pe.sem_inc(turned, 2)

            def turn(t, b):
                pe.wait_ge(x1_ready, t + 1)
                for f in range(KF):
                    last = nc.tensor.transpose(ps_turn[b][:, P * f:P * (f + 1)], x1[:, b, P * f:P * (f + 1)],
                                               k.ident[:, :])
                last.then_inc(turned, 1)

            def project(t, b):
                pe.wait_ge(turned_sb, t + 1)
                pe.wait_ge(copied, t + 1)
                for f in range(KF):
                    xt = x1_t[:, b, P * f:P * (f + 1)]
                    nc.tensor.matmul(ps_wh[b][:, :], xt, k.w[:, f, :], start=(f == 0), stop=(f == KF - 1))
                    nc.tensor.matmul(ps_sd[b][:, 0:2 * H], xt, k.wa[:, f, :], start=(f == 0), stop=(f == KF - 1))
                    last = nc.tensor.matmul(ps_srow[b][0:H, 0:P], k.wa[:, f, 0:H], xt, start=(f == 0),
                                            stop=(f == KF - 1))
                last.then_inc(projected, 1)

            turn(0, 0)
            with pe.Fori(0, NT // 2 - 1) as pair:
                turn(2 * pair + 1, 1)
                project(2 * pair, 0)
                turn(2 * pair + 2, 0)
                project(2 * pair + 1, 1)
            turn(NT - 1, 1)
            project(NT - 2, 0)
            project(NT - 1, 1)

        @block.scalar
        def _(act):
            act.sem_inc(copied, 2)

            def keep_turned(t, b):
                act.wait_ge(turned, t + 3)
                nc.scalar.copy(x1_t[:, b, :], ps_turn[b][:, :]).then_inc(turned_sb, 1)

            def keep_projected(t, b):
                act.wait_ge(projected, t + 1)
                nc.scalar.copy(row_all[:, bass.ds(t, 1), 0:GCOL].rearrange("p o (h d) -> p (o h) d", d=DH + 1)[:, :, 0:DH],
                               ps_wh[b][:, :].rearrange("p (h d) -> p h d", d=DH))
                nc.scalar.copy(sd_all[:, bass.ds(t, 1), :].rearrange("p o h -> p (o h)"), ps_sd[b][:, 0:2 * H])
                nc.scalar.copy(s_row[:, bass.ds(t * P, P)], ps_srow[b][0:H, 0:P]).then_inc(copied, 1)

            keep_turned(0, 0)
            with act.Fori(0, NT // 2 - 1) as pair:
                keep_turned(2 * pair + 1, 1)
                keep_projected(2 * pair, 0)
                keep_turned(2 * pair + 2, 0)
                keep_projected(2 * pair + 1, 1)
            keep_turned(NT - 1, 1)
            keep_projected(NT - 2, 0)
            keep_projected(NT - 1, 1)


def attention_factors(nc, k, ls, row_all, sd_all, s_row, x_sum, wh_sum):
    with ExitStack() as ctx:
        sb, ps, sem = stage(nc, ctx, "fact")
        d_own, d_max, d_col = sb("d_own", [P, H]), sb("d_max", [P, H]), sb("d_col", [H, 1])
        d_off = sb("d_off", [P, NT, H])
        v_fac = sb("v_fac", [P, NT, H])
        t_row = sb("t_row", [H, N])
        shift = sb("shift", [P, 1])
        x_col = sb("x_col", [P, KF])
        no_row = sb("no_row", [1, ROW])
        row_i, iota_ready = sb("row_i", [NT, N], i32), sem("iota_ready")
        ps_small = ps("ps_small", [P, F])
        ps_x = ps("ps_x", [P, F])
        ps_sum = ps("ps_sum", [P, F])
        own_ready, max_ready, col_ready, z_ready, t_ready = (sem("own_ready"), sem("max_ready"), sem("col_ready"),
                                                             sem("z_ready"), sem("t_ready"))
        off_ready, v_ready, shift_ready, t_st = sem("off_ready"), sem("v_ready"), sem("shift_ready"), sem("t_st")
        x_turned, x_copied, sum_ready, dve_step = (sem("x_turned"), sem("x_copied"), sem("sum_ready"),
                                                   sem("dve_step"))
        g_ready, rows_ready, no_row_st = sem("g_ready"), sem("rows_ready"), sem("no_row_st")
        block = ctx.enter_context(nc.Block())

        @block.vector
        def _(dve):
            step = Chain(dve, dve_step)
            nc.vector.memset(no_row[:, :], 0.0)
            nc.vector.memset(shift[:, :], SHIFT).then_inc(shift_ready, 1)
            nc.vector.tensor_reduce(d_own[:, :], sd_all[:, :, H:2 * H].rearrange("p t h -> p h t"), AX,
                                    ALU.max).then_inc(own_ready, 1)
            dve.wait_ge(x_turned, 1)
            nc.vector.tensor_copy(x_col[:, :], ps_x[:, 0:KF]).then_inc(x_copied, 1)
            dve.wait_ge(max_ready, 1)
            nc.vector.tensor_tensor(d_off[:, :, :], sd_all[:, :, H:2 * H],
                                    d_max[:, :].unsqueeze(1).broadcast_to([P, NT, H]),
                                    ALU.subtract).then_inc(off_ready, 1)
            dve.wait_ge(col_ready, 1)
            step.then(nc.vector.tensor_copy(d_col[:, :], ps_small[0:H, 0:1]))
            nc.vector.tensor_scalar(t_row[:, :], s_row[:, :], d_col[:, 0:1], 0.0, ALU.add,
                                    ALU.max).then_inc(z_ready, 1)
            dve.wait_ge(sum_ready, 1)
            nc.vector.tensor_copy(wh_sum[:, :], ps_sum[0:1, :])
            dve.wait_ge(v_ready, 1)
            v_rows = row_all[:, :, 0:GCOL].rearrange("p t (h d) -> p t h d", d=DH + 1)
            nc.vector.tensor_copy(v_rows[:, :, :, DH], v_fac[:, :, :])
            dve.wait_ge(g_ready, 1)
            nc.vector.tensor_scalar(row_all[:, :, ROW - 1], row_all[:, :, ROW - 2], -1.0, None, ALU.mult)
            for t in range(0, NT, CH):
                nc.vector.tensor_tensor(
                    v_rows[:, t:t + CH, :, 0:DH], v_rows[:, t:t + CH, :, 0:DH],
                    v_fac[:, t:t + CH, :].unsqueeze(3).broadcast_to([P, CH, H, DH]), ALU.mult).then_inc(rows_ready, 1)

        @block.sync
        def _(sp):
            sp.wait_ge(shift_ready, 1)
            sp.dma_start(k.row_d[N:N + 1, :], no_row[:, :]).then_inc(no_row_st, 16)
            for t in range(0, NT, CH):
                sp.wait_ge(rows_ready, t // CH + 1)
                sp.dma_start(k.row_d[P * t:P * (t + CH), :].rearrange("(t p) f -> p t f", p=P),
                             row_all[:, t:t + CH, :]).then_inc(k.rows_st, 16)
            sp.wait_ge(no_row_st, 16)

        @block.gpsimd
        def _(gp):
            gp.wait_ge(own_ready, 1)
            nc.gpsimd.partition_all_reduce(d_max[:, :], d_own[:, :], P,
                                           bass.bass_isa.ReduceOp.max).then_inc(max_ready, 1)
            nc.gpsimd.iota(row_i[:, :], [[1, N]], base=0, channel_multiplier=0).then_inc(iota_ready, 1)
            gp.wait_ge(iota_ready, 1)
            nc.gpsimd.tensor_copy(ls.slot_row[:, :], row_i[:, :])

        @block.tensor
        def _(pe):
            for f in range(KF):
                last = nc.tensor.matmul(ps_x[:, f:f + 1], x_sum[:, P * f:P * (f + 1)], k.ones[:, 0:1], start=True,
                                        stop=True)
            last.then_inc(x_turned, 1)
            pe.wait_ge(x_copied, 1)
            for f in range(KF):
                last = nc.tensor.matmul(ps_sum[0:1, :], x_col[:, f:f + 1], k.w[:, f, :], start=(f == 0),
                                        stop=(f == KF - 1))
            last.then_inc(sum_ready, 1)
            pe.wait_ge(max_ready, 1)
            nc.tensor.matmul(ps_small[0:H, 0:1], d_max[0:1, :], k.ones[0:1, 0:1], start=True,
                             stop=True).then_inc(col_ready, 1)

        @block.scalar
        def _(act):
            act.wait_ge(shift_ready, 1)
            act.wait_ge(off_ready, 1)
            nc.scalar.activation(v_fac[:, :, :], d_off[:, :, :], ACT.Exp, scale=0.2,
                                 bias=shift[:, 0:1]).then_inc(v_ready, 1)
            nc.scalar.activation(row_all[:, :, GCOL:GCOL + H], d_off[:, :, :], ACT.Exp, scale=0.8,
                                 bias=shift[:, 0:1]).then_inc(g_ready, 1)
            act.wait_ge(z_ready, 1)
            nc.scalar.activation(t_row[:, :], t_row[:, :], ACT.Exp, scale=-0.8,
                                 bias=shift[0:H, 0:1]).then_inc(t_ready, 1)
            act.wait_ge(t_ready, 1)
            act.dma_start(k.trow_d, t_row[:, :]).then_inc(t_st, 16)
            act.wait_ge(t_st, 16)


def attend(nc, k, adj_rows, num_all, den_all):
    with ExitStack() as ctx:
        sb, ps, sem = stage(nc, ctx, "att")
        HALF = GT // 2
        index = sb("index", [P, 2, HALF, 2], i32)
        rows = sb("rows", [P, GT, ROW])
        edges = sb("edges", [P, GT, DS])
        t_bc = sb("t_bc", [P, 2, H, DS])
        higher = sb("higher", [P, GT, DS])
        weights = sb("weights", [P, GT, H, DS])
        nothing = sb("nothing", [1, DS], f16)
        ps_num = [ps(f"ps_num{p}", [P, F]) for p in range(H // 2)]
        ps_den = [ps(f"ps_den{p}", [P, F]) for p in range(H // 4)]
        ps_sums = ps_num + ps_den
        BANKS = len(ps_sums)
        rows_ld = [sem(f"rows_ld{b}") for b in range(GT)]
        edges_ld = [sem(f"edges_ld{b}") for b in range(GT)]
        made, multiplied, used, summed, copied = (sem("made"), sem("multiplied"), sem("used"), sem("summed"),
                                                  sem("copied"))
        t_ld, pool_step, blank, gate = sem("t_ld"), sem("pool_step"), sem("blank"), sem("gate")
        risen, higher_ready = sem("risen"), sem("higher_ready")
        block = ctx.enter_context(nc.Block())

        def multiplied_with(g, b):
            return (GT - 1) * g + b + HALF + GT

        @block.sync
        def _(sp):
            def load_t(s, odd):
                sp.dma_start(t_bc[:, odd, :, :], k.trow_d[:, bass.ds(s * DS, DS)].unsqueeze(0)
                             .broadcast_to([P, H, DS])).then_inc(t_ld, 16)

            load_t(0, 0)
            sp.wait_ge(t_ld, 16)
            load_t(1, 1)
            with sp.Fori(0, NS // 2 - 1) as pair:
                for odd in range(2):
                    s = 2 * pair + 2 + odd
                    sp.wait_ge(copied, BANKS * s)
                    sp.sem_inc(gate, 1)
                    sp.wait_ge(t_ld, 16 * s)
                    sp.sem_inc(gate, 1)
                    load_t(s, odd)

        @block.gpsimd
        def _(gp):
            def multiply(g, b):
                gp.wait_ge(higher_ready, (GT - 1) * g + b + GT)
                gp.wait_ge(used, GT * g + b + 1 + GT)
                gp.sem_inc(gate, 1)
                nc.gpsimd.tensor_tensor(weights[:, b, H - 1, :], higher[:, b, :], edges[:, b, :],
                                        ALU.mult).then_inc(multiplied, 1)

            gp.sem_inc(multiplied, GT)
            nc.gpsimd.memset(nothing[:, :], 0.0)
            nc.gpsimd.memset(higher[:, HALF:GT, :], 0.0)
            nc.gpsimd.memset(edges[:, HALF:GT, :], 0.0).then_inc(blank, 1)
            gp.wait_ge(blank, 1)
            with gp.Fori(0, NS) as s:
                def fetch(q, g):
                    for half in range(2):
                        b = HALF * half
                        gp.wait_ge(made, GT * g + b + HALF)
                        gp.wait_ge(multiplied, multiplied_with(g - 1, b + HALF - 1))
                        gp.sem_inc(gate, 1)
                        nc.gpsimd.tensor_copy(
                            index[:, half, :, :],
                            k.index[:, bass.ds(s, 1), bass.ds(q * GT + b, HALF), :]
                            .rearrange("p o t c -> p (o t) c")).then_inc(pool_step, 1)
                        gp.wait_ge(pool_step, 2 * g + half + 1)
                        gp.sem_inc(gate, 1)
                        for i in range(HALF):
                            gp.indirect_dma_start(edges[:, b + i, :], None, adj_rows,
                                                  bass.IndirectOffsetOnAxis(ap=index[:, half, i, 1:2], axis=0),
                                                  bounds_check=N * NS - 1, oob_is_err=False).then_inc(edges_ld[b + i], 16)
                        for i in range(HALF):
                            gp.wait_ge(used, GT * g + b + i + 1 + GT)
                            gp.sem_inc(gate, 1)
                            gp.indirect_dma_start(rows[:, b + i, :], None, k.row_d,
                                                  bass.IndirectOffsetOnAxis(ap=index[:, half, i, 0:1], axis=0),
                                                  bounds_check=N, oob_is_err=False).then_inc(rows_ld[b + i], 16)
                        for tile in ((1,) if half else (2, 3)):
                            multiply(g - 1 + half, tile)

                section_groups(gp, k, s, fetch)
            last = gp.value_load(k.groups[0:1, NS - 1:NS], min_val=MG, max_val=(NS - 1) * NT // GT * PACK + NT // GT)
            end = gp.snap(last // PACK + last % PACK - 1, min_val=0, max_val=NS * NT // GT - 1)
            for i in range(HALF):
                multiply(end, HALF + i)

        @block.scalar
        def _(act):
            act.sem_inc(copied, BANKS)
            act.sem_inc(higher_ready, GT)

            def copy_out(s):
                for i, sums in enumerate(ps_sums):
                    kept, p = (num_all, i) if i < H // 2 else (den_all, i - H // 2)
                    act.wait_ge(summed, BANKS * s + i + 1)
                    act.sem_inc(gate, 1)
                    nc.scalar.copy(kept[:, p, bass.ds(s * DS, DS)], sums[:, 0:DS]).then_inc(copied, 1)

            def section(s, odd, copy_before):
                act.wait_ge(t_ld, 16 * (s + 1))

                def rise(q, g):
                    for b in range(1, GT):
                        act.wait_ge(edges_ld[b], 16 * (g + 1))
                        act.wait_ge(rows_ld[b], 16 * (g + 1))
                        act.wait_ge(multiplied, multiplied_with(g - 1, b))
                        act.sem_inc(gate, 1)
                        nc.scalar.activation(higher[:, b, :],
                                             t_bc[:, bass.ds(odd, 1), H - 1, :].rearrange("p o i -> p (o i)"),
                                             ACT.Relu, bias=rows[:, b, ROW - 1:ROW]).then_inc(risen, 1)
                        act.wait_ge(risen, (GT - 1) * g + b)
                        nc.scalar.activation(higher[:, b, :], higher[:, b, :], ACT.Identity,
                                             bias=rows[:, b, ROW - 2:ROW - 1]).then_inc(higher_ready, 1)
                        if copy_before and isinstance(q, int) and q == 0 and b == HALF - 1:
                            copy_out(s - 1)

                section_groups(act, k, s, rise)

            section(0, 0, False)
            with act.Fori(1, NS) as s:
                section(s, act.snap(s % 2, min_val=0, max_val=1), True)
            copy_out(NS - 1)

        @block.vector
        def _(dve):
            dve.sem_inc(made, GT)
            with dve.Fori(0, NS) as s:
                odd = dve.snap(s % 2, min_val=0, max_val=1)
                dve.wait_ge(t_ld, 16 * (s + 1))

                def weigh(q, g):
                    for b in range(GT):
                        dve.wait_ge(edges_ld[b], 16 * (g + 1))
                        dve.wait_ge(rows_ld[b], 16 * (g + 1))
                        dve.wait_ge(used, GT * g + b + 1 + GT)
                        for h in range(H if b == 0 else H - 1):
                            last = nc.vector.scalar_tensor_tensor(
                                weights[:, b, h, :], t_bc[:, bass.ds(odd, 1), h, :].rearrange("p o i -> p (o i)"),
                                rows[:, b, GCOL + h:GCOL + h + 1], edges[:, b, :], ALU.max, ALU.mult)
                        last.then_inc(made, 1)

                section_groups(dve, k, s, weigh)

        @block.tensor
        def _(pe):
            pe.sem_inc(used, 2 * GT)
            pe.wait_ge(blank, 1)
            with pe.Fori(0, NS) as s:
                def add(q, g):
                    for b in range(GT):
                        first = isinstance(q, int) and q == 0 and b == 0
                        pe.wait_ge(made, GT * g + b + 1 + GT)
                        for h in range(H):
                            if first and h % 2 == 0:
                                pe.wait_ge(copied, BANKS * s + h // 2 + 1)
                            if h == H - 1 and b > 0:
                                pe.wait_ge(multiplied, multiplied_with(g, b))
                            at = DH * (h % 2)
                            nc.tensor.matmul(ps_num[h // 2][at:at + DH, 0:DS],
                                             rows[:, b, (DH + 1) * h:(DH + 1) * h + DH], weights[:, b, h, :],
                                             start=first, stop=False)
                        for h in range(H):
                            at = 32 * (h % 4)
                            v = (DH + 1) * h + DH
                            if first and h % 4 == 0:
                                pe.wait_ge(copied, BANKS * s + H // 2 + h // 4 + 1)
                            last = nc.tensor.matmul(ps_den[h // 4][at:at + 32, 0:DS],
                                                    rows[:, b, v:v + 1].broadcast_to([P, 32]), weights[:, b, h, :],
                                                    start=first, stop=False, tile_position=(0, at))
                        last.then_inc(used, 1)

                section_groups(pe, k, s, add)
                for sums in ps_sums:
                    nc.tensor.matmul(sums[:, 0:DS], nothing[0:1, 0:P], nothing[0:1, :], start=False,
                                     stop=True).then_inc(summed, 1)


def lonely_nodes(nc, k, wh_sum, num_all, den_all):
    with ExitStack() as ctx:
        sb, ps, sem = stage(nc, ctx, "lone")
        empty = sb("empty", [1, N])
        flags = sb("flags", [1, SEC])
        n_row = sb("n_row", [1, 32])
        ps_num = [ps(f"ps_num{p}", [P, SEC]) for p in range(H // 2)]
        ps_den = [ps(f"ps_den{p}", [P, SEC]) for p in range(H // 4)]
        empty_ld, flags_ready, summed, added = sem("empty_ld"), sem("flags_ready"), sem("summed"), sem("added")
        block = ctx.enter_context(nc.Block())

        @block.sync
        def _(sp):
            lonely = sp.value_load(k.lonely[0:1, 0:1], min_val=0, max_val=N)
            with sp.If(lonely > 0):
                sp.dma_start(empty[:, :], k.empty_d.rearrange("n o -> o n")).then_inc(empty_ld, 16)
                sp.wait_ge(empty_ld, 16)

        @block.vector
        def _(dve):
            lonely = dve.value_load(k.lonely[0:1, 0:1], min_val=0, max_val=N)
            with dve.If(lonely > 0):
                dve.sem_inc(added, 1)
                nc.vector.memset(n_row[:, :], float(N))
                dve.wait_ge(empty_ld, 16)
                with dve.Fori(0, SECS) as c:
                    dve.wait_ge(summed, c + 1)
                    nc.vector.tensor_copy(flags[:, :], empty[:, bass.ds(c * SEC, SEC)]).then_inc(flags_ready, 1)
                    dve.wait_ge(summed, c + 2)
                    for p in range(H // 2):
                        part = num_all[:, p, bass.ds(c * SEC, SEC)]
                        nc.vector.tensor_tensor(part, part, ps_num[p][:, :], ALU.add)
                    for p in range(H // 4):
                        part = den_all[:, p, bass.ds(c * SEC, SEC)]
                        last = nc.vector.tensor_tensor(part, part, ps_den[p][:, :], ALU.add)
                    last.then_inc(added, 1)

        @block.tensor
        def _(pe):
            lonely = pe.value_load(k.lonely[0:1, 0:1], min_val=0, max_val=N)
            with pe.If(lonely > 0):
                pe.sem_inc(summed, 1)
                with pe.Fori(0, SECS) as c:
                    pe.wait_ge(flags_ready, c + 1)
                    pe.wait_ge(added, c + 1)
                    for h in range(H):
                        at = DH * (h % 2)
                        nc.tensor.matmul(ps_num[h // 2][at:at + DH, :], wh_sum[0:1, DH * h:DH * (h + 1)],
                                         flags[:, :], start=True, stop=True)
                    for h in range(H):
                        at = 32 * (h % 4)
                        last = nc.tensor.matmul(ps_den[h // 4][at:at + 32, :], n_row[0:1, :], flags[:, :],
                                                start=True, stop=True, tile_position=(0, at))
                    last.then_inc(summed, 1)


def finish_nodes(nc, k, ins, num_all, den_all, out):
    with ExitStack() as ctx:
        sb, ps, sem = stage(nc, ctx, "fin")
        den = sb("den", [P, 2, SEC])
        pick = sb("pick", [P, 4 * DH])
        low = sb("low", [P, 4, SEC])
        hid1, hid2, hid3 = sb("hid1", [P, 2, SEC]), sb("hid2", [P, SEC]), sb("hid3", [P, 2, SEC])
        w1, w2, w3, w4 = (sb("w1", [P, 4, M1]), sb("w2", [P, 2, M2]), sb("w3", [P, M3]), sb("w4", [P, 2, F]))
        b1, b2, b3 = sb("b1", [P, 2]), sb("b2", [P, 1]), sb("b3", [P, 2])
        b4 = sb("b4", [P, F])
        base = sb("base", [P, 4, F])
        y = sb("y", [P, 4, F])
        seen, moments, rstd = sb("seen", [P, 4, 6]), sb("moments", [P, 4, 2]), sb("rstd", [P, 4])
        minus_half = sb("minus_half", [P, 4])
        ps_spread = [ps(f"ps_spread{p}", [P, SEC]) for p in range(2)]
        ps_hid1 = [ps(f"ps_hid1{b}", [P, SEC]) for b in range(2)]
        ps_hid23 = [ps(f"ps_hid23{b}", [P, SEC]) for b in range(2)]
        ps_out = [ps(f"ps_out{b}", [P, SEC]) for b in range(2)]
        par_ld, x1_ld, out_st = sem("par_ld"), sem("x1_ld"), sem("out_st")
        den_ready, den_spread, ratio_ready = sem("den_ready"), sem("den_spread"), sem("ratio_ready")
        low_ready, exp_ready, enc_ready = sem("low_ready"), sem("exp_ready"), sem("enc_ready")
        mlp_ready, hid_ready, y_mlp, y_part = sem("mlp_ready"), sem("hid_ready"), sem("y_mlp"), sem("y_part")
        y_ready, y_free, base_ready = sem("y_ready"), sem("y_free"), sem("base_ready")
        dve_step, gate = sem("dve_step"), sem("gate")
        moments_ready, rstd_ready, rstd_step = sem("moments_ready"), sem("rstd_ready"), sem("rstd_step")
        PARAMS = 9
        block = ctx.enter_context(nc.Block())

        def cols(c):
            return bass.ds(c * SEC, SEC)

        @block.sync
        def _(sp):
            for dst, name in ((pick, "pick"), (b1, "b1"), (b2, "b2"), (b3, "b3"), (w3, "w3_t")):
                sp.dma_start(dst[:, :], ins[name]).then_inc(par_ld, 16)
            for dst, name in ((w1, "w1_t"), (w2, "w2_t"), (w4, "w4_t")):
                sp.dma_start(dst[:, :, :], tiles_of(ins[name])).then_inc(par_ld, 16)
            sp.dma_start(b4[:, :], ins["b4"].broadcast_to([P, F])).then_inc(par_ld, 16)
            with sp.Fori(0, SECS) as c:
                sp.wait_ge(y_part, 2 * c + 2)
                sp.sem_inc(gate, 1)
                sp.dma_start(base[:, :, :], tiles_of(k.x1_d)[:, bass.ds(4 * c, 4), :]).then_inc(x1_ld, 16)

        @block.vector
        def _(dve):
            dve.sem_inc(y_part, 2)

            def invert_sums(c):
                dve.wait_ge(den_spread, 2 * c + 2)
                nc.vector.reciprocal(den[:, :, :], den_all[:, :, cols(c)]).then_inc(den_ready, 1)

            def divide(c, half):
                dve.wait_ge(den_spread, 2 * c + half + 3)
                for p in range(2):
                    part = num_all[:, 2 * half + p, cols(c)]
                    last = nc.vector.tensor_tensor(part, part, ps_spread[p][:, :], ALU.mult)
                last.then_inc(ratio_ready, 1)

            def add_residual(c, half):
                if half == 0:
                    dve.wait_ge(base_ready, c + 1)
                    dve.wait_ge(y_free, c + 1)
                dve.wait_ge(y_mlp, 2 * c + half + 1)
                for b in range(2):
                    i = 2 * half + b
                    last = nc.vector.tensor_tensor(y[:, i, :], ps_out[b][:, :], base[:, i, :], ALU.add)
                last.then_inc(y_part, 1)

            def normalise(c):
                dve.wait_ge(y_part, 2 * c + 4)
                for i in range(4):
                    last = nc.vector.bn_stats(seen[:, i, :], y[:, i, :])
                last.then_inc(dve_step, 1)
                dve.wait_ge(dve_step, c + 1)
                dve.sem_inc(gate, 1)
                for i in range(4):
                    last = nc.vector.bn_aggr(moments[:, i, :], seen[:, i, :])
                last.then_inc(moments_ready, 1)

            def scale_rows(c):
                dve.wait_ge(rstd_ready, c + 1)
                for i in range(4):
                    last = nc.vector.tensor_scalar(y[:, i, :], y[:, i, :], moments[:, i, 0:1], rstd[:, i:i + 1],
                                                   ALU.subtract, ALU.mult)
                last.then_inc(y_ready, 1)

            def finish_elu(c):
                dve.wait_ge(exp_ready, c + 1)
                part = num_all[:, :, cols(c)]
                nc.vector.scalar_tensor_tensor(part, low[:, :, :], -1.0, part, ALU.add, ALU.add).then_inc(enc_ready, 1)

            invert_sums(0)
            for c in range(3):
                for half in range(2):
                    divide(c, half)
                invert_sums(c + 1)
                if c < 2:
                    finish_elu(c)
            with dve.Fori(1, SECS - 3) as c:
                divide(c + 2, 0)
                finish_elu(c + 1)
                add_residual(c - 1, 0)
                divide(c + 2, 1)
                add_residual(c - 1, 1)
                normalise(c - 1)
                invert_sums(c + 3)
                scale_rows(c - 1)
            c = SECS - 3
            divide(c + 2, 0)
            finish_elu(c + 1)
            add_residual(c - 1, 0)
            divide(c + 2, 1)
            add_residual(c - 1, 1)
            normalise(c - 1)
            scale_rows(c - 1)
            for c in range(SECS - 3, SECS):
                if c == SECS - 3:
                    finish_elu(SECS - 1)
                add_residual(c, 0)
                add_residual(c, 1)
                normalise(c)
                scale_rows(c)

        @block.tensor
        def _(pe):
            pe.wait_ge(par_ld, 16 * PARAMS)
            pe.sem_inc(den_spread, 2)

            def spread_sums(c, half):
                pe.wait_ge(den_ready, c + 1)
                pe.wait_ge(ratio_ready, 2 * c + half + 1)
                for p in range(2):
                    last = nc.tensor.matmul(ps_spread[p][:, :], pick[:, P * p:P * (p + 1)], den[:, half, :],
                                            start=True, stop=True)
                last.then_inc(den_spread, 1)

            def hidden1(c):
                pe.wait_ge(enc_ready, c + 1)
                if not (isinstance(c, int) and c == 0):
                    pe.wait_ge(hid_ready, 3 * c)
                for m in range(2):
                    for e in range(4):
                        last = nc.tensor.matmul(ps_hid1[m][:, :], w1[:, e, P * m:P * (m + 1)], num_all[:, e, cols(c)],
                                                start=(e == 0), stop=(e == 3))
                last.then_inc(mlp_ready, 1)

            def hidden2(c):
                pe.wait_ge(hid_ready, 3 * c + 1)
                for e in range(2):
                    last = nc.tensor.matmul(ps_hid23[0][:, :], w2[:, e, :], hid1[:, e, :], start=(e == 0), stop=(e == 1))
                last.then_inc(mlp_ready, 1)

            def hidden3(c):
                pe.wait_ge(hid_ready, 3 * c + 2)
                for m in range(2):
                    last = nc.tensor.matmul(ps_hid23[m][:, :], w3[:, P * m:P * (m + 1)], hid2[:, :], start=True,
                                            stop=True)
                last.then_inc(mlp_ready, 1)

            def output(c, half):
                pe.wait_ge(hid_ready, 3 * c + 3)
                pe.wait_ge(y_part, 2 * c + half + 2)
                for b in range(2):
                    i = 2 * half + b
                    for e in range(2):
                        last = nc.tensor.matmul(ps_out[b][:, :], hid3[:, e, P * i:P * (i + 1)], w4[:, e, :],
                                                start=(e == 0), stop=(e == 1))
                last.then_inc(y_mlp, 1)

            for c in range(2):
                for half in range(2):
                    spread_sums(c, half)
            hidden1(0)
            spread_sums(2, 0)
            hidden2(0)
            spread_sums(2, 1)
            hidden3(0)
            with pe.Fori(1, SECS - 2) as c:
                hidden1(c)
                spread_sums(c + 2, 0)
                hidden2(c)
                output(c - 1, 0)
                spread_sums(c + 2, 1)
                hidden3(c)
                output(c - 1, 1)
            for c in range(SECS - 2, SECS):
                hidden1(c)
                hidden2(c)
                output(c - 1, 0)
                hidden3(c)
                output(c - 1, 1)
            output(SECS - 1, 0)
            output(SECS - 1, 1)

        @block.scalar
        def _(act):
            act.wait_ge(par_ld, 16 * PARAMS)

            def elu(c):
                act.wait_ge(ratio_ready, 2 * c + 3)
                if not (isinstance(c, int) and c == 0):
                    act.wait_ge(enc_ready, c)
                part = num_all[:, :, cols(c)]
                nc.scalar.activation(low[:, :, :], part, ACT.Relu, scale=-1.0).then_inc(low_ready, 1)
                act.wait_ge(low_ready, c + 1)
                nc.scalar.activation(low[:, :, :], low[:, :, :], ACT.Exp, scale=-1.0)
                nc.scalar.activation(part, part, ACT.Relu).then_inc(exp_ready, 1)

            def hidden(c):
                act.wait_ge(mlp_ready, 3 * c + 1)
                nc.scalar.activation(hid1[:, 0, :], ps_hid1[0][:, :], ACT.Relu, bias=b1[:, 0:1])
                nc.scalar.activation(hid1[:, 1, :], ps_hid1[1][:, :], ACT.Relu, bias=b1[:, 1:2]).then_inc(hid_ready, 1)
                act.wait_ge(mlp_ready, 3 * c + 2)
                nc.scalar.activation(hid2[:, :], ps_hid23[0][:, :], ACT.Relu, bias=b2[:, 0:1]).then_inc(hid_ready, 1)
                act.wait_ge(mlp_ready, 3 * c + 3)
                if not (isinstance(c, int) and c == 0):
                    act.wait_ge(y_mlp, 2 * c)
                nc.scalar.activation(hid3[:, 0, :], ps_hid23[0][:, :], ACT.Relu, bias=b3[:, 0:1])
                nc.scalar.activation(hid3[:, 1, :], ps_hid23[1][:, :], ACT.Relu, bias=b3[:, 1:2]).then_inc(hid_ready, 1)

            elu(0)
            elu(1)
            hidden(0)
            with act.Fori(1, SECS - 1) as c:
                elu(c + 1)
                hidden(c)
            hidden(SECS - 1)

        @block.gpsimd
        def _(gp):
            gp.sem_inc(ratio_ready, 1)
            gp.sem_inc(y_free, 1)
            nc.gpsimd.memset(minus_half[:, :], -0.5).then_inc(rstd_step, 1)
            gp.wait_ge(par_ld, 16 * PARAMS)

            def add_bias(c):
                gp.wait_ge(x1_ld, 16 * (c + 1))
                nc.gpsimd.tensor_tensor(base[:, :, :], base[:, :, :],
                                        b4[:, :].unsqueeze(1).broadcast_to([P, 4, F]), ALU.add).then_inc(base_ready, 1)

            def end(c):
                gp.wait_ge(moments_ready, c + 1)
                gp.sem_inc(gate, 1)
                nc.gpsimd.tensor_scalar(rstd[:, :], moments[:, :, 1], EPS, None, ALU.add).then_inc(rstd_step, 1)
                gp.wait_ge(rstd_step, c + 2)
                nc.gpsimd.tensor_tensor(rstd[:, :], rstd[:, :], minus_half[:, :], ALU.pow).then_inc(rstd_ready, 1)
                gp.wait_ge(y_ready, c + 1)
                gp.sem_inc(gate, 1)
                gp.dma_start(tiles_of(out)[:, bass.ds(4 * c, 4), :], y[:, :, :]).then_inc(out_st, 16)
                gp.wait_ge(out_st, 16 * (c + 1))
                gp.sem_inc(y_free, 1)

            with gp.Fori(1, SECS - 1) as c:
                add_bias(c - 1)
                end(c - 1)
            for c in range(SECS - 2, SECS):
                add_bias(c)
                end(c)


def build(nc, ins, out):
    with ExitStack() as ctx:
        k = make_kept(nc, ctx)
        c_all = ctx.enter_context(nc.sbuf_tensor("c_all", [P, NT], f32))
        cx_all = ctx.enter_context(nc.sbuf_tensor("cx_all", [P, NT], f32))
        with nc.sbuf_tensor("key_row", [P, LIST], f32) as key_row:
            with nc.sbuf_tensor("xs", [P, NT, 2 * F], f16) as xs:
                split_features(nc, k, ins, xs)
                neighbour_sums(nc, k, ins, xs, key_row)
            with (nc.sbuf_tensor("att_all", [P, RT * H], f32) as att_all,
                  nc.sbuf_tensor("weight_all", [P, RT], f32) as weight_all):
                relation_scores(nc, k, ins, key_row, att_all, weight_all)
                node_coefficients(nc, k, ins, c_all, cx_all)
                relation_values(nc, k, ins, att_all, weight_all)
        wh_sum = ctx.enter_context(nc.sbuf_tensor("wh_sum", [1, F], f32))
        with ExitStack() as rows_kept:
            def sb(name, shape, dt=f32):
                return rows_kept.enter_context(nc.sbuf_tensor(name, shape, dt))

            row_all = sb("row_all", [P, NT, ROW])
            ls = make_lists(sb)
            with (nc.sbuf_tensor("sd_all", [P, NT, 2 * H], f32) as sd_all,
                  nc.sbuf_tensor("s_row", [H, N], f32) as s_row,
                  nc.sbuf_tensor("x_sum", [P, F], f32) as x_sum):
                project_nodes(nc, k, ins, c_all, cx_all, row_all, sd_all, s_row, x_sum)
                attention_factors(nc, k, ls, row_all, sd_all, s_row, x_sum, wh_sum)
            source_index(nc, k, ins, ls)
            source_lists(nc, k, ls)
            list_rows(nc, k, ls)
        num_all = ctx.enter_context(nc.sbuf_tensor("num_all", [P, 4, N], f32))
        den_all = ctx.enter_context(nc.sbuf_tensor("den_all", [P, 2, N], f32))
        adj_rows = ins["adj_t"].rearrange("j (s i) -> (j s) i", i=DS)
        attend(nc, k, adj_rows, num_all, den_all)
        lonely_nodes(nc, k, wh_sum, num_all, den_all)
        finish_nodes(nc, k, ins, num_all, den_all, out)

_LAY = {
    "x": lambda np, a: a["x"],
    "adj_t": lambda np, a: a["adj"].T,
    "adj_diag": lambda np, a: np.diagonal(a["adj"]).reshape(NT, P).T,
    "pairs": lambda np, a: a["L0_gnn_rel_pair_index"],
    "W": lambda np, a: a["L1_gnn_W"].transpose(1, 0, 2).reshape(F, H * DH),
    "a1": lambda np, a: a["L1_gnn_a1"].reshape(1, F),
    "a2": lambda np, a: a["L1_gnn_a2"].reshape(1, F),
    "wq_t": lambda np, a: a["L0_gnn_Wq"].T,
    "wk_t": lambda np, a: a["L0_gnn_Wk"].T,
    "bq": lambda np, a: a["L0_gnn_bq"].reshape(1, F),
    "bk": lambda np, a: a["L0_gnn_bk"].reshape(1, F),
    "w1_t": lambda np, a: a["L1_gnn_W1"].T,
    "w2_t": lambda np, a: a["L1_gnn_W2"].T,
    "w3_t": lambda np, a: a["L1_gnn_W3"].T,
    "w4_t": lambda np, a: a["L1_gnn_W4"].T,
    "b1": lambda np, a: a["L1_gnn_b1"].reshape(2, P).T,
    "b2": lambda np, a: a["L1_gnn_b2"].reshape(1, P).T,
    "b3": lambda np, a: a["L1_gnn_b3"].reshape(2, P).T,
    "b4": lambda np, a: a["L1_gnn_b4"].reshape(1, F),
    "ident": lambda np, a: np.eye(P, dtype=np.float32),
    "before": lambda np, a: np.tril(np.ones((P, P), np.float32), -1),
    "differ": lambda np, a: 0.5 * np.concatenate([np.eye(NT, dtype=np.float32) - np.eye(NT, k=1, dtype=np.float32)]
                                                 + 2 * [np.eye(NT, dtype=np.float32)[:, -1:]], axis=1),
    "tile_step": lambda np, a: np.array([[0.0, 0.0]] + [[P / 2, 0.0]] * (NT - 1)
                                        + [[P * (NT - 1) / 2, 0.0], [0.0, -1.0]], np.float32),
    "pick": lambda np, a: np.concatenate([np.repeat(np.eye(P, dtype=np.float32)[:, 32 * h:32 * h + 1], DH, axis=1)
                                          for h in range(4)], axis=1),
}


def kernel(**inputs):
    import numpy as _np
    import concourse.bacc as _bacc
    from concourse.bass_utils import run_bass_kernel_spmd as _run

    nc = _bacc.Bacc("TRN2", target_bir_lowering=False, num_devices=1)
    given = {n: _np.asarray(v) for n, v in inputs.items()}
    arrays, ins = {}, {}
    for name, lay in _LAY.items():
        a = _np.ascontiguousarray(lay(_np, given))
        arrays[f"in_{name}_dram"] = a
        ins[name] = nc.dram_tensor(f"in_{name}_dram", a.shape, mybir.dt.from_np(a.dtype), kind="ExternalInput").ap()
    out = nc.dram_tensor("out_0_dram", (N, F), f32, kind="ExternalOutput").ap()
    build(nc, ins, out)
    return _run(nc, [arrays], core_ids=[0]).results[0]["out_0_dram"]
```
